# Optimizing a Trainium2 kernel written in Bass

```python
import numpy as np
import jax
import jax.numpy as jnp

def _softmax(x, axis=-1):
    return jax.nn.softmax(x, axis=axis)

def _gelu(x):
    return jax.nn.gelu(x, approximate=True)

def _silu(x):
    return jax.nn.silu(x)

def _sigmoid(x):
    return jax.nn.sigmoid(x)

def _layernorm(x, axis=-1, eps=1e-05):
    m = jnp.mean(x, axis=axis, keepdims=True)
    v = jnp.var(x, axis=axis, keepdims=True)
    return (x - m) / jnp.sqrt(v + eps)

def _scatter_add(tgt, idx, src, axis=0):
    return tgt.at[idx].add(src)

def _segment_sum(src, seg, n):
    return jax.ops.segment_sum(src, seg, n)
kernel_name = 'mk_macaron_d2_jaxref_r8_4db2c9'

def setup_inputs(seed: int=0):
    np.random.seed(seed)
    _w = jnp.asarray

    def _L0_attn_setup():
        import jax, jax.numpy as jnp
        import numpy as np
        BATCH, SEQ, HIDDEN = (2, 512, 512)
        HEADS, HEAD_DIM, BLOCK = (32, 128, 32)
        LAYER_IDX, N_LAYERS = (1, 32)
        EPS = 1e-05

        def _decays():
            base = 1.0 / 2.0 ** (8.0 / HEADS)
            exponent = jnp.arange(HEADS, dtype=jnp.float32) + 1.0
            factor = 1.0 - LAYER_IDX / (N_LAYERS - 1 + 1e-05) + 1e-05
            slope = (base ** exponent * factor)[:, None, None]
            r = jnp.arange(BLOCK, dtype=jnp.float32) + 1.0
            q_decay = jnp.exp(-slope * r[:, None])
            k_decay = jnp.exp(-slope * (BLOCK - r)[:, None])
            diff = r[:, None] - r[None, :]
            diag = slope[None] * diff[None, None]
            diag = jnp.where(diag >= 0, -diag, -jnp.inf)
            diag_decay = jnp.exp(diag)
            block_decay = jnp.exp(-slope * BLOCK)
            return (q_decay, k_decay, diag_decay, block_decay)
        key = jax.random.key(seed)
        ks = jax.random.split(key, 5)
        s = 0.02
        return {'hidden_states': jax.random.normal(ks[0], (BATCH, SEQ, HIDDEN), jnp.float32), 'qkv_w': jax.random.normal(ks[1], (3 * HEADS * HEAD_DIM, HIDDEN), jnp.float32) * s, 'out_w': jax.random.normal(ks[2], (HIDDEN, HEADS * HEAD_DIM), jnp.float32) * s, 'gate_w': jax.random.normal(ks[3], (HEADS * HEAD_DIM, HIDDEN), jnp.float32) * s, 'norm_w': jnp.ones((HEADS * HEAD_DIM,), jnp.float32)}
    _L0_attn_in = _L0_attn_setup()

    def _L0_ffn_setup():
        import jax, jax.numpy as jnp
        import numpy as np
        BATCH, TOK, DIM, OUT = (4, 256, 512, 512)
        E, R, TOP_K = (8, 16, 2)
        SCALING = 16.0 / R
        key = jax.random.key(seed)
        ks = jax.random.split(key, 6)
        return {'x': jax.random.normal(ks[0], (BATCH, TOK, DIM), dtype=jnp.float32), 'W_base': jax.random.normal(ks[1], (OUT, DIM), dtype=jnp.float32) / np.sqrt(DIM), 'b_base': jax.random.normal(ks[2], (OUT,), dtype=jnp.float32) * 0.01, 'W_gate': jax.random.normal(ks[3], (E, DIM), dtype=jnp.float32) * 0.01, 'A': jax.random.normal(ks[4], (E, R, DIM), dtype=jnp.float32) / np.sqrt(DIM), 'B': jax.random.normal(ks[5], (OUT, OUT // OUT * R * 0 + R), dtype=jnp.float32)[None].repeat(E, 0) * 0.0 + jax.random.normal(ks[5], (E, OUT, R), dtype=jnp.float32) * 0.02}
    _L0_ffn_in = _L0_ffn_setup()

    def _L1_attn_setup():
        import jax, jax.numpy as jnp
        import numpy as np
        EMBED = 512
        H = 32
        KV = 8
        D = EMBED // H
        REP = H // KV

        def _rope(t, cos, sin):
            t = t.reshape(*t.shape[:-1], 2, D // 2)
            t1, t2 = (t[..., 0, :], t[..., 1, :])
            return jnp.concatenate([t1 * cos - t2 * sin, t1 * sin + t2 * cos], axis=-1)
        key = jax.random.key(seed)
        ks = jax.random.split(key, 7)
        B, S = (1, 256)
        x = jax.random.normal(ks[0], (B, S, EMBED), dtype=jnp.float32)
        wq = jax.random.normal(ks[1], (EMBED, EMBED), dtype=jnp.float32) * 0.02
        bq = jax.random.normal(ks[2], (EMBED,), dtype=jnp.float32) * 0.02
        wk = jax.random.normal(ks[3], (EMBED, KV * D), dtype=jnp.float32) * 0.02
        bk = jax.random.normal(ks[4], (KV * D,), dtype=jnp.float32) * 0.02
        wv = jax.random.normal(ks[5], (EMBED, KV * D), dtype=jnp.float32) * 0.02
        bv = jax.random.normal(ks[6], (KV * D,), dtype=jnp.float32) * 0.02
        return {'x': x, 'wq': wq, 'bq': bq, 'wk': wk, 'bk': bk, 'wv': wv, 'bv': bv}
    _L1_attn_in = _L1_attn_setup()

    def _L1_ffn_setup():
        import jax, jax.numpy as jnp
        import numpy as np
        HID, BOT, RDIM, NSLOT, K, VB = (512, 64, 48, 128, 8, 32)
        TAU_LOW, TAU_HIGH, EARLY_EXIT = (0.5, 2.0, 0.05)

        def _uncertainty(h, Wu1, bu1, Wu2, bu2):
            var = jnp.var(h, axis=-1)
            log_var = jnp.log1p(var)
            norm_var = log_var / (jnp.mean(log_var) + 1e-06)
            learned = (jax.nn.gelu(h @ Wu1.T + bu1) @ Wu2.T + bu2)[..., 0]
            return jnp.clip(norm_var * 0.5 + jax.nn.sigmoid(learned) * 2.5, 0.0, 5.0)
        key = jax.random.key(seed)
        ks = jax.random.split(key, 12)
        B, S = (2, 256)
        return {'hidden_states': jax.random.normal(ks[0], (B, S, HID), dtype=jnp.float32), 'Wq': jax.random.normal(ks[1], (BOT, HID), dtype=jnp.float32) / np.sqrt(HID), 'Wr': jax.random.normal(ks[2], (RDIM, BOT), dtype=jnp.float32) / np.sqrt(BOT), 'aux_keys': jax.random.normal(ks[3], (NSLOT, BOT), dtype=jnp.float32) * 0.01, 'aux_values': jax.random.normal(ks[4], (NSLOT, HID), dtype=jnp.float32) * 0.02, 'Wvd': jax.random.normal(ks[5], (VB, HID), dtype=jnp.float32) * 0.1 / np.sqrt(HID), 'Wvu': jax.random.normal(ks[6], (HID, VB), dtype=jnp.float32) * 0.1 / np.sqrt(VB), 'Wu1': jax.random.normal(ks[7], (HID // 4, HID), dtype=jnp.float32) / np.sqrt(HID), 'bu1': jnp.zeros((HID // 4,), dtype=jnp.float32), 'Wu2': jax.random.normal(ks[8], (1, HID // 4), dtype=jnp.float32) * 0.01, 'bu2': jnp.zeros((1,), dtype=jnp.float32), 'gate_w1': jnp.float32(0.5), 'gate_bias': jnp.float32(-1.0), 'log_rel': jnp.zeros((NSLOT,), dtype=jnp.float32)}
    _L1_ffn_in = _L1_ffn_setup()
    _d = {'L0_attn_hidden_states': _L0_attn_in['hidden_states'], 'L0_attn_qkv_w': _L0_attn_in['qkv_w'], 'L0_attn_out_w': _L0_attn_in['out_w'], 'L0_attn_gate_w': _L0_attn_in['gate_w'], 'L0_attn_norm_w': _L0_attn_in['norm_w'], 'L0_ffn_W_base': _L0_ffn_in['W_base'], 'L0_ffn_b_base': _L0_ffn_in['b_base'], 'L0_ffn_W_gate': _L0_ffn_in['W_gate'], 'L0_ffn_A': _L0_ffn_in['A'], 'L0_ffn_B': _L0_ffn_in['B'], 'L1_attn_wq': _L1_attn_in['wq'], 'L1_attn_bq': _L1_attn_in['bq'], 'L1_attn_wk': _L1_attn_in['wk'], 'L1_attn_bk': _L1_attn_in['bk'], 'L1_attn_wv': _L1_attn_in['wv'], 'L1_attn_bv': _L1_attn_in['bv'], 'L1_ffn_Wq': _L1_ffn_in['Wq'], 'L1_ffn_Wr': _L1_ffn_in['Wr'], 'L1_ffn_aux_keys': _L1_ffn_in['aux_keys'], 'L1_ffn_aux_values': _L1_ffn_in['aux_values'], 'L1_ffn_Wvd': _L1_ffn_in['Wvd'], 'L1_ffn_Wvu': _L1_ffn_in['Wvu'], 'L1_ffn_Wu1': _L1_ffn_in['Wu1'], 'L1_ffn_bu1': _L1_ffn_in['bu1'], 'L1_ffn_Wu2': _L1_ffn_in['Wu2'], 'L1_ffn_bu2': _L1_ffn_in['bu2'], 'L1_ffn_gate_w1': _L1_ffn_in['gate_w1'], 'L1_ffn_gate_bias': _L1_ffn_in['gate_bias'], 'L1_ffn_log_rel': _L1_ffn_in['log_rel']}
    _x0 = _d['L0_attn_hidden_states']
    _d['L0_attn_hidden_states'] = jax.random.normal(jax.random.fold_in(jax.random.key(seed), 1), (2, 1024, 512), dtype=_x0.dtype)
    del _x0
    return _d

def reference(L0_attn_hidden_states, L0_attn_qkv_w, L0_attn_out_w, L0_attn_gate_w, L0_attn_norm_w, L0_ffn_W_base, L0_ffn_b_base, L0_ffn_W_gate, L0_ffn_A, L0_ffn_B, L1_attn_wq, L1_attn_bq, L1_attn_wk, L1_attn_bk, L1_attn_wv, L1_attn_bv, L1_ffn_Wq, L1_ffn_Wr, L1_ffn_aux_keys, L1_ffn_aux_values, L1_ffn_Wvd, L1_ffn_Wvu, L1_ffn_Wu1, L1_ffn_bu1, L1_ffn_Wu2, L1_ffn_bu2, L1_ffn_gate_w1, L1_ffn_gate_bias, L1_ffn_log_rel):

    def _L0_attn_ref(hidden_states, qkv_w, out_w, gate_w, norm_w):
        import jax, jax.numpy as jnp
        import numpy as np
        BATCH, SEQ, HIDDEN = (2, 512, 512)
        HEADS, HEAD_DIM, BLOCK = (32, 128, 32)
        LAYER_IDX, N_LAYERS = (1, 32)
        EPS = 1e-05

        def _decays():
            base = 1.0 / 2.0 ** (8.0 / HEADS)
            exponent = jnp.arange(HEADS, dtype=jnp.float32) + 1.0
            factor = 1.0 - LAYER_IDX / (N_LAYERS - 1 + 1e-05) + 1e-05
            slope = (base ** exponent * factor)[:, None, None]
            r = jnp.arange(BLOCK, dtype=jnp.float32) + 1.0
            q_decay = jnp.exp(-slope * r[:, None])
            k_decay = jnp.exp(-slope * (BLOCK - r)[:, None])
            diff = r[:, None] - r[None, :]
            diag = slope[None] * diff[None, None]
            diag = jnp.where(diag >= 0, -diag, -jnp.inf)
            diag_decay = jnp.exp(diag)
            block_decay = jnp.exp(-slope * BLOCK)
            return (q_decay, k_decay, diag_decay, block_decay)
        b, s, _ = hidden_states.shape
        h, d, bs = (HEADS, HEAD_DIM, BLOCK)
        nb = s // bs
        q_decay, k_decay, diag_decay, block_decay = _decays()
        qkv = jax.nn.silu(hidden_states @ qkv_w.T)
        qkv = qkv.reshape(b, s, h, 3, d)
        q = jnp.moveaxis(qkv[:, :, :, 0], 2, 1)
        k = jnp.moveaxis(qkv[:, :, :, 1], 2, 1)
        v = jnp.moveaxis(qkv[:, :, :, 2], 2, 1)

        def to_blocks(x):
            return jnp.moveaxis(x.reshape(b, h, nb, bs, d), 2, 0)
        qb, kb, vb = (to_blocks(q), to_blocks(k), to_blocks(v))

        def step(kv, blk):
            cq, ck, cv = blk
            scores = jnp.einsum('bhnd,bhmd->bhnm', cq, ck) * diag_decay
            intra = jnp.einsum('bhnm,bhmd->bhnd', scores, cv)
            inter = jnp.einsum('bhnd,bhde->bhne', cq * q_decay, kv)
            kv_next = kv * block_decay + jnp.einsum('bhnd,bhne->bhde', ck * k_decay, cv)
            return (kv_next, intra + inter)
        kv0 = jnp.zeros((b, h, d, d), hidden_states.dtype)
        _, out_blocks = jax.lax.scan(step, kv0, (qb, kb, vb))
        attn = jnp.moveaxis(out_blocks, 0, 2)
        attn = attn.reshape(b, h, s, d).transpose(0, 2, 1, 3).reshape(b, s, h * d)
        xf = attn.astype(jnp.float32)
        xf = xf * jax.lax.rsqrt(jnp.mean(xf * xf, axis=-1, keepdims=True) + EPS)
        normed = norm_w * xf.astype(attn.dtype)
        gate = jax.nn.sigmoid(hidden_states @ gate_w.T)
        return gate * normed @ out_w.T

    def _L0_ffn_ref(x, W_base, b_base, W_gate, A, B):
        import jax, jax.numpy as jnp
        import numpy as np
        BATCH, TOK, DIM, OUT = (4, 256, 512, 512)
        E, R, TOP_K = (8, 16, 2)
        SCALING = 16.0 / R
        result = jnp.einsum('bnd,od->bno', x, W_base) + b_base
        logits = jnp.einsum('bnd,ed->bne', x, W_gate)
        probs = jax.nn.softmax(logits.astype(jnp.float32), axis=-1)
        top_p, top_i = jax.lax.top_k(probs, TOP_K)
        top_p = top_p / jnp.sum(top_p, axis=-1, keepdims=True)
        top_p = top_p.astype(x.dtype)
        route_w = jnp.sum(jax.nn.one_hot(top_i, E, dtype=x.dtype) * top_p[..., None], axis=-2)
        h = jnp.einsum('bnd,erd->bner', x, A)
        hw = h * route_w[..., None]
        delta = jnp.einsum('bner,eor->bno', hw, B)
        return result + delta * SCALING

    def _L1_attn_ref(x, wq, bq, wk, bk, wv, bv):
        import jax, jax.numpy as jnp
        import numpy as np
        EMBED = 512
        H = 32
        KV = 8
        D = EMBED // H
        REP = H // KV

        def _rope(t, cos, sin):
            t = t.reshape(*t.shape[:-1], 2, D // 2)
            t1, t2 = (t[..., 0, :], t[..., 1, :])
            return jnp.concatenate([t1 * cos - t2 * sin, t1 * sin + t2 * cos], axis=-1)
        B, S, E = x.shape
        xq = (x @ wq + bq).reshape(B, S, H, D)
        xk = (x @ wk + bk).reshape(B, S, KV, D)
        xv = (x @ wv + bv).reshape(B, S, KV, D)
        inv_freq = 1.0 / 10000.0 ** (jnp.arange(0, D, 2, dtype=jnp.float32) / D)
        ang = jnp.arange(S, dtype=jnp.float32)[:, None] * inv_freq[None, :]
        cos, sin = (jnp.cos(ang)[:, None, :], jnp.sin(ang)[:, None, :])
        q = _rope(xq, cos, sin)
        k = _rope(xk, cos, sin)
        k = jnp.repeat(k, REP, axis=2)
        v = jnp.repeat(xv, REP, axis=2)
        scores = jnp.einsum('bqhd,bkhd->bhqk', q, k) / jnp.sqrt(jnp.float32(D))
        probs = jax.nn.softmax(scores.astype(jnp.float32), axis=-1)
        out = jnp.einsum('bhqk,bkhd->bqhd', probs, v).reshape(B, S, E)
        return out

    def _L1_ffn_ref(hidden_states, Wq, Wr, aux_keys, aux_values, Wvd, Wvu, Wu1, bu1, Wu2, bu2, gate_w1, gate_bias, log_rel):
        import jax, jax.numpy as jnp
        import numpy as np
        HID, BOT, RDIM, NSLOT, K, VB = (512, 64, 48, 128, 8, 32)
        TAU_LOW, TAU_HIGH, EARLY_EXIT = (0.5, 2.0, 0.05)

        def _uncertainty(h, Wu1, bu1, Wu2, bu2):
            var = jnp.var(h, axis=-1)
            log_var = jnp.log1p(var)
            norm_var = log_var / (jnp.mean(log_var) + 1e-06)
            learned = (jax.nn.gelu(h @ Wu1.T + bu1) @ Wu2.T + bu2)[..., 0]
            return jnp.clip(norm_var * 0.5 + jax.nn.sigmoid(learned) * 2.5, 0.0, 5.0)
        query = hidden_states @ Wq.T
        rq = query @ Wr.T
        rk = aux_keys @ Wr.T
        router_scores = jnp.einsum('bsr,nr->bsn', rq, rk) / np.sqrt(RDIM) + log_rel
        top_scores, top_idx = jax.lax.top_k(router_scores, K)
        sel_keys = aux_keys[top_idx]
        attn = jnp.einsum('bsd,bskd->bsk', query, sel_keys) / np.sqrt(BOT) + log_rel[top_idx]
        w = jax.nn.softmax(attn, axis=-1)
        sel_vals = aux_values[top_idx]
        aux_out = jnp.einsum('bsk,bskh->bsh', w, sel_vals)
        aux_out = aux_out @ Wvd.T @ Wvu.T
        u = _uncertainty(hidden_states, Wu1, bu1, Wu2, bu2)
        u_norm = jnp.clip((u - TAU_LOW) / (TAU_HIGH - TAU_LOW), 0.0, 1.0)
        gate = jax.nn.sigmoid(gate_w1 * u_norm + gate_bias)
        gate = jnp.where(gate < EARLY_EXIT, 0.0, gate)
        return hidden_states + gate[..., None] * aux_out
    x = L0_attn_hidden_states
    x = x + 0.5 * _L0_ffn_ref(_layernorm(x, axis=-1), L0_ffn_W_base, L0_ffn_b_base, L0_ffn_W_gate, L0_ffn_A, L0_ffn_B)
    x = x + _L0_attn_ref(_layernorm(x, axis=-1), L0_attn_qkv_w, L0_attn_out_w, L0_attn_gate_w, L0_attn_norm_w)
    x = x + 0.5 * _L0_ffn_ref(_layernorm(x, axis=-1), L0_ffn_W_base, L0_ffn_b_base, L0_ffn_W_gate, L0_ffn_A, L0_ffn_B)
    x = x + 0.5 * _L1_ffn_ref(_layernorm(x, axis=-1), L1_ffn_Wq, L1_ffn_Wr, L1_ffn_aux_keys, L1_ffn_aux_values, L1_ffn_Wvd, L1_ffn_Wvu, L1_ffn_Wu1, L1_ffn_bu1, L1_ffn_Wu2, L1_ffn_bu2, L1_ffn_gate_w1, L1_ffn_gate_bias, L1_ffn_log_rel)
    x = x + _L1_attn_ref(_layernorm(x, axis=-1), L1_attn_wq, L1_attn_bq, L1_attn_wk, L1_attn_bk, L1_attn_wv, L1_attn_bv)
    x = x + 0.5 * _L1_ffn_ref(_layernorm(x, axis=-1), L1_ffn_Wq, L1_ffn_Wr, L1_ffn_aux_keys, L1_ffn_aux_values, L1_ffn_Wvd, L1_ffn_Wvu, L1_ffn_Wu1, L1_ffn_bu1, L1_ffn_Wu2, L1_ffn_bu2, L1_ffn_gate_w1, L1_ffn_gate_bias, L1_ffn_log_rel)
    return x

_drawn_inputs = setup_inputs


def setup_inputs(seed=0):
    import zlib

    import numpy as np

    out = dict(_drawn_inputs(seed))
    spreads = {'L0_attn_norm_w': (1.0, 0.2), 'L1_ffn_bu1': (0.0, 2.0), 'L1_ffn_log_rel': (0.0, 2.0)}
    factors = {'L0_ffn_b_base': 5.472,
     'L1_attn_wq': 8.0,
     'L1_attn_bq': 8.0,
     'L1_attn_wk': 8.0,
     'L1_attn_bk': 8.0,
     'L1_attn_bv': 5.538,
     'L1_ffn_Wq': 54.985,
     'L1_ffn_Wr': 64.0,
     'L1_ffn_aux_keys': 55.481,
     'L1_ffn_aux_values': 50.843,
     'L1_ffn_Wvd': 51.381,
     'L1_ffn_Wvu': 50.881,
     'L1_ffn_Wu1': 64.0,
     'L1_ffn_Wu2': 64.0}
    for name, (base, spread) in spreads.items():
        noise = np.random.default_rng([zlib.crc32(name.encode()), seed]).standard_normal(out[name].shape)
        drawn = base * np.exp(spread * noise) if base else spread * noise
        out[name] = jnp.asarray(drawn.astype(out[name].dtype))
    for name, factor in factors.items():
        out[name] = (out[name] * factor).astype(out[name].dtype)
    return out
```

```python
from contextlib import ExitStack

import numpy as np

import concourse.bass as bass
from concourse import mybir

F32 = mybir.dt.float32
F32R = mybir.dt.float32r
BF16 = mybir.dt.bfloat16
ALU = mybir.AluOpType
ACT = mybir.ActivationFunctionType
AX = mybir.AxisListType.X

P = 128
D = 512
KC = D // P
NT = 16
T = NT * P
B = 2
TB = NT // B
EPS = 1e-5

E, R = 8, 16
LH = 32
G = 4
GT = T // G
CH = GT // P
BOT, RDIM, NSLOT, VB = 64, 48, 128, 32
H, KV, HD = 32, 8, 16
REP = H // KV
QK = H + KV
NSPLIT = 6
KS = NSPLIT * HD
VW = 32

SENTINEL, TAKEN, TAKEN_LINE = -3.0e38, -3.3e38, -3.2e38
LOW = -1.0e30
GELU_SCALE = float(np.sqrt(2.0 / np.pi))


def fixed_below(value, n):
    return type(value) is int and value < n


class Chain:

    def __init__(self, eng, sem):
        self.eng, self.sem, self.n, self.base = eng, sem, 0, 0

    def __call__(self, ins):
        self.n += 1
        ins.then_inc(self.sem, 1)
        self.eng.wait_ge(self.sem, self.base + self.n)


def apart(eng, sem):
    eng.sem_inc(sem, 1)


def looped(chains, eng, start, stop, steps, body):
    (chain,) = chains if chains else (None,)
    with eng.Fori(start, stop) as i:
        eng.get_value_cache().nocache = True
        if chain:
            before = chain.n
            chain.base = (i - start) * steps
        body(i)
        if chain:
            assert chain.n - before == steps, (chain.n - before, steps)
            chain.base = 0
            chain.n = before + steps * (stop - start)


def program(nc, a, out):
    ctx = ExitStack()
    with ctx:
        def sb(name, shape, dt=F32, where=ctx):
            return where.enter_context(nc.sbuf_tensor(name, shape, dt))

        sems = {}

        def sem(name):
            if name not in sems:
                sems[name] = ctx.enter_context(nc.semaphore(name))
            return sems[name]

        bank = [ctx.enter_context(nc.psum_tensor(f"bank{i}", [P, 512], F32)) for i in range(8)]

        x = sb("x", [P, NT, D])
        ident = sb("ident", [P, P])
        identb = sb("identb", [P, P], BF16)
        ones = sb("ones", [P, P])
        stats = sb("stats", [P, NT, 6])
        rstd = sb("rstd", [P, NT])
        nmr = sb("nmr", [P, NT])
        ve = sb("ve", [P, NT])
        sm = [sb(f"sm{i}", [P, NT]) for i in range(4)]
        hb = sb("half_bias", [P, D])
        wb_hi = sb("wb_hi", [P, KC, D], F32R)
        wb_lo = sb("wb_lo", [P, KC, D], F32R)
        wa_hi = sb("wa_hi", [P, KC, 256], F32R)
        wa_lo = sb("wa_lo", [P, KC, 256], F32R)
        lora_b = sb("lora_b", [P, D])
        x_dram = nc.dram_tensor("x_kept", [NT, P, D], F32, kind="Internal").ap()

        tctx = ExitStack()
        xn = sb("xn", [P, 2, D], where=tctx)
        xt_hi = sb("xt_hi", [P, 2, KC, P], F32R, where=tctx)
        xt_lo = sb("xt_lo", [P, 2, KC, P], F32R, where=tctx)
        xb = sb("xb", [P, 2, D], where=tctx)
        raw = sb("raw", [P, D], where=tctx)
        lg = sb("lg", [P, 2, 16], where=tctx)
        top = sb("top", [P, 2, 8], where=tctx)
        rep = sb("rep", [P, 2, 8], where=tctx)
        rest = sb("rest", [P, 2, 16], where=tctx)
        ex = sb("ex", [P, 2, 8], where=tctx)
        mk = sb("mk", [P, 2, 8], where=tctx)
        rw = sb("rw", [P, 2, 8], where=tctx)
        c1 = sb("c1", [P, 2, 8], where=tctx)
        hw = sb("hw", [P, 2, P], where=tctx)
        hwt = sb("hwt", [P, 2, P], where=tctx)
        w1_hi = sb("w1_hi", [P, KC, 384], F32R, where=tctx)
        w1_lo = sb("w1_lo", [P, KC, 384], F32R, where=tctx)
        v3 = sb("v3", [P, D], where=tctx)
        lrel = sb("lrel", [P, NSLOT], where=tctx)
        bu1 = sb("bu1", [P, P], where=tctx)
        wu2 = sb("wu2", [P, P], where=tctx)
        sc3 = sb("sc3", [P, 4], where=tctx)
        nv = sb("nv", [P, NT], where=tctx)
        lv = sb("lv", [P, NT], where=tctx)
        lsum = sb("lsum", [P, 2], where=tctx)
        mean1 = sb("mean1", [P, 2], where=tctx)
        rt = sb("rt", [P, 2, NSLOT], where=tctx)
        rt2 = sb("rt2", [P, 2, NSLOT], where=tctx)
        am = sb("am", [P, 2, NSLOT], where=tctx)
        pr = sb("pr", [P, 2, NSLOT], where=tctx)
        prt = sb("prt", [P, 2, NSLOT], where=tctx)
        gu = sb("gu", [P, 2, P], where=tctx)
        gc = sb("gc", [P, 2, P], where=tctx)
        gt = sb("gt", [P, 2, P], where=tctx)
        gg = sb("gg", [P, 2, P], where=tctx)
        small = sb("small", [P, 256], where=tctx)
        small2 = sb("small2", [P, 256], where=tctx)
        v2t = sb("v2t", [P, NSLOT], where=tctx)
        qk = sb("qk", [P, NT, QK, HD], where=tctx)
        vv = sb("vv", [P, NT, KV, HD], where=tctx)
        actx = ExitStack()
        wq_hi = sb("wq_hi", [P, KC, 768], F32R, where=actx)
        wq_lo = sb("wq_lo", [P, KC, 768], F32R, where=actx)
        bqkv = sb("bqkv", [P, 768], where=actx)
        rope = sb("rope", [P, TB, 2, HD], where=actx)
        qkb = sb("qkb", [P, 2, QK, HD], where=actx)
        rot = sb("rot", [P, 2, QK, HD], where=actx)
        actx.close()
        qs = sb("qs", [P, TB, REP, KS], BF16, where=tctx)
        ks = sb("ks", [P, TB, KS], BF16, where=tctx)
        qst = sb("qst", [P, 2, REP, TB * P], BF16, where=tctx)
        kst = sb("kst", [P, 2, TB * P], BF16, where=tctx)
        vst = sb("vst", [P, 2, TB, VW], where=tctx)
        pp = sb("pp", [P, 8, 512], where=tctx)
        mx = sb("mx", [P, REP, TB, 2], where=tctx)
        m1 = sb("m1", [P, REP, TB], where=tctx)
        nm = sb("nm", [P, 2, REP * TB], BF16, where=tctx)
        nmt = sb("nmt", [2 * REP * TB, P], BF16, where=tctx)
        pvs = raw
        qr = xb[:, 0, :].rearrange("p (t j d) -> p t j d", t=TB, j=REP)
        kr = xn[:, 0, 0:TB * HD].rearrange("p (t d) -> p t d", t=TB)
        rec = sb("rec", [P, 4, REP], where=tctx)
        oo = sb("oo", [P, 4, REP, HD], where=tctx)
        tctx.close()

        lctx = ExitStack()
        l_xn = sb("l_xn", [P, 2, D], where=lctx)
        xa_hi = sb("xa_hi", [P, KC, T], F32R, where=lctx)
        xa_lo = sb("xa_lo", [P, KC, T], F32R, where=lctx)
        sq = sb("sq", [P, T], where=lctx)
        w_raw = sb("w_raw", [P, 4, KC, P], where=lctx)
        w_hi = sb("w_hi", [P, 4, KC, P], F32R, where=lctx)
        w_lo = sb("w_lo", [P, 4, KC, P], F32R, where=lctx)
        ow_raw = sb("ow_raw", [P, D], where=lctx)
        ow_hi = sb("ow_hi", [P, D], F32R, where=lctx)
        ow_lo = sb("ow_lo", [P, D], F32R, where=lctx)
        dt_tab = sb("dt_tab", [P, 2, P], where=lctx)
        kdec = sb("kdec", [P, LH], where=lctx)
        bdec = sb("bdec", [P, LH], where=lctx)
        nwh = sb("nwh", [P, LH], where=lctx)
        qT = sb("qT", [P, 2, GT], where=lctx)
        kT = sb("kT", [P, 2, GT], where=lctx)
        vT = sb("vT", [P, 2, GT], where=lctx)
        gate = sb("gate", [P, GT], where=lctx)
        qd = sb("qd", [P, GT], where=lctx)
        ktok = sb("ktok", [P, GT], where=lctx)
        vtok = sb("vtok", [P, GT], where=lctx)
        sc = sb("sc", [P, GT], where=lctx)
        kvs = sb("kvs", [P, CH, P], where=lctx)
        at = sb("at", [P, GT], where=lctx)
        at2 = sb("at2", [P, GT], where=lctx)
        y1 = sb("y1", [P, GT], where=lctx)
        y_hi = sb("y_hi", [P, GT], F32R, where=lctx)
        y_lo = sb("y_lo", [P, GT], F32R, where=lctx)
        rnorm = sb("rnorm", [P, NT], where=lctx)
        x_in = sb("x_in", [P, 2, D], where=lctx)
        lctx.close()

        PHASES = ["ffn_a", "lin", "ffn_b", "mem_a", "att", "mem_b"]
        phase_done = {p: sem(f"{p}_done") for p in PHASES}
        x_loaded, consts_loaded = sem("x_loaded"), sem("consts_loaded")
        pe_steps, act_steps = sem("pe_steps"), sem("act_steps")
        dve_steps, pool_steps = sem("dve_steps"), sem("pool_steps")

        PIECES = {"ffn_a": 2 * KC, "mem_a": KC, "att": 2 * KC}
        PRODUCT = ["ffn_a", "ffn_b", "mem_a", "att", "mem_b"]
        RAISED = {}
        for what in ("bn", "xn", "xt", "xhi", "xlo"):
            RAISED[what] = {p: NT for p in PHASES}
        for what in ("ve", "sd", "norm"):
            RAISED[what] = {p: 1 for p in PHASES}
        for what in ("piece_hi", "piece_lo"):
            RAISED[what] = PIECES
        RAISED["piece"] = {p: 16 * n for p, n in PIECES.items()}
        RAISED["used"] = {p: NT for p in PRODUCT}
        for what in ("a", "lg", "ex", "ht", "hw", "hwt", "xb"):
            RAISED[what] = {p: NT for p in ("ffn_a", "ffn_b")}
        for what in ("x", "y"):
            RAISED[what] = {p: NT for p in ("ffn_a", "ffn_b", "mem_a", "mem_b")}
        for what in ("read", "pr", "prt", "pt", "cubic", "gt", "am", "learned", "t1", "u", "t2"):
            RAISED[what] = {p: NT for p in ("mem_a", "mem_b")}
        for what in ("ls", "lm", "nv", "vh", "lv"):
            RAISED[what] = {p: 1 for p in ("mem_a", "mem_b")}

        def past(phase, what):
            return sum(n for p, n in RAISED[what].items() if PHASES.index(p) < PHASES.index(phase))

        block = ctx.enter_context(nc.Block())

        def before(phase):
            n = PHASES.index(phase)
            return phase_done[PHASES[n - 1]] if n else None

        def enter(eng, phase):
            if before(phase) is not None:
                eng.wait_ge(before(phase), 1)

        def pieces(phase):
            if phase == "ffn_a":
                return ([(a["w_base_t"][:, k, :], wb_hi[:, k, :], wb_lo[:, k, :], D) for k in range(KC)]
                        + [(a["w_ag_t"][:, k, :], wa_hi[:, k, :], wa_lo[:, k, :], 256) for k in range(KC)])
            if phase == "mem_a":
                return [(a["wu1_t"][:, k, :], w1_hi[:, k, 256:384], w1_lo[:, k, 256:384], P) for k in range(KC)]
            return [(a["wqkv"][:, k, c:c + 384], wq_hi[:, k, c:c + 384], wq_lo[:, k, c:c + 384], 384)
                    for k in range(KC) for c in (0, 384)]

        def load_pieces_sync(sp, phase):
            for n, (src, _, _, w) in enumerate(pieces(phase)):
                if n:
                    sp.wait_ge(sem("piece_lo"), past(phase, "piece_lo") + n)
                sp.dma_start(raw[:, 0:w], src).then_inc(sem("piece"), 16)

        def split_pieces_act(act, phase):
            for n, (_, hi, _, w) in enumerate(pieces(phase)):
                act.wait_ge(sem("piece"), past(phase, "piece") + 16 * (n + 1))
                act.activation(hi, raw[:, 0:w], ACT.Copy).then_inc(sem("piece_hi"), 1)

        def split_pieces_dve(dve, phase):
            for n, (_, hi, lo, w) in enumerate(pieces(phase)):
                dve.wait_ge(sem("piece_hi"), past(phase, "piece_hi") + n + 1)
                dve.tensor_tensor(lo, raw[:, 0:w], hi.bitcast(F32), ALU.subtract)\
                   .then_inc(sem("piece_lo"), 1)

        def stats_dve(dve, chain, phase):
            done = sem("bn")
            with dve.Fori(0, NT) as t:
                dve.bn_stats(stats[:, t, :], x[:, t, :]).then_inc(done, 1)
            dve.wait_ge(done, past(phase, "bn") + NT)
            s, d, m2, q = sm
            chain(dve.tensor_tensor(s[:, :], stats[:, :, 1], stats[:, :, 4], ALU.add))
            chain(dve.tensor_tensor(d[:, :], stats[:, :, 1], stats[:, :, 4], ALU.subtract))
            chain(dve.tensor_tensor(m2[:, :], stats[:, :, 2], stats[:, :, 5], ALU.add))
            chain(dve.scalar_tensor_tensor(q[:, :], d[:, :], 0.25, d[:, :], ALU.mult, ALU.mult))
            chain(dve.scalar_tensor_tensor(q[:, :], m2[:, :], 1.0 / D, q[:, :], ALU.mult, ALU.add))
            dve.tensor_scalar(ve[:, :], q[:, :], EPS, None, ALU.add).then_inc(sem("ve"), 1)
            dve.wait_ge(sem("sd"), past(phase, "sd") + 1)
            chain(dve.reciprocal(rstd[:, :], rstd[:, :]))
            chain(dve.tensor_tensor(d[:, :], rstd[:, :], rstd[:, :], ALU.mult))
            chain(dve.scalar_tensor_tensor(d[:, :], d[:, :], -0.5, ve[:, :], ALU.mult, ALU.mult))
            chain(dve.scalar_tensor_tensor(rstd[:, :], d[:, :], 1.5, rstd[:, :], ALU.add, ALU.mult))
            dve.scalar_tensor_tensor(nmr[:, :], s[:, :], -0.5, rstd[:, :], ALU.mult, ALU.mult)\
               .then_inc(sem("norm"), 1)
            dve.wait_ge(sem("norm"), past(phase, "norm") + 1)

        def stats_act(act, phase):
            act.wait_ge(sem("ve"), past(phase, "ve") + 1)
            act.activation(rstd[:, :], ve[:, :], ACT.Sqrt).then_inc(sem("sd"), 1)

        def norm_dve(dve, phase, t, s, first, buf=None):
            buf = xn if buf is None else buf
            if not first:
                dve.wait_ge(sem("xt"), past(phase, "xt") + t - 1)
            dve.tensor_scalar(buf[:, s, :], x[:, t, :], rstd[:, bass.ds(t, 1)], nmr[:, bass.ds(t, 1)],
                              ALU.mult, ALU.add).then_inc(sem("xn"), 1)

        def transpose_pe(pe, phase, t, s, first, ps, buf=None):
            buf = xn if buf is None else buf
            pe.wait_ge(sem("xn"), past(phase, "xn") + t + 1)
            if not first:
                pe.wait_ge(sem("xlo"), past(phase, "xlo") + t - 1)
            for k in range(KC):
                last = pe.transpose(ps[:, k * P:(k + 1) * P], buf[:, s, k * P:(k + 1) * P], ident[:, :])
            last.then_inc(sem("xt"), 1)

        def hi_act(act, phase, t, s, first, ps):
            act.wait_ge(sem("xt"), past(phase, "xt") + t + 1)
            if not first:
                act.wait_ge(sem("used"), past(phase, "used") + t - 1)
            act.activation(xt_hi[:, s, :, :], ps[:, :].rearrange("p (k n) -> p k n", k=KC), ACT.Copy)\
               .then_inc(sem("xhi"), 1)

        def lo_dve(dve, phase, t, s, ps):
            dve.wait_ge(sem("xhi"), past(phase, "xhi") + t + 1)
            dve.tensor_tensor(xt_lo[:, s, :, :], ps[:, :].rearrange("p (k n) -> p k n", k=KC),
                              xt_hi[:, s, :, :].bitcast(F32), ALU.subtract).then_inc(sem("xlo"), 1)

        def product_pe(pe, ps, s, hi, lo, c0, c1_):
            n = 0
            for left, right in ((xt_hi, hi), (xt_hi, lo), (xt_lo, hi)):
                for k in range(KC):
                    last = pe.matmul(ps, left[:, s, k, :], right[:, k, c0:c1_], start=(n == 0), stop=(n == 3 * KC - 1))
                    n += 1
            return last

        def tiles(eng, chain, steps, tile):
            for s in (0, 1):
                tile(s, s, True, False)

            def pair(j):
                for s in (0, 1):
                    tile(2 * j + s, s, False, False)
            looped([chain] if chain else [], eng, 1, NT // 2 - 1, 2 * steps, pair)
            for s in (0, 1):
                tile(NT - 2 + s, s, False, s == 1)

        FFN_XT = [bank[0], bank[1]]
        FFN_A = [bank[2], bank[3]]
        FFN_Y = [bank[4], bank[5]]
        FFN_H = [bank[6], bank[7]]

        def ffn_pe(pe, phase):
            transpose_pe(pe, phase, 0, 0, True, FFN_XT[0])

            def tile(t, s, first, last):
                if not last:
                    transpose_pe(pe, phase, t + 1, 1 - s, first and s == 0, FFN_XT[1 - s])
                pe.wait_ge(sem("xlo"), past(phase, "xlo") + t + 1)
                if not first:
                    pe.wait_ge(sem("hw"), past(phase, "hw") + t - 1)
                product_pe(pe, FFN_A[s][:, 0:256], s, wa_hi, wa_lo, 0, 256).then_inc(sem("a"), 1)
                if not first:
                    pe.wait_ge(sem("x"), past(phase, "x") + t - 1)
                n = 0
                for left, right in ((xt_hi, wb_hi), (xt_hi, wb_lo), (xt_lo, wb_hi)):
                    for k in range(KC):
                        mm = pe.matmul(FFN_Y[s][:, :], left[:, s, k, :], right[:, k, :], start=(n == 0), stop=False)
                        n += 1
                mm.then_inc(sem("used"), 1)
                pe.wait_ge(sem("hw"), past(phase, "hw") + t + 1)
                if not first:
                    pe.wait_ge(sem("hwt"), past(phase, "hwt") + t - 1)
                pe.transpose(FFN_H[s][:, 0:P], hw[:, s, :], ident[:, :]).then_inc(sem("ht"), 1)
                pe.wait_ge(sem("hwt"), past(phase, "hwt") + t + 1)
                pe.matmul(FFN_Y[s][:, :], hwt[:, s, :], lora_b[:, :], start=False, stop=True)\
                  .then_inc(sem("y"), 1)

            tiles(pe, None, 0, tile)

        def ffn_act(act, phase):
            hi_act(act, phase, 0, 0, True, FFN_XT[0])

            def tile(t, s, first, last):
                if not last:
                    hi_act(act, phase, t + 1, 1 - s, first and s == 0, FFN_XT[1 - s])
                act.wait_ge(sem("lg"), past(phase, "lg") + t + 1)
                act.activation(ex[:, s, :], lg[:, s, 0:8], ACT.Exp, bias=c1[:, s, 0:1]).then_inc(sem("ex"), 1)
                act.wait_ge(sem("ht"), past(phase, "ht") + t + 1)
                if not first:
                    act.wait_ge(sem("y"), past(phase, "y") + t - 1)
                act.activation(hwt[:, s, :], FFN_H[s][:, 0:P], ACT.Copy).then_inc(sem("hwt"), 1)

            tiles(act, None, 0, tile)

        def ffn_pool(pool, phase):
            def tile(t, s, first, last):
                if not first:
                    pool.wait_ge(sem("x"), past(phase, "x") + t - 1)
                pool.tensor_tensor(xb[:, s, :], x[:, t, :], hb[:, :], ALU.add).then_inc(sem("xb"), 1)

            tiles(pool, None, 0, tile)

        def ffn_dve(dve, chain, phase):
            norm_dve(dve, phase, 0, 0, True)
            lo_dve(dve, phase, 0, 0, FFN_XT[0])

            def tile(t, s, first, last):
                if not last:
                    norm_dve(dve, phase, t + 1, 1 - s, first and s == 0)
                    lo_dve(dve, phase, t + 1, 1 - s, FFN_XT[1 - s])
                A_ = FFN_A[s]
                dve.wait_ge(sem("a"), past(phase, "a") + t + 1)
                chain(dve.tensor_copy(lg[:, s, 0:8], A_[:, P:P + 8]))
                apart(dve, sem("apart_dve"))
                chain(dve.max(top[:, s, :], lg[:, s, 0:8]))
                dve.tensor_scalar(c1[:, s, 0:1], top[:, s, 0:1], -1.0, None, ALU.mult).then_inc(sem("lg"), 1)
                chain(dve.tensor_copy(rep[:, s, 0:2], top[:, s, 0:2]))
                apart(dve, sem("apart_dve"))
                chain(dve.match_replace(out=rest[:, s, :], in_to_replace=rep[:, s, :], in_values=lg[:, s, :],
                                        imm_value=TAKEN))
                chain(dve.tensor_scalar(mk[:, s, :], rest[:, s, 0:8], TAKEN_LINE, None, ALU.is_lt))
                dve.wait_ge(sem("ex"), past(phase, "ex") + t + 1)
                chain(dve.tensor_tensor(rw[:, s, :], ex[:, s, :], mk[:, s, :], ALU.mult))
                chain(dve.tensor_reduce(c1[:, s, 1:2], rw[:, s, :], AX, ALU.add))
                chain(dve.reciprocal(c1[:, s, 2:3], c1[:, s, 1:2]))
                chain(dve.tensor_scalar(rw[:, s, :], rw[:, s, :], c1[:, s, 2:3], None, ALU.mult))
                if not first:
                    dve.wait_ge(sem("ht"), past(phase, "ht") + t - 1)
                dve.tensor_tensor(hw[:, s, :].rearrange("p (e r) -> p e r", e=E),
                                  A_[:, 0:P].rearrange("p (e r) -> p e r", e=E),
                                  rw[:, s, :].unsqueeze(2).to_broadcast([P, E, R]), ALU.mult)\
                   .then_inc(sem("hw"), 1)
                dve.wait_ge(sem("y"), past(phase, "y") + t + 1)
                dve.wait_ge(sem("xb"), past(phase, "xb") + t + 1)
                dve.scalar_tensor_tensor(x[:, t, :], FFN_Y[s][:, :], 0.5, xb[:, s, :], ALU.mult, ALU.add)\
                   .then_inc(sem("x"), 1)

            tiles(dve, chain, 9, tile)
            dve.wait_ge(sem("x"), past(phase, "x") + NT)
            dve.sem_inc(phase_done[phase], 1)

        QQ, KK, VV, GG = range(4)
        PJ = [bank[0], bank[1]]
        TRK, TRV, KVP, ATP = bank[2], bank[3], bank[4], bank[5]
        OUTP = [bank[6], bank[7]]
        SLOTS = LH * G
        KINDS = ["q", "k", "v", "g", "o"]

        def c_(c):
            return slice(c * P, (c + 1) * P)

        def heads(eng, chain, steps, slot):
            def head(h, first):
                for g in range(G):
                    slot(4 * h + g, h, g, h if g >= 1 else h - 1, h if g >= 2 else h - 1,
                         not first or g >= 1, not first or g >= 2, True)
            head(0, True)
            looped([chain] if chain else [], eng, 1, LH, steps, lambda h: head(h, False))
            slot(SLOTS, LH, 0, LH - 1, LH - 1, True, True, False)
            slot(SLOTS + 1, LH, 1, LH, LH - 1, False, True, False)

        def lin_pe(pe):
            def tile(t, s, first, last):
                transpose_pe(pe, "lin", t, s, first, bank[s], l_xn)
            tiles(pe, None, 0, tile)
            pe.wait_ge(sem("xlo"), past("lin", "xlo") + NT)

            def project(kind, h, g, ps):
                pe.wait_ge(sem(f"w_lo_{KINDS[kind]}"), h + 1)
                n = 0
                for w, xs in ((w_hi, xa_hi), (w_hi, xa_lo), (w_lo, xa_hi)):
                    for k in range(KC):
                        last = pe.matmul(ps[:, :], w[:, kind, k, :], xs[:, k, g * GT:(g + 1) * GT],
                                         start=(n == 0), stop=(n == 3 * KC - 1))
                        n += 1
                last.then_inc(sem(f"proj_{KINDS[kind]}"), 1)

            def slot(k, h, g, h1, h2, has1, has2, has0):
                r, r1 = g % 2, (g + 1) % 2
                m, g1 = k - 1, (g - 1) % G
                if has0:
                    if has1:
                        pe.wait_ge(sem("act_v"), k)
                    project(QQ, h, g, PJ[0])
                if has1:
                    pe.wait_ge(sem("act_k"), m + 1)
                    if has2:
                        pe.wait_ge(sem("masked"), m)
                    for c in range(CH):
                        mm = pe.transpose(TRK[:, c_(c)], kT[:, r1, c_(c)], ident[:, :])
                    mm.then_inc(sem("tr_k"), 1)
                    pe.wait_ge(sem("act_v"), m + 1)
                    for c in range(CH):
                        mm = pe.transpose(TRV[:, c_(c)], vT[:, r1, c_(c)], ident[:, :])
                    mm.then_inc(sem("tr_v"), 1)
                if has2:
                    pe.wait_ge(sem("w_lo_o"), h2 + 1)
                    pe.wait_ge(sem("y_lo_ready"), k - 1)
                    for c in range(CH):
                        u = 4 * (k - 2) + c
                        if not fixed_below(u, 2):
                            pe.wait_ge(sem("acc_done"), u - 1)
                        for n, (l, w) in enumerate(((y_hi, ow_hi), (y_hi, ow_lo), (y_lo, ow_hi))):
                            mm = pe.matmul(OUTP[c % 2][:, :], l[:, c_(c)], w[:, :], start=(n == 0), stop=(n == 2))
                        mm.then_inc(sem("out_ps"), 1)
                if has0:
                    if has2:
                        pe.wait_ge(sem("act_g"), k - 1)
                    project(KK, h, g, PJ[1])
                if has1:
                    pe.wait_ge(sem("ktok_ready"), m + 1)
                    pe.wait_ge(sem("vtok_ready"), m + 1)
                    if has2:
                        pe.wait_ge(sem("kv_ready"), m)
                    for c in range(CH):
                        mm = pe.matmul(KVP[:, c_(c)], ktok[:, c_(c)], vtok[:, c_(c)], start=True, stop=True)
                    mm.then_inc(sem("kv_ps"), 1)
                    pe.wait_ge(sem("act_q"), m + 1)
                    for c in range(CH):
                        mm = pe.matmul(TRV[:, c_(c)], kT[:, r1, c_(c)], qT[:, r1, c_(c)], start=True, stop=True)
                    mm.then_inc(sem("score_ps"), 1)
                if has0:
                    pe.wait_ge(sem("act_q"), k + 1)
                    project(VV, h, g, PJ[0])
                if has1:
                    if has0:
                        pe.wait_ge(sem("act_k"), k + 1)
                    project(GG, h1, g1, PJ[1])
                    pe.wait_ge(sem("masked"), m + 1)
                    pe.wait_ge(sem("qd_ready"), m + 1)
                    pe.wait_ge(sem("kv_ready"), m + 1)
                    if has2:
                        pe.wait_ge(sem("at_ready"), m)
                    for c in range(CH):
                        state = (c - 1) % CH if c or g1 % 2 else None
                        pe.matmul(ATP[:, c_(c)], vtok[:, c_(c)], sc[:, c_(c)], start=True, stop=state is None)
                        if state is not None:
                            mm = pe.matmul(ATP[:, c_(c)], kvs[:, state, :], qd[:, c_(c)], start=False, stop=True)
                    mm.then_inc(sem("at_ps"), 1)

            heads(pe, None, 0, slot)
            pe.wait_ge(sem("sq_done"), SLOTS)
            pe.wait_ge(sem("act_g"), SLOTS)
            for t in range(NT):
                mm = pe.matmul(bank[0][:, 2 * t:2 * t + 2], sq[:, t * P:(t + 1) * P], ones[:, 0:2],
                               start=True, stop=True)
            mm.then_inc(sem("ss_ps"), 1)

        def lin_act(act):
            stats_act(act, "lin")

            def tile(t, s, first, last):
                act.wait_ge(sem("xt"), past("lin", "xt") + t + 1)
                act.activation(xa_hi[:, :, bass.ds(t * P, P)],
                               bank[s][:, :].rearrange("p (k n) -> p k n", k=KC), ACT.Copy)\
                   .then_inc(sem("xhi"), 1)
            tiles(act, None, 0, tile)

            def whi(kind, n, h):
                if h is not None:
                    act.wait_ge(sem("out_ps" if kind == 4 else f"proj_{KINDS[kind]}"), (16 if kind == 4 else 4) * (h + 1))
                if kind == 4:
                    act.wait_ge(sem("ow_loaded"), 16 * (n + 1))
                    act.activation(ow_hi[:, :], ow_raw[:, :], ACT.Copy).then_inc(sem("w_hi_o"), 1)
                else:
                    act.wait_ge(sem("w_loaded"), 16 * (n + 1))
                    act.activation(w_hi[:, kind, :, :], w_raw[:, kind, :, :], ACT.Copy)\
                       .then_inc(sem(f"w_hi_{KINDS[kind]}"), 1)

            for kind in range(5):
                whi(kind, 0, None)

            def slot(k, h, g, h1, h2, has1, has2, has0):
                r, r1 = g % 2, (g + 1) % 2
                m = k - 1
                more = has0 and not (type(h) is int and h == LH)
                if has0:
                    act.wait_ge(sem("proj_q"), k + 1)
                    if has2:
                        act.wait_ge(sem("at_ps"), k - 1)
                        act.wait_ge(sem("qd_ready"), k - 1)
                    act.activation(qT[:, r, :], PJ[0][:, :], ACT.Silu).then_inc(sem("act_q"), 1)
                    if g == 3:
                        whi(QQ, h + 1, h)
                if has1:
                    act.wait_ge(sem("tr_v"), m + 1)
                    if has2:
                        act.wait_ge(sem("at_ps"), m)
                    act.activation(vtok[:, :], TRV[:, :], ACT.Copy).then_inc(sem("vtok_ready"), 1)
                if has0:
                    act.wait_ge(sem("proj_k"), k + 1)
                    act.activation(kT[:, r, :], PJ[1][:, :], ACT.Silu).then_inc(sem("act_k"), 1)
                    if g == 3:
                        whi(KK, h + 1, h)
                    act.wait_ge(sem("proj_v"), k + 1)
                    act.activation(vT[:, r, :], PJ[0][:, :], ACT.Silu).then_inc(sem("act_v"), 1)
                    if g == 3:
                        whi(VV, h + 1, h)
                if has1:
                    act.wait_ge(sem("proj_g"), m + 1)
                    if has2:
                        act.wait_ge(sem("y1_ready"), m)
                    act.activation(gate[:, :], PJ[1][:, :], ACT.Tanh, scale=0.5).then_inc(sem("act_g"), 1)
                    if g == 0 and has0:
                        whi(GG, h, h - 1)
                    act.wait_ge(sem("at_ps"), m + 1)
                    if has2:
                        act.wait_ge(sem("sq_done"), m)
                    act.activation(at[:, :], ATP[:, :], ACT.Copy).then_inc(sem("at_ready"), 1)
                    if has2:
                        act.wait_ge(sem("out_ps"), 4 * m)
                        if g == 1 and has0:
                            whi(4, h, h - 1)
                    act.wait_ge(sem("y1_ready"), m + 1)
                    act.activation(y_hi[:, :], y1[:, :], ACT.Copy, scale=nwh[:, bass.ds(h1, 1)])\
                       .then_inc(sem("y_hi_ready"), 1)

            heads(act, None, 0, slot)
            act.wait_ge(sem("ss_ve"), 1)
            act.activation(rnorm[:, :], rnorm[:, :], ACT.Sqrt).then_inc(sem("ss_sd"), 1)

        def lin_dve(dve, chain):
            stats_dve(dve, chain, "lin")

            def tile(t, s, first, last):
                norm_dve(dve, "lin", t, s, first, l_xn)
                dve.wait_ge(sem("xhi"), past("lin", "xhi") + t + 1)
                sl = xa_lo[:, :, bass.ds(t * P, P)]
                dve.tensor_tensor(sl, bank[s][:, :].rearrange("p (k n) -> p k n", k=KC),
                                  xa_hi[:, :, bass.ds(t * P, P)].bitcast(F32), ALU.subtract)\
                   .then_inc(sem("xlo"), 1)
            tiles(dve, None, 0, tile)
            dve.wait_ge(sem("x_kept"), 16)
            chain(dve.memset(x[:, :, :], 0.0))
            dve.wait_ge(sem("lin_consts"), 48)
            chain(dve.tensor_scalar(nwh[:, :], nwh[:, :], 0.5, None, ALU.mult))
            dve.sem_inc(sem("nwh_ready"), 1)

            def slot(k, h, g, h1, h2, has1, has2, has0):
                r1 = (g + 1) % 2
                m, g1 = k - 1, (g - 1) % G
                if has1:
                    dve.wait_ge(sem("tr_k"), m + 1)
                    if has2:
                        dve.wait_ge(sem("kv_ps"), m)
                        dve.wait_ge(sem("at_ps"), m)
                    dve.tensor_scalar(ktok[:, :], TRK[:, :], kdec[:, bass.ds(h1, 1)], None, ALU.mult)\
                       .then_inc(sem("ktok_ready"), 1)
                    dve.wait_ge(sem("tab_loaded"), 16 * (h1 + 1))
                    dve.wait_ge(sem("act_q"), m + 1)
                    dve.tensor_tensor(qd[:, :].rearrange("p (c n) -> p c n", c=CH),
                                      qT[:, r1, :].rearrange("p (c n) -> p c n", c=CH),
                                      dt_tab[:, 1, :].unsqueeze(1).to_broadcast([P, CH, P]), ALU.mult)\
                       .then_inc(sem("qd_ready"), 1)
                if has2:
                    for c in range(CH):
                        u = 4 * (k - 2) + c
                        tt = ((g - 2) % G) * CH + c
                        dve.wait_ge(sem("out_ps"), u + 1)
                        dve.tensor_tensor(x[:, tt, :], OUTP[c % 2][:, :], x[:, tt, :], ALU.add)\
                           .then_inc(sem("acc_done"), 1)
                if has1:
                    dve.wait_ge(sem("kv_ps"), m + 1)
                    for c in range(CH):
                        if g1 % 2 == 0 and c == 0:
                            chain(dve.tensor_copy(kvs[:, 0, :], KVP[:, c_(0)]))
                        else:
                            chain(dve.scalar_tensor_tensor(kvs[:, c, :], kvs[:, (c - 1) % CH, :],
                                                           bdec[:, bass.ds(h1, 1)], KVP[:, c_(c)],
                                                           ALU.mult, ALU.add)) \
                                if not (g1 % 2 and c == CH - 1) else None
                    dve.sem_inc(sem("kv_ready"), 1)
                    dve.wait_ge(sem("score_ps"), m + 1)
                    dve.tensor_tensor(sc[:, :].rearrange("p (c n) -> p c n", c=CH),
                                      TRV[:, :].rearrange("p (c n) -> p c n", c=CH),
                                      dt_tab[:, 0, :].unsqueeze(1).to_broadcast([P, CH, P]), ALU.mult)\
                       .then_inc(sem("masked"), 1)
                    dve.wait_ge(sem("act_g"), m + 1)
                    dve.wait_ge(sem("at_ready"), m + 1)
                    if has2:
                        dve.wait_ge(sem("y_hi_ready"), m)
                    dve.scalar_tensor_tensor(y1[:, :], gate[:, :], 1.0, at[:, :], ALU.add, ALU.mult)\
                       .then_inc(sem("y1_ready"), 1)
                    dve.wait_ge(sem("y_hi_ready"), m + 1)
                    dve.scalar_tensor_tensor(y_lo[:, :], y1[:, :], nwh[:, bass.ds(h1, 1)],
                                             y_hi[:, :].bitcast(F32), ALU.mult, ALU.subtract)\
                       .then_inc(sem("y_lo_ready"), 1)

            heads(dve, chain, 14, slot)
            dve.wait_ge(sem("acc_done"), 4 * SLOTS)
            dve.wait_ge(sem("ss_ps"), 1)
            dve.tensor_scalar(rnorm[:, :], bank[0][:, 0:2 * NT].rearrange("p (t c) -> p t c", c=2)[:, :, 0],
                              1.0 / (LH * P), EPS, ALU.mult, ALU.add).then_inc(sem("ss_ve"), 1)
            dve.wait_ge(sem("ss_sd"), 1)
            chain(dve.reciprocal(rnorm[:, :], rnorm[:, :]))

            def tile(t, s, first, last):
                dve.wait_ge(sem(f"x_back{s}"), 8 * (t - s) + 16)
                dve.scalar_tensor_tensor(x[:, t, :], x[:, t, :], rnorm[:, bass.ds(t, 1)], x_in[:, s, :],
                                         ALU.mult, ALU.add).then_inc(sem("lin_x"), 1)
            tiles(dve, None, 0, tile)
            dve.wait_ge(sem("lin_x"), NT)
            dve.sem_inc(phase_done["lin"], 1)

        def lin_pool(pool, chain):
            def wlo(kind, n):
                pool.wait_ge(sem(f"w_hi_{KINDS[kind]}"), n + 1)
                if kind == 4:
                    pool.tensor_tensor(ow_lo[:, :], ow_raw[:, :], ow_hi[:, :].bitcast(F32), ALU.subtract)\
                        .then_inc(sem("w_lo_o"), 1)
                else:
                    pool.tensor_tensor(w_lo[:, kind, :, :], w_raw[:, kind, :, :],
                                       w_hi[:, kind, :, :].bitcast(F32), ALU.subtract)\
                        .then_inc(sem(f"w_lo_{KINDS[kind]}"), 1)
            chain(pool.memset(sq[:, :], 0.0))
            for kind in range(5):
                wlo(kind, 0)

            def slot(k, h, g, h1, h2, has1, has2, has0):
                m, g1 = k - 1, (g - 1) % G
                if has0 and g == 3:
                    for kind in (QQ, KK, VV):
                        wlo(kind, h + 1)
                if has1:
                    if g == 0 and has0:
                        wlo(GG, h)
                    if g == 1 and has0 and has2:
                        wlo(4, h)
                    pool.wait_ge(sem("at_ready"), m + 1)
                    chain(pool.tensor_tensor(at2[:, :], at[:, :], at[:, :], ALU.mult))
                    part = sq[:, g1 * GT:(g1 + 1) * GT]
                    chain(pool.tensor_tensor(part, part, at2[:, :], ALU.add))
                    pool.wait_ge(sem("y1_ready"), m + 1)
                    pool.sem_inc(sem("sq_done"), 1)

            heads(pool, chain, 8, slot)

        def lin_sync(sp):
            sp.dma_start(kdec[:, :], a["kdec"]).then_inc(sem("lin_consts"), 16)
            sp.dma_start(bdec[:, :], a["bdec"]).then_inc(sem("lin_consts"), 16)
            sp.dma_start(nwh[:, :], a["norm_w"]).then_inc(sem("lin_consts"), 16)
            sp.dma_start(w_raw[:, :, :, :], a["w_heads"][0]).then_inc(sem("w_loaded"), 16)
            sp.dma_start(ow_raw[:, :], a["ow_heads"][0]).then_inc(sem("ow_loaded"), 16)
            sp.dma_start(dt_tab[:, :, :], a["decay"][0]).then_inc(sem("tab_loaded"), 16)
            sp.dma_start(x_dram.rearrange("t p n -> p t n"), x[:, :, :]).then_inc(sem("x_kept"), 16)

            def head(n):
                sp.wait_ge(sem("w_lo_g"), n)
                sp.dma_start(w_raw[:, :, :, :], a["w_heads"][n]).then_inc(sem("w_loaded"), 16)
                sp.wait_ge(sem("w_lo_o"), n)
                sp.dma_start(ow_raw[:, :], a["ow_heads"][n]).then_inc(sem("ow_loaded"), 16)
                sp.wait_ge(sem("masked"), 4 * n)
                sp.wait_ge(sem("qd_ready"), 4 * n)
                sp.dma_start(dt_tab[:, :, :], a["decay"][n])\
                  .then_inc(sem("tab_loaded"), 16)
            with sp.Fori(1, LH) as n:
                head(n)
            sp.wait_ge(sem("w_lo_g"), LH)
            sp.dma_start(w_raw[:, :, :, :], a["w_heads"][0]).then_inc(sem("w_loaded"), 16)

            def tile(t, s, first, last):
                if not first:
                    sp.wait_ge(sem("lin_x"), t - 1)
                sp.dma_start(x_in[:, s, :], x_dram[t]).then_inc(sem(f"x_back{s}"), 16)
            tiles(sp, None, 0, tile)

        MEM_XT = [bank[0], bank[1]]
        MEM_A = [bank[2], bank[3]]
        MEM_P = [bank[4], bank[5]]
        MEM_Y = [bank[6], bank[7]]

        def mem_prep_sync(sp):
            for n, (dst, src) in enumerate((
                    (small[0:BOT, 0:RDIM], a["wr_t"]), (small[0:RDIM, 64:64 + BOT], a["wr"]),
                    (small2[0:BOT, P:2 * P], a["keys_t"]),
                    (qk[0:BOT, 0, 0:32, :].rearrange("p h d -> p (h d)"), a["wq_mem"]),
                    (qk[:, 1, 0:8, :].rearrange("p h d -> p (h d)"), a["wvd_t"]),
                    (qk[:, 2, 0:32, :].rearrange("p h d -> p (h d)"), a["values_t"]),
                    (qk[0:VB, 3, 0:32, :].rearrange("p h d -> p (h d)"), a["wvu_t"]),
                    (lrel[:, :], a["log_rel"]), (bu1[:, :], a["bu1"]), (wu2[:, :], a["wu2"]),
                    (sc3[:, 0:3], a["scalars"]))):
                sp.dma_start(dst, src).then_inc(sem("mem_loaded"), 16)
            load_pieces_sync(sp, "mem_a")

        def flat(ap):
            return ap.rearrange("p h d -> p (h d)")

        def mem_prep_pe(pe):
            pe.wait_ge(sem("mem_loaded"), 16 * 11)
            pe.matmul(bank[0][0:RDIM, 0:NSLOT], small[0:BOT, 0:RDIM], small2[0:BOT, P:2 * P], start=True, stop=True)\
              .then_inc(sem("mp_rk"), 1)
            wvd, val = flat(qk[:, 1, 0:8, :]), flat(qk[:, 2, 0:32, :])
            for k in range(KC):
                mm = pe.matmul(bank[1][0:VB, 0:NSLOT], wvd[:, k * VB:(k + 1) * VB], val[:, k * P:(k + 1) * P],
                               start=(k == 0), stop=(k == KC - 1))
            mm.then_inc(sem("mp_v2"), 1)
            pe.wait_ge(sem("mp_rk_sb"), 1)
            pe.matmul(bank[2][0:BOT, 0:NSLOT], small[0:RDIM, 64:64 + BOT], small[0:RDIM, P:2 * P], start=True, stop=True)\
              .then_inc(sem("mp_m"), 1)
            pe.wait_ge(sem("mp_v2_sb"), 1)
            pe.matmul(bank[3][:, :], v2t[0:VB, :], flat(qk[0:VB, 3, 0:32, :]), start=True, stop=True)\
              .then_inc(sem("mp_v3"), 1)
            pe.wait_ge(sem("mp_m_sb"), 1)
            for k in range(KC):
                pe.matmul(bank[4 + k][:, 0:2 * NSLOT], flat(qk[0:BOT, 0, 0:32, :])[:, k * P:(k + 1) * P],
                          small2[0:BOT, 0:2 * P], start=True, stop=True).then_inc(sem("mp_w"), 1)

        def mem_prep_act(act):
            split_pieces_act(act, "mem_a")
            act.wait_ge(sem("mp_v2"), 1)
            act.activation(v2t[0:VB, :], bank[1][0:VB, 0:NSLOT], ACT.Copy).then_inc(sem("mp_v2_sb"), 1)
            act.wait_ge(sem("mp_v3"), 1)
            act.activation(v3[:, :], bank[3][:, :], ACT.Copy).then_inc(sem("mp_v3_sb"), 1)
            for k in range(KC):
                act.wait_ge(sem("mp_w"), k + 1)
                act.activation(w1_hi[:, k, 0:P], bank[4 + k][:, 0:P], ACT.Copy, scale=float(1 / np.sqrt(RDIM)))
                act.activation(w1_hi[:, k, P:2 * P], bank[4 + k][:, P:2 * P], ACT.Copy, scale=float(1 / np.sqrt(BOT)))\
                   .then_inc(sem("mp_w_hi"), 1)

        def mem_prep_dve(dve, chain):
            split_pieces_dve(dve, "mem_a")
            dve.wait_ge(sem("mp_rk"), 1)
            dve.tensor_copy(small[0:RDIM, P:2 * P], bank[0][0:RDIM, 0:NSLOT]).then_inc(sem("mp_rk_sb"), 1)
            dve.wait_ge(sem("mp_m"), 1)
            dve.tensor_copy(small2[0:BOT, 0:P], bank[2][0:BOT, 0:NSLOT]).then_inc(sem("mp_m_sb"), 1)
            for k in range(KC):
                dve.wait_ge(sem("mp_w_hi"), k + 1)
                dve.scalar_tensor_tensor(w1_lo[:, k, 0:P], bank[4 + k][:, 0:P], float(1 / np.sqrt(RDIM)),
                                         w1_hi[:, k, 0:P].bitcast(F32), ALU.mult, ALU.subtract)
                dve.scalar_tensor_tensor(w1_lo[:, k, P:2 * P], bank[4 + k][:, P:2 * P], float(1 / np.sqrt(BOT)),
                                         w1_hi[:, k, P:2 * P].bitcast(F32), ALU.mult, ALU.subtract)\
                   .then_inc(sem("mp_w_lo"), 1)
            dve.wait_ge(sem("mp_w_lo"), KC)
            dve.wait_ge(sem("piece_lo"), past("mem_a", "piece_lo") + KC)
            dve.wait_ge(sem("mp_v3_sb"), 1)
            dve.wait_ge(sem("mem_loaded"), 16 * 11)
            chain(dve.tensor_scalar(wu2[:, :], wu2[:, :], 0.5, None, ALU.mult))
            dve.sem_inc(sem("mem_ready"), 1)

        def mem_pe(pe, phase):
            pe.wait_ge(sem("ls"), past(phase, "ls") + 1)
            pe.matmul(MEM_Y[0][:, 0:2], ones[:, :], lsum[:, 0:2], start=True, stop=True).then_inc(sem("lm"), 1)
            transpose_pe(pe, phase, 0, 0, True, MEM_XT[0])
            pe.wait_ge(sem("nv"), past(phase, "nv") + 1)

            def tile(t, s, first, last):
                if not last:
                    transpose_pe(pe, phase, t + 1, 1 - s, first and s == 0, MEM_XT[1 - s])
                pe.wait_ge(sem("xlo"), past(phase, "xlo") + t + 1)
                if not first:
                    pe.wait_ge(sem("read"), past(phase, "read") + t - 1)
                product_pe(pe, MEM_A[s][:, 0:384], s, w1_hi, w1_lo, 0, 384).then_inc(sem("used"), 1)
                pe.wait_ge(sem("pr"), past(phase, "pr") + t + 1)
                if not first:
                    pe.wait_ge(sem("prt"), past(phase, "prt") + t - 1)
                pe.transpose(MEM_P[s][:, 0:P], pr[:, s, :], ident[:, :]).then_inc(sem("pt"), 1)
                pe.wait_ge(sem("prt"), past(phase, "prt") + t + 1)
                if not first:
                    pe.wait_ge(sem("x"), past(phase, "x") + t - 1)
                pe.matmul(MEM_Y[s][:, :], prt[:, s, :], v3[:, :], start=True, stop=True).then_inc(sem("y"), 1)

            tiles(pe, None, 0, tile)

        def mem_act(act, phase):
            act.wait_ge(sem("vh"), past(phase, "vh") + 1)
            act.activation(lv[:, :], lv[:, :], ACT.Ln, bias=1.0, accum_out=lsum[:, 0:1]).then_inc(sem("lv"), 1)
            hi_act(act, phase, 0, 0, True, MEM_XT[0])

            def tile(t, s, first, last):
                if not last:
                    hi_act(act, phase, t + 1, 1 - s, first and s == 0, MEM_XT[1 - s])
                act.wait_ge(sem("cubic"), past(phase, "cubic") + t + 1)
                act.activation(gt[:, s, :], gc[:, s, :], ACT.Tanh, scale=GELU_SCALE).then_inc(sem("gt"), 1)
                act.wait_ge(sem("am"), past(phase, "am") + t + 1)
                if not first:
                    act.wait_ge(sem("pt"), past(phase, "pt") + t - 1)
                act.activation(pr[:, s, :], am[:, s, :], ACT.Exp, bias=c1[:, s, 0:1], accum_out=c1[:, s, 1:2])\
                   .then_inc(sem("pr"), 1)
                act.wait_ge(sem("learned"), past(phase, "learned") + t + 1)
                act.activation(c1[:, s, 3:4], c1[:, s, 2:3], ACT.Tanh, scale=0.5).then_inc(sem("t1"), 1)
                act.wait_ge(sem("pt"), past(phase, "pt") + t + 1)
                if not first:
                    act.wait_ge(sem("y"), past(phase, "y") + t - 1)
                act.activation(prt[:, s, :], MEM_P[s][:, 0:P], ACT.Copy).then_inc(sem("prt"), 1)
                act.wait_ge(sem("u"), past(phase, "u") + t + 1)
                act.activation(c1[:, s, 5:6], c1[:, s, 4:5], ACT.Tanh, scale=0.5).then_inc(sem("t2"), 1)

            tiles(act, None, 0, tile)

        def mem_pool(pool, chain, phase):
            def tile(t, s, first, last):
                pool.wait_ge(sem("read"), past(phase, "read") + t + 1)
                if not first:
                    pool.wait_ge(sem("gt"), past(phase, "gt") + t - 1)
                chain(pool.tensor_tensor(gc[:, s, :], gu[:, s, :], gu[:, s, :], ALU.mult))
                apart(pool, sem("apart_pool"))
                chain(pool.tensor_scalar(gc[:, s, :], gc[:, s, :], 0.044715, 1.0, ALU.mult, ALU.add))
                pool.tensor_tensor(gc[:, s, :], gc[:, s, :], gu[:, s, :], ALU.mult).then_inc(sem("cubic"), 1)

            tiles(pool, chain, 2, tile)

        def mem_dve(dve, chain, phase):
            chain(dve.tensor_tensor(lv[:, :], rstd[:, :], rstd[:, :], ALU.mult))
            dve.scalar_tensor_tensor(lv[:, :], ve[:, :], -EPS, lv[:, :], ALU.add, ALU.mult).then_inc(sem("vh"), 1)
            chain(dve.memset(lsum[:, 1:2], 0.0))
            dve.wait_ge(sem("lv"), past(phase, "lv") + 1)
            dve.sem_inc(sem("ls"), 1)
            dve.wait_ge(sem("lm"), past(phase, "lm") + 1)
            chain(dve.tensor_scalar(mean1[:, 0:1], MEM_Y[0][:, 0:1], 1.0 / T, 1e-6, ALU.mult, ALU.add))
            chain(dve.reciprocal(mean1[:, 1:2], mean1[:, 0:1]))
            dve.tensor_scalar(nv[:, :], lv[:, :], mean1[:, 1:2], 0.5, ALU.mult, ALU.mult).then_inc(sem("nv"), 1)
            norm_dve(dve, phase, 0, 0, True)
            lo_dve(dve, phase, 0, 0, MEM_XT[0])

            def tile(t, s, first, last):
                if not last:
                    norm_dve(dve, phase, t + 1, 1 - s, first and s == 0)
                    lo_dve(dve, phase, t + 1, 1 - s, MEM_XT[1 - s])
                A_ = MEM_A[s]
                dve.wait_ge(sem("used"), past(phase, "used") + t + 1)
                chain(dve.tensor_tensor(gu[:, s, :], A_[:, 256:384], bu1[:, :], ALU.add))
                chain(dve.tensor_tensor(rt[:, s, :], A_[:, 0:P], lrel[:, :], ALU.add))
                if not first:
                    dve.wait_ge(sem("pr"), past(phase, "pr") + t - 1)
                dve.tensor_tensor(am[:, s, :], A_[:, P:2 * P], lrel[:, :], ALU.add).then_inc(sem("read"), 1)
                apart(dve, sem("apart_dve"))
                chain(dve.max(top[:, s, :], rt[:, s, :]))
                apart(dve, sem("apart_dve"))
                chain(dve.match_replace(out=rt2[:, s, :], in_to_replace=top[:, s, :], in_values=rt[:, s, :],
                                        imm_value=TAKEN))
                chain(dve.tensor_scalar(rt[:, s, :], rt2[:, s, :], TAKEN_LINE, LOW, ALU.is_gt, ALU.mult))
                chain(dve.tensor_tensor(am[:, s, :], am[:, s, :], rt[:, s, :], ALU.add))
                chain(dve.tensor_reduce(c1[:, s, 6:7], am[:, s, :], AX, ALU.max))
                dve.tensor_scalar(c1[:, s, 0:1], c1[:, s, 6:7], -1.0, None, ALU.mult).then_inc(sem("am"), 1)
                dve.wait_ge(sem("gt"), past(phase, "gt") + t + 1)
                chain(dve.scalar_tensor_tensor(gg[:, s, :], gt[:, s, :], 1.0, gu[:, s, :], ALU.add, ALU.mult))
                chain(dve.tensor_tensor(gg[:, s, :], gg[:, s, :], wu2[:, :], ALU.mult))
                chain(dve.tensor_reduce(c1[:, s, 7:8], gg[:, s, :], AX, ALU.add))
                dve.tensor_scalar(c1[:, s, 2:3], c1[:, s, 7:8], sc3[:, 0:1], None, ALU.add)\
                   .then_inc(sem("learned"), 1)
                chain(dve.tensor_scalar(mk[:, s, 0:1], rstd[:, bass.ds(t, 1)], 0.5, 1.0, ALU.mult, ALU.add))
                chain(dve.tensor_scalar(mk[:, s, 1:2], nmr[:, bass.ds(t, 1)], 0.5, None, ALU.mult))
                chain(dve.tensor_scalar(xb[:, s, :], x[:, t, :], mk[:, s, 0:1], mk[:, s, 1:2], ALU.mult, ALU.add))
                dve.wait_ge(sem("t1"), past(phase, "t1") + t + 1)
                chain(dve.tensor_scalar(c1[:, s, 3:4], c1[:, s, 3:4], 1.25, 1.25, ALU.mult, ALU.add))
                chain(dve.tensor_scalar(c1[:, s, 3:4], c1[:, s, 3:4], nv[:, bass.ds(t, 1)], 0.0, ALU.add, ALU.max))
                chain(dve.tensor_scalar(c1[:, s, 3:4], c1[:, s, 3:4], 5.0, -0.5, ALU.min, ALU.add))
                chain(dve.tensor_scalar(c1[:, s, 3:4], c1[:, s, 3:4], 1.0 / 1.5, 0.0, ALU.mult, ALU.max))
                chain(dve.tensor_scalar(c1[:, s, 3:4], c1[:, s, 3:4], 1.0, None, ALU.min))
                dve.tensor_scalar(c1[:, s, 4:5], c1[:, s, 3:4], sc3[:, 1:2], sc3[:, 2:3], ALU.mult, ALU.add)\
                   .then_inc(sem("u"), 1)
                dve.wait_ge(sem("t2"), past(phase, "t2") + t + 1)
                chain(dve.tensor_scalar(c1[:, s, 5:6], c1[:, s, 5:6], 0.5, 0.5, ALU.mult, ALU.add))
                chain(dve.tensor_scalar(c1[:, s, 6:7], c1[:, s, 5:6], 0.05, None, ALU.is_ge))
                dve.wait_ge(sem("pr"), past(phase, "pr") + t + 1)
                chain(dve.reciprocal(c1[:, s, 7:8], c1[:, s, 1:2]))
                chain(dve.scalar_tensor_tensor(c1[:, s, 5:6], c1[:, s, 5:6], 0.5, c1[:, s, 6:7], ALU.mult, ALU.mult))
                chain(dve.tensor_tensor(c1[:, s, 5:6], c1[:, s, 5:6], c1[:, s, 7:8], ALU.mult))
                dve.wait_ge(sem("y"), past(phase, "y") + t + 1)
                dve.scalar_tensor_tensor(x[:, t, :], MEM_Y[s][:, :], c1[:, s, 5:6], xb[:, s, :], ALU.mult, ALU.add)\
                   .then_inc(sem("x"), 1)

            tiles(dve, chain, 23, tile)
            dve.wait_ge(sem("x"), past(phase, "x") + NT)
            dve.sem_inc(phase_done[phase], 1)

        PRJ_XT = [bank[0], bank[1]]
        PRJ_Q = [bank[2], bank[3]]
        PRJ_KV = [bank[4], bank[5]]

        def qkv_pe(pe):
            phase = "att"
            transpose_pe(pe, phase, 0, 0, True, PRJ_XT[0])
            pe.wait_ge(sem("piece_lo"), past("att", "piece_lo") + 2 * KC)

            def tile(t, s, first, last):
                if not last:
                    transpose_pe(pe, phase, t + 1, 1 - s, first and s == 0, PRJ_XT[1 - s])
                pe.wait_ge(sem("xlo"), past("att", "xlo") + t + 1)
                if not first:
                    pe.wait_ge(sem("att_biased"), t - 1)
                product_pe(pe, PRJ_Q[s][:, :], s, wq_hi, wq_lo, 0, 512)
                product_pe(pe, PRJ_KV[s][:, 0:256], s, wq_hi, wq_lo, 512, 768).then_inc(sem("used"), 1)
            tiles(pe, None, 0, tile)

        def qkv_act(act):
            hi_act(act, "att", 0, 0, True, PRJ_XT[0])

            def tile(t, s, first, last):
                if not last:
                    hi_act(act, "att", t + 1, 1 - s, first and s == 0, PRJ_XT[1 - s])
            tiles(act, None, 0, tile)

        def qkv_pool(pool):
            def tile(t, s, first, last, pos):
                pool.wait_ge(sem("att_biased"), t + 1)
                if not first:
                    pool.wait_ge(sem("att_qk"), t - 1)
                sin = rope[:, pos, 1, :]
                for half in (0, 1):
                    lo_, hi_ = half * (HD // 2), (1 - half) * (HD // 2)
                    ins = pool.tensor_tensor(rot[:, s, :, lo_:lo_ + HD // 2], qkb[:, s, :, hi_:hi_ + HD // 2],
                                             sin[:, lo_:lo_ + HD // 2].unsqueeze(1).to_broadcast([P, QK, HD // 2]),
                                             ALU.mult)
                ins.then_inc(sem("att_rot"), 1)
            by_sequence(pool, tile)

        def by_sequence(eng, tile):
            for b in range(B):
                for s in (0, 1):
                    tile(b * TB + s, s, b == 0, False, s)
                with eng.Fori(1, TB // 2) as j:
                    for s in (0, 1):
                        tile(b * TB + 2 * j + s, s, False, False, 2 * j + s)

        def qkv_dve(dve, chain):
            dve.wait_ge(sem("att_loaded"), 32)
            norm_dve(dve, "att", 0, 0, True)
            lo_dve(dve, "att", 0, 0, PRJ_XT[0])

            def tile(t, s, first, last, pos):
                if not last:
                    norm_dve(dve, "att", t + 1, 1 - s, first and s == 0)
                    lo_dve(dve, "att", t + 1, 1 - s, PRJ_XT[1 - s])
                dve.wait_ge(sem("used"), past("att", "used") + t + 1)
                if not first:
                    dve.wait_ge(sem("att_rot"), t - 1)
                    dve.wait_ge(sem("att_qk"), t - 1)
                dve.tensor_tensor(vv[:, t, :, :], PRJ_KV[s][:, P:2 * P].rearrange("p (h d) -> p h d", d=HD),
                                  bqkv[:, 640:768].rearrange("p (h d) -> p h d", d=HD), ALU.add)
                dve.tensor_tensor(qkb[:, s, 0:H, :], PRJ_Q[s][:, :].rearrange("p (h d) -> p h d", d=HD),
                                  bqkv[:, 0:512].rearrange("p (h d) -> p h d", d=HD), ALU.add)
                dve.tensor_tensor(qkb[:, s, H:QK, :], PRJ_KV[s][:, 0:P].rearrange("p (h d) -> p h d", d=HD),
                                  bqkv[:, 512:640].rearrange("p (h d) -> p h d", d=HD), ALU.add)\
                   .then_inc(sem("att_biased"), 1)
                dve.wait_ge(sem("att_biased"), t + 1)
                dve.tensor_tensor(qk[:, t, :, :], qkb[:, s, :, :],
                                  rope[:, pos, 0, :].unsqueeze(1).to_broadcast([P, QK, HD]), ALU.mult)\
                   .then_inc(sem("att_cos"), 1)
                dve.wait_ge(sem("att_cos"), t + 1)
                dve.wait_ge(sem("att_rot"), t + 1)
                dve.tensor_tensor(qk[:, t, :, :], qk[:, t, :, :], rot[:, s, :, :], ALU.add).then_inc(sem("att_qk"), 1)

            for b in range(B):
                for s in (0, 1):
                    tile(b * TB + s, s, b == 0, False, s)
                with dve.Fori(1, TB // 2 - 1) as j:
                    for s in (0, 1):
                        tile(b * TB + 2 * j + s, s, False, False, 2 * j + s)
                for s in (0, 1):
                    tile(b * TB + TB - 2 + s, s, False, b == B - 1 and s == 1, TB - 2 + s)
            dve.wait_ge(sem("att_qk"), NT)
            dve.memset(kst[KS:KS + 2, :, :], 1.0).then_inc(sem("att_preset"), 1)
            dve.memset(vst[:, :, :, :], 0.0).then_inc(sem("att_preset"), 1)
            dve.wait_ge(sem("att_preset"), 2)
            dve.memset(vst[:, :, :, HD:HD + 1], 1.0).then_inc(sem("att_preset"), 1)
            dve.wait_ge(sem("att_preset"), 3)
            dve.sem_inc(sem("att_qkv"), 1)

        SP_ = [bank[0], bank[1]]
        ST_ = [bank[2], bank[3], bank[4], bank[5]]
        PV_ = bank[6]
        TR_ = bank[7]
        TRB = TR_[:, :].bitcast(BF16)
        AHF = 2
        STEPS = AHF * TB
        T_AT = {0: ["k", 0], 3: [1], 6: [2], 9: [3]}
        S_AT = {1: (0, 0, 5), 2: (0, 5, 10), 3: (0, 10, 16), 4: (1, 0, 5), 5: (1, 5, 10), 6: (1, 10, 16),
                7: (2, 0, 5), 8: (2, 5, 10), 9: (2, 10, 16), 10: (3, 0, 5), 11: (3, 5, 10), 12: (3, 10, 16)}
        NM_AT = 14
        OUT_AT = {3: 1, TB + 3: 0}

        def slots(eng, chain, steps, slot, ahead):
            ahead(0, 0, 0, True)
            slot(0, 0, 0, 0, True, True)
            slot(1, 0, 1, 1, True, False)

            def body(kv):
                slot(2 * kv, kv, 0, kv, True, False)
                slot(2 * kv + 1, kv, 1, kv + 1, True, False)
            looped([chain] if chain else [], eng, 1, KV - 1, steps, body)
            slot(2 * KV - 2, KV - 1, 0, KV - 1, True, False)
            slot(2 * KV - 1, KV - 1, 1, KV, False, False)

        T_N, S_N, X_N = 5, 64, 64
        def att_pe(pe):
            pe.wait_ge(sem("att_qkv"), 1)

            def stack(n, p, which, started=True):
                if which == "k":
                    if started:
                        pe.wait_ge(sem("nmt_ready"), n)
                elif which == 2 and not fixed_below(n, 2):
                    pe.wait_ge(sem("out_read"), 2 * n - 2)
                else:
                    pe.wait_ge(sem("stack_sb"), T_N * n + which + 1)
                pe.wait_ge(sem("stacked"), 2 * n + 1 if which == "k" else 2 * n + 2)
                for t in range(TB):
                    src = ks[:, t, :] if which == "k" else qs[:, t, which, :]
                    mm = pe.transpose(TRB[0:KS, t * P:(t + 1) * P], src, identb[:, :])
                mm.then_inc(sem("stack_ps"), 1)

            def score(n, p, j, lo, hi):
                for i in range(lo, hi):
                    u = S_N * n + 16 * j + i
                    if i == lo:
                        pe.wait_ge(sem("stack_sb"), T_N * n + 2 + j)
                    if not fixed_below(u, 2):
                        pe.wait_ge(sem("max_read"), u - 1)
                    t, hf = i // 2, i % 2
                    pe.matmul(SP_[i % 2][:, :], qst[0:KS, p, j, t * P:(t + 1) * P], kst[0:KS, p, hf * 512:(hf + 1) * 512],
                              start=True, stop=True).then_inc(sem("score2"), 1)

            def maxima(n, started=True):
                pe.wait_ge(sem("nm_ready"), n + 1)
                if started:
                    pe.wait_ge(sem("out_read"), 2 * n - 1)
                else:
                    pe.wait_ge(sem("stack_sb"), T_N)
                apart(pe, sem("apart_pe"))
                pe.transpose(TRB[0:2 * REP * TB, 0:P], nm[:, :, :].rearrange("p a c -> p (a c)"), identb[:, :])\
                  .then_inc(sem("nm_ps"), 1)

            def ahead(n, kv, p, whole):
                stack(n, p, "k", False)
                for j in range(REP):
                    stack(n, p, j)
                    score(n, p, j, 0, 16)
                maxima(n, False)

            def turn_out(half):
                pe.wait_ge(sem("pv_sb"), half + 1)
                for i in range(4):
                    mm = pe.transpose(TR_[:, i * P:(i + 1) * P], pvs[:, i * P:(i + 1) * P], ident[:, :])
                mm.then_inc(sem("out_turned"), 1)

            def values(n, p, st):
                hf, kt = st // TB, st % TB
                if st == 0 and kt == 0:
                    pe.wait_ge(sem("v_ready"), n + 1)
                for j in range(REP):
                    u = X_N * n + 4 * st + j
                    pe.wait_ge(sem("probs"), u + 1)
                    if kt == 0 and j == 0 and not fixed_below(2 * n + hf, 1):
                        pe.wait_ge(sem("pv_sb"), 2 * n + hf)
                    mm = pe.matmul(PV_[32 * j:32 * j + 32, :], vst[:, p, kt, :], pp[:, (4 * st + j) % 8, :],
                                   start=(kt == 0), stop=(kt == TB - 1), tile_position=(0, 32 * j))
                mm.then_inc(sem("pv_step"), 1)

            def slot(n, kv, b, nkv, has_next, first):
                pe.wait_ge(sem("rows_in"), 32 * (n + 1))
                for st in range(STEPS):
                    hf, kt = st // TB, st % TB
                    for j in range(REP):
                        u = X_N * n + 4 * st + j
                        if not fixed_below(u, 4):
                            pe.wait_ge(sem("probs"), u - 3)
                        pe.matmul(ST_[j][:, :], kst[0:KS + 2, b, kt * P:(kt + 1) * P],
                                  qst[0:KS + 2, b, j, hf * 512:(hf + 1) * 512], start=True, stop=True)\
                          .then_inc(sem("score1"), 1)
                    if has_next:
                        for w in T_AT.get(st, []):
                            stack(n + 1, 1 - b, w)
                        if st in S_AT:
                            score(n + 1, 1 - b, *S_AT[st])
                    if st:
                        values(n, b, st - 1)
                    if st in OUT_AT and not (first and OUT_AT[st] == 1):
                        if has_next:
                            pe.wait_ge(sem("stack_sb"), T_N * (n + 1) + (3 if OUT_AT[st] == 1 else 5))
                        elif OUT_AT[st] == 1:
                            pe.wait_ge(sem("nmt_ready"), n + 1)
                        else:
                            pe.wait_ge(sem("out_read"), 2 * n)
                        turn_out(2 * n - 1 if OUT_AT[st] == 1 else 2 * n)
                    if has_next and st == NM_AT:
                        maxima(n + 1)
                values(n, b, STEPS - 1)

            slots(pe, None, 0, slot, ahead)
            pe.wait_ge(sem("out_read"), 4 * KV - 1)
            turn_out(4 * KV - 1)

        def att_act(act):
            act.wait_ge(sem("att_qkv"), 1)

            def stack(n, p, which, lag):
                i = 0 if which == "k" else which + 1
                act.wait_ge(sem("stack_ps"), T_N * n + i + 1)
                if which == "k":
                    if not fixed_below(n, 2):
                        act.wait_ge(sem("pv_step"), STEPS * (n - 1))
                    dst = kst[0:KS, p, :]
                else:
                    dst = qst[0:KS, p, which, :]
                act.activation(dst, TRB[0:KS, :], ACT.Copy).then_inc(sem("stack_sb"), 1)

            def maxima(n):
                act.wait_ge(sem("nm_ps"), n + 1)
                if not fixed_below(n, 1):
                    act.wait_ge(sem("rows_in"), 32 * n)
                act.activation(nmt[:, :], TRB[0:2 * REP * TB, 0:P], ACT.Copy).then_inc(sem("nmt_ready"), 1)

            def ahead(n, kv, p, whole):
                stack(n, p, "k", 0)
                for j in range(REP):
                    stack(n, p, j, 0)
                maxima(n)

            def half_out(n):
                act.wait_ge(sem("pv_step"), TB * (n + 1))
                if not fixed_below(n, 1):
                    act.wait_ge(sem("out_turned"), n)
                act.activation(pvs[:, :], PV_[:, :], ACT.Copy).then_inc(sem("pv_sb"), 1)

            def slot(n, kv, b, nkv, has_next, first):
                for st in range(STEPS):
                    for j in range(REP):
                        u = X_N * n + 4 * st + j
                        act.wait_ge(sem("score1"), u + 1)
                        if not fixed_below(STEPS * n + st, 2):
                            if j == 0:
                                act.wait_ge(sem("pv_step"), STEPS * n + st - 1)
                        act.activation(pp[:, (4 * st + j) % 8, :], ST_[j][:, :], ACT.Exp, scale=0.25)\
                           .then_inc(sem("probs"), 1)
                    if has_next:
                        for w in T_AT.get(st, []):
                            stack(n + 1, 1 - b, w, 0)
                    if st == TB:
                        half_out(2 * n)
                    if st == 0 and not first:
                        half_out(2 * n - 1)
                    if has_next and st == NM_AT:
                        maxima(n + 1)

            slots(act, None, 0, slot, ahead)
            half_out(4 * KV - 1)

        def att_dve(dve, chain):
            def score(n, j, lo, hi):
                for i in range(lo, hi):
                    u = S_N * n + 16 * j + i
                    dve.wait_ge(sem("score2"), u + 1)
                    dve.tensor_reduce(mx[:, j, i // 2, i % 2:i % 2 + 1], SP_[i % 2][:, :], AX, ALU.max)\
                       .then_inc(sem("max_read"), 1)

            def maxima(n):
                dve.wait_ge(sem("max_read"), S_N * (n + 1))
                if not fixed_below(n, 1):
                    dve.wait_ge(sem("nm_ps"), n)
                chain(dve.tensor_reduce(m1[:, :, :], mx[:, :, :, :], AX, ALU.max))
                flat_m = m1[:, :, :].rearrange("p a c -> p (a c)")
                chain(dve.tensor_scalar(nm[:, 0, :], flat_m, -1.0, None, ALU.mult))
                dve.scalar_tensor_tensor(nm[:, 1, :], flat_m, -1.0, nm[:, 0, :], ALU.mult, ALU.subtract)\
                   .then_inc(sem("nm_ready"), 1)

            def ahead(n, kv, p, whole):
                for j in range(REP):
                    score(n, j, 0, 16)
                maxima(n)

            def finish(n, kv, b, hf):
                dve.wait_ge(sem("out_turned"), n + 1)
                O = TR_[:, :].rearrange("p (i j d) -> p i j d", i=4, j=REP)
                chain(dve.reciprocal(rec[:, :, :], O[:, :, :, HD]))
                chain(dve.tensor_tensor(oo[:, :, :, :], O[:, :, :, 0:HD],
                                        rec[:, :, :].unsqueeze(3).to_broadcast([P, 4, REP, HD]), ALU.mult))
                dve.sem_inc(sem("out_read"), 1)
                t0 = b * TB + hf * 4
                view = x[:, t0:t0 + 4, bass.ds(kv * REP * HD, REP * HD)]
                chain(dve.tensor_tensor(view, view, oo[:, :, :, :].rearrange("p i j d -> p i (j d)"), ALU.add))

            def slot(n, kv, b, nkv, has_next, first):
                for st in range(STEPS):
                    if has_next and st in S_AT:
                        score(n + 1, *S_AT[st])
                    if has_next and st == NM_AT:
                        maxima(n + 1)
                    if st in OUT_AT and not (first and OUT_AT[st] == 1):
                        if OUT_AT[st] == 1:
                            finish(2 * n - 1, kv if b == 1 else kv - 1, 1 - b, 1)
                        else:
                            finish(2 * n, kv, b, 0)

            slots(dve, chain, 16, slot, ahead)
            finish(4 * KV - 1, KV - 1, 1, 1)
            dve.sem_inc(phase_done["att"], 1)

        def att_pool(pool, chain):
            pool.wait_ge(sem("att_qkv"), 1)

            def ahead(n, kv, p, whole):
                t0 = p * TB
                kk = qk[:, t0:t0 + TB, bass.ds(H + kv, 1), :].rearrange("p t h d -> p t (h d)")
                qq = qk[:, t0:t0 + TB, bass.ds(kv * REP, REP), :]
                first = type(n) is int and n == 0

                def row(i, which):
                    return (ks[:, :, i * HD:(i + 1) * HD] if which == "k" else qs[:, :, :, i * HD:(i + 1) * HD])
                for which, src, res, (h0, hs, m0, ms, l0) in (
                        ("k", kk, kr, (0, (2, 5), 1, (3,), 4)), ("q", qq, qr, (0, (1, 4), 2, (3,), 5))):
                    if not first:
                        pool.wait_ge(sem("stack_ps"), T_N * n if which == "q" else T_N * (n - 1) + 1)
                    apart(pool, sem("apart_pool"))
                    chain(pool.tensor_copy(row(h0, which), src))
                    chain(pool.tensor_tensor(res, src, row(h0, which), ALU.subtract))
                    apart(pool, sem("apart_pool"))
                    chain(pool.tensor_copy(row(m0, which), res))
                    chain(pool.tensor_tensor(row(l0, which), res, row(m0, which), ALU.subtract))
                    for i in hs:
                        apart(pool, sem("apart_pool"))
                        chain(pool.tensor_copy(row(i, which), row(h0, which)))
                    for i in ms:
                        apart(pool, sem("apart_pool"))
                        chain(pool.tensor_copy(row(i, which), row(m0, which)))
                    pool.sem_inc(sem("stacked"), 1)
                if not fixed_below(n, 2):
                    pool.wait_ge(sem("pv_step"), STEPS * (n - 1))
                apart(pool, sem("apart_pool"))
                chain(pool.tensor_copy(vst[:, p, :, 0:HD], vv[:, t0:t0 + TB, bass.ds(kv, 1), :]
                                       .rearrange("p t h d -> p t (h d)")))
                pool.sem_inc(sem("v_ready"), 1)

            def slot(n, kv, b, nkv, has_next, first):
                if has_next:
                    ahead(n + 1, nkv, 1 - b, True)

            slots(pool, chain, 30, slot, ahead)

        def att_sync(sp):
            def rows(n, p):
                sp.wait_ge(sem("nmt_ready"), n + 1)
                if not fixed_below(n, 2):
                    sp.wait_ge(sem("score1"), X_N * (n - 1))
                for part in range(2):
                    sp.dma_start(qst[KS + part:KS + part + 1, p, :, :].rearrange("p j (t c) -> p (j t) c", c=P),
                                 nmt[part * REP * TB:(part + 1) * REP * TB, :]).then_inc(sem("rows_in"), 16)
            slots(sp, None, 0, lambda n, kv, b, nkv, has_next, first: rows(n + 1, 1 - b) if has_next else None,
                  lambda n, kv, p, whole: rows(n, p))

        @block.sync
        def _(sp):
            for dst, src in ((x[:, :, :], a["x"].rearrange("(t p) n -> p t n", p=P)), (ident[:, :], a["ident"]),
                             (hb[:, :], a["b_base"]), (lora_b[:, :], a["lora_b_t"])):
                sp.dma_start(dst, src).then_inc(x_loaded, 16)
            load_pieces_sync(sp, "ffn_a")
            enter(sp, "lin")
            lin_sync(sp)
            enter(sp, "mem_a")
            mem_prep_sync(sp)
            enter(sp, "att")
            sp.dma_start(bqkv[:, :], a["b_qkv"]).then_inc(sem("att_loaded"), 16)
            sp.dma_start(rope[:, :, :, :], a["rope"]).then_inc(sem("att_loaded"), 16)
            load_pieces_sync(sp, "att")
            att_sync(sp)
            sp.wait_ge(phase_done["mem_b"], 1)
            sp.dma_start(out.rearrange("(t p) n -> p t n", p=P), x[:, :, :]).then_inc(sem("stored"), 16)
            sp.wait_ge(sem("stored"), 16)

        @block.scalar
        def _(act):
            split_pieces_act(act, "ffn_a")
            act.wait_ge(x_loaded, 64)
            act.activation(identb[:, :], ident[:, :], ACT.Copy).then_inc(sem("identb_ready"), 1)
            stats_act(act, "ffn_a")
            ffn_act(act, "ffn_a")
            enter(act, "lin")
            lin_act(act)
            enter(act, "ffn_b")
            stats_act(act, "ffn_b")
            ffn_act(act, "ffn_b")
            enter(act, "mem_a")
            mem_prep_act(act)
            stats_act(act, "mem_a")
            mem_act(act, "mem_a")
            enter(act, "att")
            split_pieces_act(act, "att")
            stats_act(act, "att")
            qkv_act(act)
            att_act(act)
            enter(act, "mem_b")
            stats_act(act, "mem_b")
            mem_act(act, "mem_b")

        @block.gpsimd
        def _(pool):
            chain = Chain(pool, pool_steps)
            pool.wait_ge(x_loaded, 64)
            pool.wait_ge(sem("hb_ready"), 1)
            ffn_pool(pool, "ffn_a")
            enter(pool, "lin")
            lin_pool(pool, chain)
            enter(pool, "ffn_b")
            ffn_pool(pool, "ffn_b")
            enter(pool, "mem_a")
            mem_pool(pool, chain, "mem_a")
            enter(pool, "att")
            qkv_pool(pool)
            att_pool(pool, chain)
            enter(pool, "mem_b")
            mem_pool(pool, chain, "mem_b")

        def presets_dve(dve, chain):
            chain(dve.memset(lg[:, :, :], SENTINEL))
            chain(dve.memset(rep[:, :, :], SENTINEL))

        @block.vector
        def _(dve):
            chain = Chain(dve, dve_steps)
            chain(dve.memset(ones[:, :], 1.0))
            dve.wait_ge(x_loaded, 64)
            chain(dve.tensor_scalar(hb[:, :], hb[:, :], 0.5, None, ALU.mult))
            dve.sem_inc(sem("hb_ready"), 1)
            presets_dve(dve, chain)
            split_pieces_dve(dve, "ffn_a")
            stats_dve(dve, chain, "ffn_a")
            ffn_dve(dve, chain, "ffn_a")
            lin_dve(dve, chain)
            presets_dve(dve, chain)
            stats_dve(dve, chain, "ffn_b")
            ffn_dve(dve, chain, "ffn_b")
            mem_prep_dve(dve, chain)
            stats_dve(dve, chain, "mem_a")
            mem_dve(dve, chain, "mem_a")
            split_pieces_dve(dve, "att")
            stats_dve(dve, chain, "att")
            qkv_dve(dve, chain)
            att_dve(dve, chain)
            stats_dve(dve, chain, "mem_b")
            mem_dve(dve, chain, "mem_b")

        @block.tensor
        def _(pe):
            pe.wait_ge(x_loaded, 64)
            pe.wait_ge(sem("piece_lo"), past("ffn_a", "piece_lo") + 2 * KC)
            ffn_pe(pe, "ffn_a")
            enter(pe, "lin")
            lin_pe(pe)
            enter(pe, "ffn_b")
            ffn_pe(pe, "ffn_b")
            enter(pe, "mem_a")
            mem_prep_pe(pe)
            pe.wait_ge(sem("mem_ready"), 1)
            mem_pe(pe, "mem_a")
            enter(pe, "att")
            pe.wait_ge(sem("identb_ready"), 1)
            qkv_pe(pe)
            att_pe(pe)
            enter(pe, "mem_b")
            mem_pe(pe, "mem_b")


def decay_tables():
    f = np.float32
    slope = ((1.0 / 2.0 ** (8.0 / LH)) ** (np.arange(LH) + 1.0) * (1.0 - 1 / (32 - 1 + 1e-05) + 1e-05)).astype(f)
    slope = slope.astype(np.float64)[:, None]
    r = np.arange(P) + 1.0
    q = np.exp(-slope * r)
    k = np.exp(-slope * (P - r))
    diff = r[None, :] - r[:, None]
    diag = np.where(diff >= 0, np.exp(-slope[:, :, None] * np.maximum(diff, 0)), 0.0)
    both = np.stack([diag, np.broadcast_to(q[:, None, :], diag.shape)], axis=2)
    block = np.broadcast_to(np.exp(-slope * P).T, (P, LH))
    return both.astype(f), np.ascontiguousarray(k.T).astype(f), np.ascontiguousarray(block).astype(f)


def rope_tables():
    f = np.float32
    inv = (1.0 / np.power(f(10000.0), np.arange(0, HD, 2, dtype=f) / f(HD))).astype(f)
    ang = (np.arange(TB * P, dtype=f)[:, None] * inv[None, :]).astype(f).astype(np.float64)
    c, s = np.cos(ang), np.sin(ang)
    both = np.stack([np.concatenate([c, c], 1), np.concatenate([-s, s], 1)], axis=1)
    return np.ascontiguousarray(both.reshape(TB, P, 2, HD).transpose(1, 0, 2, 3)).astype(f)


def chunked(w):
    return np.ascontiguousarray(w.reshape(KC, P, -1).transpose(1, 0, 2))


def rows(v):
    return np.ascontiguousarray(np.broadcast_to(v.reshape(1, -1), (P, v.size)))


def kernel(**inputs):
    import concourse.bacc as _bacc
    from concourse.bass_utils import run_bass_kernel_spmd as _run

    i = {n: np.asarray(v) for n, v in inputs.items()}
    f = np.float32
    decay, kdec, bdec = decay_tables()
    arr = {}
    arr["x"] = i["L0_attn_hidden_states"].reshape(T, D)
    arr["ident"] = np.eye(P, dtype=f)
    arr["b_base"] = rows(i["L0_ffn_b_base"])
    arr["w_base_t"] = chunked(i["L0_ffn_W_base"].T)
    a_t = i["L0_ffn_A"].reshape(E * R, D).T
    arr["w_ag_t"] = chunked(np.concatenate([a_t, i["L0_ffn_W_gate"].T, np.zeros((D, 256 - P - E), f)], axis=1))
    arr["lora_b_t"] = i["L0_ffn_B"].transpose(0, 2, 1).reshape(E * R, D)
    qkv = i["L0_attn_qkv_w"].reshape(LH, 3, P, KC, P)
    gw = i["L0_attn_gate_w"].reshape(LH, 1, P, KC, P)
    arr["w_heads"] = np.concatenate([qkv, gw], axis=1).transpose(0, 4, 1, 3, 2)
    arr["ow_heads"] = i["L0_attn_out_w"].T.reshape(LH, P, D)
    arr["norm_w"] = i["L0_attn_norm_w"].reshape(LH, P).T
    arr["decay"], arr["kdec"], arr["bdec"] = decay, kdec, bdec
    arr["wqkv"] = chunked(np.concatenate([i["L1_attn_wq"], i["L1_attn_wk"], i["L1_attn_wv"]], axis=1))
    arr["b_qkv"] = rows(np.concatenate([i["L1_attn_bq"], i["L1_attn_bk"], i["L1_attn_bv"]]))
    arr["rope"] = rope_tables()
    arr["wq_mem"] = i["L1_ffn_Wq"]
    arr["wr"] = i["L1_ffn_Wr"]
    arr["wr_t"] = i["L1_ffn_Wr"].T
    arr["keys_t"] = i["L1_ffn_aux_keys"].T
    arr["values_t"] = chunked(i["L1_ffn_aux_values"].T).reshape(P, KC * NSLOT)
    arr["wvd_t"] = chunked(i["L1_ffn_Wvd"].T).reshape(P, KC * VB)
    arr["wvu_t"] = i["L1_ffn_Wvu"].T
    arr["wu1_t"] = chunked(i["L1_ffn_Wu1"].T)
    arr["log_rel"] = rows(i["L1_ffn_log_rel"])
    arr["bu1"] = rows(i["L1_ffn_bu1"])
    arr["wu2"] = rows(i["L1_ffn_Wu2"])
    arr["scalars"] = rows(np.concatenate([i["L1_ffn_bu2"].reshape(1), i["L1_ffn_gate_w1"].reshape(1),
                                          i["L1_ffn_gate_bias"].reshape(1)]))
    arr = {n: np.ascontiguousarray(v) for n, v in arr.items()}

    nc = _bacc.Bacc("TRN2", target_bir_lowering=False, num_devices=1)
    aps = {n: nc.dram_tensor(f"in_{n}", v.shape, F32, kind="ExternalInput").ap() for n, v in arr.items()}
    out = nc.dram_tensor("out_x", (T, D), F32, kind="ExternalOutput").ap()
    program(nc, aps, out)
    r = _run(nc, [{f"in_{n}": v for n, v in arr.items()}], core_ids=[0])
    return np.asarray(r.results[0]["out_x"]).reshape(B, T // B, D)
```

```python
from contextlib import ExitStack

import numpy as np

import concourse.bass as bass
from concourse import mybir

F32 = mybir.dt.float32
F32R = mybir.dt.float32r
BF16 = mybir.dt.bfloat16
ALU = mybir.AluOpType
ACT = mybir.ActivationFunctionType
AX = mybir.AxisListType.X

P = 128
D = 512
KC = D // P
NT = 16
T = NT * P
B = 2
XL = 4
TB = NT // B
EPS = 1e-5

E, R = 8, 16
LH = 32
G = 4
GT = T // G
CH = GT // P
BOT, RDIM, NSLOT, VB = 64, 48, 128, 32
H, KV, HD = 32, 8, 16
REP = H // KV
QK = H + KV
NSPLIT = 6
KS = NSPLIT * HD
VW = 32

SENTINEL, TAKEN, TAKEN_LINE = -3.0e38, -3.3e38, -3.2e38
LOW = -1.0e30
GELU_SCALE = float(np.sqrt(2.0 / np.pi))


def fixed_below(value, n):
    return type(value) is int and value < n


class Chain:

    def __init__(self, eng, sem):
        self.eng, self.sem, self.n, self.base = eng, sem, 0, 0

    def beside(self, ins):
        self.n += 1
        ins.then_inc(self.sem, 1)

    def __call__(self, ins):
        self.n += 1
        ins.then_inc(self.sem, 1)
        self.eng.wait_ge(self.sem, self.base + self.n)


def apart(eng, sem):
    eng.sem_inc(sem, 1)


def looped(chains, eng, start, stop, steps, body):
    (chain,) = chains if chains else (None,)
    with eng.Fori(start, stop) as i:
        eng.get_value_cache().nocache = True
        if chain:
            before = chain.n
            chain.base = (i - start) * steps
        body(i)
        if chain:
            assert chain.n - before == steps, (chain.n - before, steps)
            chain.base = 0
            chain.n = before + steps * (stop - start)


def program(nc, a, out):
    ctx = ExitStack()
    with ctx:
        def sb(name, shape, dt=F32, where=ctx):
            return where.enter_context(nc.sbuf_tensor(name, shape, dt))

        sems = {}

        def sem(name):
            if name not in sems:
                sems[name] = ctx.enter_context(nc.semaphore(name))
            return sems[name]

        psum = ctx.enter_context(nc.psum_tensor("psum", [P, 8, 512], F32))
        bank = [psum[:, i, :] for i in range(8)]

        x = sb("x", [P, NT, D])
        ident = sb("ident", [P, P])
        identb = sb("identb", [P, P], BF16)
        ones = sb("ones", [P, P])
        stats = sb("stats", [P, NT, 6])
        rstd = sb("rstd", [P, NT])
        nmr = sb("nmr", [P, NT])
        ve = sb("ve", [P, NT])
        sm = [sb(f"sm{i}", [P, NT]) for i in range(4)]
        hb = sb("half_bias", [P, D])
        wb_hi = sb("wb_hi", [P, KC, D], F32R)
        wb_lo = sb("wb_lo", [P, KC, D], F32R)
        wa_hi = sb("wa_hi", [P, KC, 256], F32R)
        wa_lo = sb("wa_lo", [P, KC, 256], F32R)
        lora_b = sb("lora_b", [P, D])
        x_dram = nc.dram_tensor("x_kept", [NT, P, D], F32, kind="Internal").ap()

        tctx = ExitStack()
        xn = sb("xn", [P, 2, D], where=tctx)
        xt_hi = sb("xt_hi", [P, 2, KC, P], F32R, where=tctx)
        xt_lo = sb("xt_lo", [P, 2, KC, P], F32R, where=tctx)
        xb = sb("xb", [P, 2, D], where=tctx)
        lg = sb("lg", [P, 2, 16], where=tctx)
        top = sb("top", [P, 2, 8], where=tctx)
        rep = sb("rep", [P, 2, 8], where=tctx)
        rest = sb("rest", [P, 2, 16], where=tctx)
        lgm = sb("lgm", [P, 2, 8], where=tctx)
        ex = sb("ex", [P, 2, 8], where=tctx)
        mk = sb("mk", [P, 2, 8], where=tctx)
        rw = sb("rw", [P, 2, 8], where=tctx)
        rsum = sb("rsum", [P, 2, 2], where=tctx)
        hw = sb("hw", [P, 2, P], where=tctx)
        hwt = sb("hwt", [P, 2, P], where=tctx)
        w1_hi = sb("w1_hi", [P, KC, 384], F32R, where=tctx)
        w1_lo = sb("w1_lo", [P, KC, 384], F32R, where=tctx)
        v3 = sb("v3", [P, D], where=tctx)
        brow = sb("brow", [P, 384], where=tctx)
        wu2 = sb("wu2", [P, P], where=tctx)
        sc3 = sb("sc3", [P, 4], where=tctx)
        nv = sb("nv", [P, NT], where=tctx)
        lv = sb("lv", [P, NT], where=tctx)
        hr = sb("hr", [P, NT], where=tctx)
        hn = sb("hn", [P, NT], where=tctx)
        lsum = sb("lsum", [P, 2], where=tctx)
        mean1 = sb("mean1", [P, 2], where=tctx)
        rt2 = sb("rt2", [P, 2, NSLOT], where=tctx)
        mtop = sb("mtop", [P, 2, 8], where=tctx)
        nmx = sb("nmx", [P, 2, 2], where=tctx)
        psm = sb("psm", [P, 2, 2], where=tctx)
        lrn = sb("lrn", [P, 2, 2], where=tctx)
        th1 = sb("th1", [P, 2, 2], where=tctx)
        uu = sb("uu", [P, 2, 2], where=tctx)
        th2 = sb("th2", [P, 2, 2], where=tctx)
        gm = sb("gm", [P, 4, 2], where=tctx)
        gu_in = sb("gu_in", [P, 2], where=tctx)
        small = sb("small", [P, 256], where=tctx)
        small2 = sb("small2", [P, 256], where=tctx)
        v2t = sb("v2t", [P, NSLOT], where=tctx)
        sctx = ExitStack()
        xt2_hi = sb("xt2_hi", [P, 2, KC, P], F32R, where=sctx)
        xt2_lo = sb("xt2_lo", [P, 2, KC, P], F32R, where=sctx)
        stage = sb("stage", [P, 6272], where=sctx)
        sctx.close()
        XT_HI, XT_LO = [xt_hi, xt2_hi], [xt_lo, xt2_lo]
        qk = sb("qk", [P, NT, QK, HD], where=tctx)
        vv = sb("vv", [P, NT, KV, HD], where=tctx)
        actx = ExitStack()
        wq_hi = sb("wq_hi", [P, KC, 768], F32R, where=actx)
        wq_lo = sb("wq_lo", [P, KC, 768], F32R, where=actx)
        bqkv = sb("bqkv", [P, 768], where=actx)
        rope = sb("rope", [P, TB, 2, HD], where=actx)
        qkb = sb("qkb", [P, 2, QK, HD], where=actx)
        rot = sb("rot", [P, 2, QK, HD], where=actx)
        rg = sb("rg", [P, 2, 2, 384], where=actx)
        pr = sb("pr", [P, 2, 2, NSLOT], where=actx)
        prt = sb("prt", [P, 2, 2, NSLOT], where=actx)
        gc = sb("gc", [P, 2, 2, P], where=actx)
        gt = sb("gt", [P, 2, 2, P], where=actx)
        gg = sb("gg", [P, 2, P], where=actx)
        actx.close()
        rec = sb("rec", [P, 4, 2, 2], where=tctx)
        qs = sb("qs", [P, 2, TB, 2, KS], BF16, where=tctx)
        ks = sb("ks", [P, TB, KS], BF16, where=tctx)
        qst = sb("qst", [P, 4, 2, TB * P], BF16, where=tctx)
        kst = sb("kst", [P, 2, TB * P], BF16, where=tctx)
        vst = sb("vst", [P, 2, TB, VW], where=tctx)
        pp = sb("pp", [P, 8, 512], where=tctx)
        m1 = sb("m1", [P, 2, TB], where=tctx)
        nm = sb("nm", [P, 2, 2 * TB], BF16, where=tctx)
        nmt = sb("nmt", [4 * TB, P], BF16, where=tctx)
        pvs = xb[:, 1, :]
        qr = xb[:, 0, 0:2 * TB * HD].rearrange("p (t j d) -> p t j d", t=TB, j=2)
        kr = xn[:, 0, 0:TB * HD].rearrange("p (t d) -> p t d", t=TB)
        osb = sb("osb", [P, 512], where=tctx)
        oo = sb("oo", [P, 2, 4, 2, HD], where=tctx)
        tctx.close()

        lctx = ExitStack()
        l_xn = sb("l_xn", [P, 2, D], where=lctx)
        back = ExitStack()
        x_in = sb("x_in", [P, NT, D], where=back)
        back.close()
        xa_hi = sb("xa_hi", [P, KC, T], F32R, where=lctx)
        xa_lo = sb("xa_lo", [P, KC, T], F32R, where=lctx)
        sq = sb("sq", [P, T], where=lctx)
        w_raw = sb("w_raw", [P, 4, KC, P], where=lctx)
        w_hi = sb("w_hi", [P, 4, KC, P], F32R, where=lctx)
        w_lo = sb("w_lo", [P, 4, KC, P], F32R, where=lctx)
        ow_raw = sb("ow_raw", [P, D], where=lctx)
        ow_hi = sb("ow_hi", [P, D], F32R, where=lctx)
        ow_lo = sb("ow_lo", [P, D], F32R, where=lctx)
        dt_tab = sb("dt_tab", [P, 2, P], where=lctx)
        kdec = sb("kdec", [P, LH], where=lctx)
        bdec = sb("bdec", [P, LH], where=lctx)
        nwh = sb("nwh", [P, LH], where=lctx)
        qT = sb("qT", [P, 2, GT], where=lctx)
        kvt = sb("kvt", [P, 2, CH, 2, P], where=lctx)
        kT = sb("kT", [P, GT], where=lctx)
        gate = sb("gate", [P, GT], where=lctx)
        qd = sb("qd", [P, GT], where=lctx)
        ktok = sb("ktok", [P, GT], where=lctx)
        sc = sb("sc", [P, GT], where=lctx)
        kvs = sb("kvs", [P, CH, P], where=lctx)
        at = sb("at", [P, GT], where=lctx)
        at2 = sb("at2", [P, GT], where=lctx)
        y1 = sb("y1", [P, GT], where=lctx)
        y_hi = sb("y_hi", [P, GT], F32R, where=lctx)
        y_lo = sb("y_lo", [P, GT], F32R, where=lctx)
        rnorm = sb("rnorm", [P, NT], where=lctx)
        lctx.close()

        PHASES = ["ffn_a", "lin", "ffn_b", "mem_a", "att", "mem_b"]
        phase_done = {p: sem(f"{p}_done") for p in PHASES}
        x_loaded, consts_loaded = sem("x_loaded"), sem("consts_loaded")
        pe_steps, act_steps = sem("pe_steps"), sem("act_steps")
        dve_steps, pool_steps = sem("dve_steps"), sem("pool_steps")

        RAISED = {}
        for what in ("bn", "xn", "xt", "xhi", "xlo"):
            RAISED[what] = {p: NT for p in PHASES}
        for what in ("ve", "sd", "norm"):
            RAISED[what] = {p: 1 for p in PHASES}
        RAISED["used"] = {"ffn_a": NT // 2, "ffn_b": NT // 2, "mem_a": NT // 2, "att": NT, "mem_b": NT // 2}
        for what in ("a", "lg", "ex", "ht", "hw", "hwt"):
            RAISED[what] = {p: NT // 2 for p in ("ffn_a", "ffn_b")}
        for what in ("x", "y", "xb"):
            RAISED[what] = {p: NT for p in ("ffn_a", "ffn_b", "mem_a", "mem_b")}
        for what in ("read", "pr", "prt", "pt", "cubic", "gt", "gelu", "am", "learned", "t1", "u", "t2"):
            RAISED[what] = {p: NT // 2 for p in ("mem_a", "mem_b")}
        for what in ("ls", "lm", "nv", "vh", "lv"):
            RAISED[what] = {p: 1 for p in ("mem_a", "mem_b")}

        def past(phase, what):
            return sum(n for p, n in RAISED[what].items() if PHASES.index(p) < PHASES.index(phase))

        block = ctx.enter_context(nc.Block())

        def before(phase):
            n = PHASES.index(phase)
            return phase_done[PHASES[n - 1]] if n else None

        def enter(eng, phase):
            if before(phase) is not None:
                eng.wait_ge(before(phase), 1)

        def kc(cols):
            return stage[:, cols[0]:cols[1]].rearrange("p (k n) -> p k n", k=KC)
        WB, WA = (0, 2048), (2048, 3072)
        WU1, VAL, WVD, WVU, WQM, WQKV, W1F = ((0, 512), (512, 1024), (1024, 1152), (1152, 1664), (1664, 2176),
                                              (2176, 5248), (5248, 6272))
        FFN_SPLITS = [(kc(WB), wb_hi[:, :, :], wb_lo[:, :, :]), (kc(WA), wa_hi[:, :, :], wa_lo[:, :, :])]
        MEM_SPLITS = [(kc(WU1), w1_hi[:, :, 256:384], w1_lo[:, :, 256:384]),
                      (kc(W1F), w1_hi[:, :, 0:256], w1_lo[:, :, 0:256])]
        ATT_SPLITS = [(kc(WQKV)[:, k, :], wq_hi[:, k, :], wq_lo[:, k, :]) for k in range(KC)]

        def bn_dve(dve, phase, t):
            dve.bn_stats(stats[:, t, :], x[:, t, :]).then_inc(sem("bn"), 1)

        def stats_dve(dve, chain, phase):
            dve.wait_ge(sem("bn"), past(phase, "bn") + NT)
            s, d, m2, q = sm
            chain(dve.tensor_tensor(s[:, :], stats[:, :, 1], stats[:, :, 4], ALU.add))
            chain(dve.tensor_tensor(d[:, :], stats[:, :, 1], stats[:, :, 4], ALU.subtract))
            chain(dve.tensor_tensor(m2[:, :], stats[:, :, 2], stats[:, :, 5], ALU.add))
            chain(dve.scalar_tensor_tensor(q[:, :], d[:, :], 0.25, d[:, :], ALU.mult, ALU.mult))
            chain(dve.scalar_tensor_tensor(q[:, :], m2[:, :], 1.0 / D, q[:, :], ALU.mult, ALU.add))
            dve.tensor_scalar(ve[:, :], q[:, :], EPS, None, ALU.add).then_inc(sem("ve"), 1)
            dve.wait_ge(sem("sd"), past(phase, "sd") + 1)
            chain(dve.reciprocal(rstd[:, :], rstd[:, :]))
            chain(dve.tensor_tensor(d[:, :], rstd[:, :], rstd[:, :], ALU.mult))
            chain(dve.scalar_tensor_tensor(d[:, :], d[:, :], -0.5, ve[:, :], ALU.mult, ALU.mult))
            chain(dve.scalar_tensor_tensor(rstd[:, :], d[:, :], 1.5, rstd[:, :], ALU.add, ALU.mult))
            dve.scalar_tensor_tensor(nmr[:, :], s[:, :], -0.5, rstd[:, :], ALU.mult, ALU.mult)\
               .then_inc(sem("norm"), 1)
            dve.wait_ge(sem("norm"), past(phase, "norm") + 1)

        def stats_act(act, phase):
            act.wait_ge(sem("ve"), past(phase, "ve") + 1)
            act.activation(rstd[:, :], ve[:, :], ACT.Sqrt).then_inc(sem("sd"), 1)

        def norm_dve(dve, phase, t, s, first, buf=None):
            buf = xn if buf is None else buf
            if not first:
                dve.wait_ge(sem("xt"), past(phase, "xt") + t - 1)
            dve.tensor_scalar(buf[:, s, :], x[:, t, :], rstd[:, bass.ds(t, 1)], nmr[:, bass.ds(t, 1)],
                              ALU.mult, ALU.add).then_inc(sem("xn"), 1)

        def norm_act(act, t, s):
            act.activation(xn[:, s, :], x[:, t, :], ACT.Identity, scale=rstd[:, bass.ds(t, 1)],
                           bias=nmr[:, bass.ds(t, 1)]).then_inc(sem("xn"), 1)

        def first_norms_act(act, phase):
            act.wait_ge(sem("norm"), past(phase, "norm") + 1)
            for s in (0, 1):
                norm_act(act, s, s)

        def transpose_pe(pe, phase, t, s, first, ps, buf=None):
            buf = xn if buf is None else buf
            pe.wait_ge(sem("xn"), past(phase, "xn") + t + 1)
            if not first:
                pe.wait_ge(sem("xlo"), past(phase, "xlo") + t - 1)
            for k in range(KC):
                last = pe.transpose(ps[:, k * P:(k + 1) * P], buf[:, s, k * P:(k + 1) * P], ident[:, :])
            last.then_inc(sem("xt"), 1)

        def hi_act(act, phase, t, s, used, ps, xh=None):
            xh = xt_hi if xh is None else xh
            act.wait_ge(sem("xt"), past(phase, "xt") + t + 1)
            if used is not None:
                act.wait_ge(sem("used"), past(phase, "used") + used)
            act.activation(xh[:, s, :, :], ps[:, :].rearrange("p (k n) -> p k n", k=KC), ACT.Copy)\
               .then_inc(sem("xhi"), 1)

        def lo_dve(dve, phase, t, s, ps, xh=None, xl=None):
            xh, xl = (xt_hi, xt_lo) if xh is None else (xh, xl)
            dve.wait_ge(sem("xhi"), past(phase, "xhi") + t + 1)
            dve.tensor_tensor(xl[:, s, :, :], ps[:, :].rearrange("p (k n) -> p k n", k=KC),
                              xh[:, s, :, :].bitcast(F32), ALU.subtract).then_inc(sem("xlo"), 1)

        def product_pe(pe, ps, s, hi, lo, c0, c1_, xh=None, xl=None, stop=True):
            xh, xl = (xt_hi, xt_lo) if xh is None else (xh, xl)
            n = 0
            for left, right in ((xh, hi), (xh, lo), (xl, hi)):
                for k in range(KC):
                    last = pe.matmul(ps, left[:, s, k, :], right[:, k, c0:c1_], start=(n == 0),
                                     stop=(stop and n == 3 * KC - 1))
                    n += 1
            return last

        def exists(n, limit):
            return type(n) is not int or 0 <= n < limit

        NP = NT // 2

        def pairs(eng, chain, steps, pair):
            for q in (-1, 0, 1):
                pair(q, q % 2)

            def two(j):
                pair(2 * j, 0)
                pair(2 * j + 1, 1)
            looped([chain] if chain else [], eng, 1, NP // 2 - 1, steps, two)
            for q in (NP - 2, NP - 1, NP):
                pair(q, q % 2)

        def tiles(eng, chain, steps, tile):
            for s in (0, 1):
                tile(s, s, True, False)

            def pair(j):
                for s in (0, 1):
                    tile(2 * j + s, s, False, False)
            looped([chain] if chain else [], eng, 1, NT // 2 - 1, 2 * steps, pair)
            for s in (0, 1):
                tile(NT - 2 + s, s, False, s == 1)

        XTB = [bank[0], bank[1]]
        FFN_A = [bank[2], bank[3]]
        FFN_Y = [bank[4], bank[5]]
        FFN_H = bank[6]

        def transposes_pe(pe, phase, q):
            for s in (0, 1):
                transpose_pe(pe, phase, 2 * q + s, s, fixed_below(q, 1), XTB[s])

        def his_act(act, phase, q, r):
            for s in (0, 1):
                hi_act(act, phase, 2 * q + s, s, None if fixed_below(q, 2) else q - 1, XTB[s], XT_HI[r])

        def norms_act(act, q):
            for s in (0, 1):
                norm_act(act, 2 * q + s, s)

        def los_dve(dve, phase, q, r):
            for s in (0, 1):
                lo_dve(dve, phase, 2 * q + s, s, XTB[s], XT_HI[r], XT_LO[r])

        def ffn_pe(pe, phase):
            def gates(q, r, s):
                return product_pe(pe, FFN_A[r][:, 256 * s:256 * s + 256], s, wa_hi, wa_lo, 0, 256, XT_HI[r], XT_LO[r])

            def pair(q, r):
                if exists(q + 1, NP):
                    transposes_pe(pe, phase, q + 1)
                if exists(q, NP):
                    for s in (0, 1):
                        if not fixed_below(q, 1):
                            pe.wait_ge(sem("x"), past(phase, "x") + 2 * q + (s - 1))
                        mm = product_pe(pe, FFN_Y[s][:, :], s, wb_hi, wb_lo, 0, D, XT_HI[r], XT_LO[r], stop=False)
                    mm.then_inc(sem("used"), 1)
                if exists(q + 1, NP):
                    pe.wait_ge(sem("xlo"), past(phase, "xlo") + 2 * q + 4)
                    if not fixed_below(q, 1):
                        pe.wait_ge(sem("hw"), past(phase, "hw") + q)
                    gates(q + 1, 1 - r, 0)
                if exists(q, NP):
                    pe.wait_ge(sem("hw"), past(phase, "hw") + q + 1)
                    if not fixed_below(q, 1):
                        pe.wait_ge(sem("hwt"), past(phase, "hwt") + q)
                    for s in (0, 1):
                        mm = pe.transpose(FFN_H[:, s * P:(s + 1) * P], hw[:, s, :], ident[:, :])
                    mm.then_inc(sem("ht"), 1)
                if exists(q + 1, NP):
                    gates(q + 1, 1 - r, 1).then_inc(sem("a"), 1)
                if exists(q, NP):
                    pe.wait_ge(sem("hwt"), past(phase, "hwt") + q + 1)
                    for s in (0, 1):
                        pe.matmul(FFN_Y[s][:, :], hwt[:, s, :], lora_b[:, :], start=False, stop=True)\
                          .then_inc(sem("y"), 1)
            pairs(pe, None, 0, pair)

        def ffn_act(act, phase):
            def pair(q, r):
                if exists(q + 1, NP):
                    his_act(act, phase, q + 1, 1 - r)
                if exists(q + 2, NP):
                    norms_act(act, q + 2)
                if exists(q, NP):
                    act.wait_ge(sem("lg"), past(phase, "lg") + q + 1)
                    act.activation(ex[:, :, :], lgm[:, :, :], ACT.Exp).then_inc(sem("ex"), 1)
                    act.wait_ge(sem("ht"), past(phase, "ht") + q + 1)
                    if not fixed_below(q, 1):
                        act.wait_ge(sem("y"), past(phase, "y") + 2 * q)
                    act.activation(hwt[:, :, :], FFN_H[:, 0:2 * P].rearrange("p (s n) -> p s n", s=2), ACT.Copy)\
                       .then_inc(sem("hwt"), 1)
            first_norms_act(act, phase)
            pairs(act, None, 0, pair)

        def ffn_pool(pool, phase):
            def tile(t, s, first, last):
                if not first:
                    pool.wait_ge(sem("x"), past(phase, "x") + t - 1)
                pool.tensor_tensor(xb[:, s, :], x[:, t, :], hb[:, :], ALU.add).then_inc(sem("xb"), 1)

            tiles(pool, None, 0, tile)

        def ffn_dve(dve, chain, phase):
            def route(q, r):
                A_ = FFN_A[r].rearrange("p (s n) -> p s n", s=2)
                dve.wait_ge(sem("a"), past(phase, "a") + q + 1)
                chain(dve.tensor_copy(lg[:, :, 0:8], A_[:, :, P:P + 8]))
                apart(dve, sem("apart_dve"))
                chain.beside(dve.max(top[:, 0, :], lg[:, 0, 0:8]))
                chain(dve.max(top[:, 1, :], lg[:, 1, 0:8]))
                dve.tensor_tensor(lgm[:, :, :], lg[:, :, 0:8], top[:, :, 0:1].to_broadcast([P, 2, 8]), ALU.subtract)\
                   .then_inc(sem("lg"), 1)
                chain(dve.tensor_copy(rep[:, :, 0:2], top[:, :, 0:2]))
                apart(dve, sem("apart_dve"))
                for s, done in ((0, chain.beside), (1, chain)):
                    done(dve.match_replace(out=rest[:, s, :], in_to_replace=rep[:, s, :], in_values=lg[:, s, :],
                                           imm_value=TAKEN))
                chain(dve.tensor_scalar(mk[:, :, :], rest[:, :, 0:8], TAKEN_LINE, None, ALU.is_lt))
                dve.wait_ge(sem("ex"), past(phase, "ex") + q + 1)
                chain(dve.tensor_tensor(rw[:, :, :], ex[:, :, :], mk[:, :, :], ALU.mult))
                chain(dve.tensor_reduce(rsum[:, 0, :], rw[:, :, :], AX, ALU.add))
                chain(dve.reciprocal(rsum[:, 1, :], rsum[:, 0, :]))
                chain(dve.tensor_tensor(rw[:, :, :], rw[:, :, :], rsum[:, 1, :].unsqueeze(2).to_broadcast([P, 2, 8]),
                                        ALU.mult))
                if not fixed_below(q, 1):
                    dve.wait_ge(sem("ht"), past(phase, "ht") + q)
                dve.tensor_tensor(hw[:, :, :].rearrange("p s (e r) -> p s e r", e=E),
                                  A_[:, :, 0:P].rearrange("p s (e r) -> p s e r", e=E),
                                  rw[:, :, :].unsqueeze(3).to_broadcast([P, 2, E, R]), ALU.mult)\
                   .then_inc(sem("hw"), 1)

            def add(q):
                for s in (0, 1):
                    t = 2 * q + s
                    dve.wait_ge(sem("y"), past(phase, "y") + t + 1)
                    dve.wait_ge(sem("xb"), past(phase, "xb") + t + 1)
                    dve.scalar_tensor_tensor(x[:, t, :], FFN_Y[s][:, :], 0.5, xb[:, s, :], ALU.mult, ALU.add)\
                       .then_inc(sem("x"), 1)

            def next_stats(q):
                for s in (0, 1):
                    t = 2 * q + s
                    dve.wait_ge(sem("x"), past(phase, "x") + t + 1)
                    bn_dve(dve, phase, t)

            def pair(q, r):
                if exists(q - 1, NP):
                    add(q - 1)
                if exists(q + 1, NP):
                    los_dve(dve, phase, q + 1, 1 - r)
                if exists(q, NP):
                    route(q, r)
                if exists(q - 1, NP):
                    next_stats(q - 1)
            pairs(dve, chain, 2 * 11, pair)
            dve.wait_ge(sem("x"), past(phase, "x") + NT)
            dve.sem_inc(phase_done[phase], 1)

        QQ, KK, VV, GG = range(4)
        PJ = bank[0]
        PKV = [bank[1], bank[2]]
        TS, KVP, ATP = bank[3], bank[4], bank[5]
        OUTP = [bank[6], bank[7]]
        SLOTS = LH * G
        KINDS = ["q", "k", "v", "g", "o"]
        FIRST_TILES = [0, 1, 2, 3]
        TILES_IN = {(0, QQ): [4], (0, KK): [5], (0, VV): [6, 7],
                    (1, QQ): [8, 9], (1, KK): [10, 11, 12], (1, VV): [13, 14, 15]}

        def tiles_in(k, kind):
            return TILES_IN.get((k, kind), []) if type(k) is int else []

        def c_(c):
            return slice(c * P, (c + 1) * P)

        def heads(eng, chain, steps, slot):
            def head(h, first):
                for g in range(G):
                    slot(4 * h + g, h, g, h if g >= 1 else h - 1, h if g >= 2 else h - 1,
                         not first or g >= 1, not first or g >= 2, True)
            head(0, True)
            looped([chain] if chain else [], eng, 1, LH, steps, lambda h: head(h, False))
            slot(SLOTS, LH, 0, LH - 1, LH - 1, True, True, False)
            slot(SLOTS + 1, LH, 1, LH, LH - 1, False, True, False)

        def lin_pe(pe):
            def turn(t):
                transpose_pe(pe, "lin", t, t % 2, t < 2, OUTP[t % 2], l_xn)
            for t in FIRST_TILES:
                turn(t)

            def project(kind, h, g):
                pe.wait_ge(sem(f"w_lo_{KINDS[kind]}"), h + 1)
                n = 0
                for w, xs in ((w_hi, xa_hi), (w_hi, xa_lo), (w_lo, xa_hi)):
                    for k in range(KC):
                        last = pe.matmul(PJ[:, :], w[:, kind, k, :], xs[:, k, g * GT:(g + 1) * GT],
                                         start=(n == 0), stop=(n == 3 * KC - 1))
                        n += 1
                last.then_inc(sem(f"proj_{KINDS[kind]}"), 1)

            def project_kv(half, h, g, between=None):
                if half == 0:
                    pe.wait_ge(sem("w_lo_k"), h + 1)
                    pe.wait_ge(sem("w_lo_v"), h + 1)
                for c in (0, 1):
                    t0 = g * GT + (2 * half + c) * P
                    n = 0
                    for xs, w in ((xa_hi, w_hi), (xa_lo, w_hi), (xa_hi, w_lo)):
                        for k in range(KC):
                            last = pe.matmul(PKV[half][:, c * 256:(c + 1) * 256].rearrange("p (a n) -> p a n", a=2),
                                             xs[:, k, t0:t0 + P], w[:, KK:VV + 1, k, :],
                                             start=(n == 0), stop=(n == 3 * KC - 1))
                            n += 1
                            if between and n % 6 == 2:
                                between(2 * c + n // 6)
                last.then_inc(sem("proj_kv"), 1)

            def turned(k, kind):
                later = tiles_in(k, kind)
                return (lambda n: turn(later[n]) if n < len(later) else None) if later else None

            def slot(k, h, g, h1, h2, has1, has2, has0):
                r, r1 = g % 2, (g + 1) % 2
                m, g1 = k - 1, (g - 1) % G
                if has0:
                    if has2:
                        pe.wait_ge(sem("act_g"), k - 1)
                    if fixed_below(h, 1):
                        pe.wait_ge(sem("xlo"), past("lin", "xlo") + CH * (g + 1))
                    project(QQ, h, g)
                    for t in tiles_in(k, QQ):
                        turn(t)
                if has1:
                    pe.wait_ge(sem("act_kv"), 2 * (m + 1))
                    if has2:
                        pe.wait_ge(sem("masked"), m)
                    for c in range(CH):
                        mm = pe.transpose(TS[:, c_(c)], kvt[:, r1, c, 0, :], ident[:, :])
                    mm.then_inc(sem("tr_k"), 1)
                if has0:
                    project_kv(0, h, g, turned(k, KK))
                if has1:
                    pe.wait_ge(sem("ktok_ready"), m + 1)
                    if has2:
                        pe.wait_ge(sem("kv_ready"), m)
                    for c in range(CH - g1 % 2):
                        mm = pe.matmul(KVP[:, c_(c)], ktok[:, c_(c)], kvt[:, r1, c, 1, :], start=True, stop=True)
                    mm.then_inc(sem("kv_ps"), 1)
                    pe.wait_ge(sem("kT_ready"), m + 1)
                    pe.wait_ge(sem("act_q"), m + 1)
                    for c in range(CH):
                        mm = pe.matmul(TS[:, c_(c)], kT[:, c_(c)], qT[:, r1, c_(c)], start=True, stop=True)
                    mm.then_inc(sem("score_ps"), 1)
                if has2:
                    pe.wait_ge(sem("w_lo_o"), h2 + 1)
                    pe.wait_ge(sem("y_lo_ready"), k - 1)

                def output(c):
                    u = 4 * (k - 2) + c
                    if fixed_below(u, 2):
                        pe.wait_ge(sem("xlo"), past("lin", "xlo") + NT)
                    if not fixed_below(u, 2):
                        pe.wait_ge(sem("acc_done"), u - 1)
                    for n, (l, w) in enumerate(((y_hi, ow_hi), (y_hi, ow_lo), (y_lo, ow_hi))):
                        mm = pe.matmul(OUTP[c % 2][:, :], l[:, c_(c)], w[:, :], start=(n == 0), stop=(n == 2))
                    mm.then_inc(sem("out_ps"), 1)
                if has0:
                    project_kv(1, h, g, output if has2 else turned(k, VV))
                elif has2:
                    for c in range(CH):
                        output(c)
                if has1:
                    if has0:
                        pe.wait_ge(sem("act_q"), k + 1)
                    else:
                        pe.wait_ge(sem("act_g"), k - 1)
                    project(GG, h1, g1)
                    pe.wait_ge(sem("masked"), m + 1)
                    pe.wait_ge(sem("qd_ready"), m + 1)
                    pe.wait_ge(sem("kv_ready"), m + 1)
                    if has2:
                        pe.wait_ge(sem("at_ready"), m)
                    for c in range(CH):
                        state = (c - 1) % CH if c or g1 % 2 else None
                        pe.matmul(ATP[:, c_(c)], kvt[:, r1, c, 1, :], sc[:, c_(c)], start=True, stop=state is None)
                        if state is not None:
                            mm = pe.matmul(ATP[:, c_(c)], kvs[:, state, :], qd[:, c_(c)], start=False, stop=True)
                    mm.then_inc(sem("at_ps"), 1)

            heads(pe, None, 0, slot)
            pe.wait_ge(sem("sq_done"), SLOTS)
            pe.wait_ge(sem("act_g"), SLOTS)
            for t in range(NT):
                mm = pe.matmul(bank[0][:, 2 * t:2 * t + 2], sq[:, t * P:(t + 1) * P], ones[:, 0:2],
                               start=True, stop=True)
            mm.then_inc(sem("ss_ps"), 1)

        def lin_act(act):
            stats_act(act, "lin")

            def hi(t):
                act.wait_ge(sem("xt"), past("lin", "xt") + t + 1)
                act.activation(xa_hi[:, :, t * P:(t + 1) * P],
                               OUTP[t % 2].rearrange("p (k n) -> p k n", k=KC), ACT.Copy).then_inc(sem("xhi"), 1)
            for t in FIRST_TILES:
                hi(t)

            def whi(kind, n, h):
                if h is not None:
                    over, times = {4: ("out_ps", 4 * G), KK: ("proj_kv", 2 * G), VV: ("proj_kv", 2 * G)}.get(
                        kind, (f"proj_{KINDS[kind]}", G))
                    act.wait_ge(sem(over), times * (h + 1))
                if kind == 4:
                    act.wait_ge(sem("ow_loaded"), 16 * (n + 1))
                    act.activation(ow_hi[:, :], ow_raw[:, :], ACT.Copy).then_inc(sem("w_hi_o"), 1)
                else:
                    act.wait_ge(sem("w_loaded"), 16 * (n + 1))
                    act.activation(w_hi[:, kind, :, :], w_raw[:, kind, :, :], ACT.Copy)\
                       .then_inc(sem(f"w_hi_{KINDS[kind]}"), 1)

            for kind in range(5):
                whi(kind, 0, None)

            def slot(k, h, g, h1, h2, has1, has2, has0):
                r, r1 = g % 2, (g + 1) % 2
                m = k - 1
                more = has0 and not (type(h) is int and h == LH)
                if has0:
                    for t in tiles_in(k, QQ):
                        hi(t)
                    act.wait_ge(sem("proj_q"), k + 1)
                    if has2:
                        act.wait_ge(sem("at_ps"), k - 1)
                        act.wait_ge(sem("qd_ready"), k - 1)
                    act.activation(qT[:, r, :], PJ[:, :], ACT.Silu).then_inc(sem("act_q"), 1)
                    if g == 3:
                        whi(QQ, h + 1, h)
                if has1:
                    act.wait_ge(sem("tr_k"), m + 1)
                    if has2:
                        act.wait_ge(sem("score_ps"), m)
                    act.activation(kT[:, :], TS[:, :], ACT.Copy).then_inc(sem("kT_ready"), 1)
                if has0:
                    for half, kind in ((0, KK), (1, VV)):
                        for t in tiles_in(k, kind):
                            hi(t)
                        act.wait_ge(sem("proj_kv"), 2 * k + (half + 1))
                        act.activation(kvt[:, r, 2 * half:2 * half + 2, :, :],
                                       PKV[half].rearrange("p (c a n) -> p c a n", c=2, a=2), ACT.Silu)\
                           .then_inc(sem("act_kv"), 1)
                    if g == 3:
                        whi(KK, h + 1, h)
                        whi(VV, h + 1, h)
                if has1:
                    act.wait_ge(sem("proj_g"), m + 1)
                    if has2:
                        act.wait_ge(sem("y1_ready"), m)
                    act.activation(gate[:, :], PJ[:, :], ACT.Tanh, scale=0.5).then_inc(sem("act_g"), 1)
                    if g == 0 and has0:
                        whi(GG, h, h - 1)
                    act.wait_ge(sem("at_ps"), m + 1)
                    if has2:
                        act.wait_ge(sem("sq_done"), m)
                    act.activation(at[:, :], ATP[:, :], ACT.Copy).then_inc(sem("at_ready"), 1)
                    if has2:
                        act.wait_ge(sem("out_ps"), 4 * m)
                        if g == 1 and has0:
                            whi(4, h, h - 1)
                    act.wait_ge(sem("y1_ready"), m + 1)
                    act.activation(y_hi[:, :], y1[:, :], ACT.Copy, scale=nwh[:, bass.ds(h1, 1)])\
                       .then_inc(sem("y_hi_ready"), 1)

            heads(act, None, 0, slot)
            act.wait_ge(sem("ss_ve"), 1)
            act.activation(rnorm[:, :], rnorm[:, :], ACT.Sqrt).then_inc(sem("ss_sd"), 1)

        def lin_dve(dve, chain):
            stats_dve(dve, chain, "lin")

            def normalise(t):
                dve.wait_ge(sem("xhi"), past("lin", "xhi") + t + 1)
                dve.tensor_tensor(xa_lo[:, :, t * P:(t + 1) * P], OUTP[t % 2].rearrange("p (k n) -> p k n", k=KC),
                                  xa_hi[:, :, t * P:(t + 1) * P].bitcast(F32), ALU.subtract)\
                   .then_inc(sem("xlo"), 1)
                if t + 2 < NT:
                    norm_dve(dve, "lin", t + 2, t % 2, False, l_xn)
            for t in (0, 1):
                norm_dve(dve, "lin", t, t, True, l_xn)
            for t in FIRST_TILES:
                normalise(t)
            dve.wait_ge(sem("lin_consts"), 48)
            chain(dve.tensor_scalar(nwh[:, :], nwh[:, :], 0.5, None, ALU.mult))

            def slot(k, h, g, h1, h2, has1, has2, has0):
                r1 = (g + 1) % 2
                m, g1 = k - 1, (g - 1) % G
                for t in tiles_in(k, QQ) + tiles_in(k, KK):
                    normalise(t)
                if has1:
                    dve.wait_ge(sem("act_kv"), 2 * (m + 1))
                    if has2:
                        dve.wait_ge(sem("kv_ps"), m)
                        dve.wait_ge(sem("at_ps"), m)
                    dve.tensor_scalar(ktok[:, :].rearrange("p (c n) -> p c n", c=CH), kvt[:, r1, :, 0, :],
                                      kdec[:, bass.ds(h1, 1)], None, ALU.mult).then_inc(sem("ktok_ready"), 1)
                    dve.wait_ge(sem("tab_loaded"), 16 * (h1 + 1))
                    dve.wait_ge(sem("act_q"), m + 1)
                    dve.tensor_tensor(qd[:, :].rearrange("p (c n) -> p c n", c=CH),
                                      qT[:, r1, :].rearrange("p (c n) -> p c n", c=CH),
                                      dt_tab[:, 1, :].unsqueeze(1).to_broadcast([P, CH, P]), ALU.mult)\
                       .then_inc(sem("qd_ready"), 1)
                    dve.wait_ge(sem("kv_ps"), m + 1)
                    for c in range(CH - g1 % 2):
                        if g1 % 2 == 0 and c == 0:
                            chain(dve.tensor_copy(kvs[:, 0, :], KVP[:, c_(0)]))
                        else:
                            chain(dve.scalar_tensor_tensor(kvs[:, c, :], kvs[:, (c - 1) % CH, :],
                                                           bdec[:, bass.ds(h1, 1)], KVP[:, c_(c)],
                                                           ALU.mult, ALU.add))
                    dve.sem_inc(sem("kv_ready"), 1)
                    dve.wait_ge(sem("score_ps"), m + 1)
                    dve.tensor_tensor(sc[:, :].rearrange("p (c n) -> p c n", c=CH),
                                      TS[:, :].rearrange("p (c n) -> p c n", c=CH),
                                      dt_tab[:, 0, :].unsqueeze(1).to_broadcast([P, CH, P]), ALU.mult)\
                       .then_inc(sem("masked"), 1)
                for t in tiles_in(k, VV):
                    normalise(t)
                if has2:
                    if fixed_below(k, 3):
                        dve.wait_ge(sem("acc_zero"), 1)
                    for c in range(CH):
                        u = 4 * (k - 2) + c
                        tt = ((g - 2) % G) * CH + c
                        dve.wait_ge(sem("out_ps"), u + 1)
                        dve.tensor_tensor(x[:, tt, :], OUTP[c % 2][:, :], x[:, tt, :], ALU.add)\
                           .then_inc(sem("acc_done"), 1)
                if has1:
                    dve.wait_ge(sem("act_g"), m + 1)
                    dve.wait_ge(sem("at_ready"), m + 1)
                    if has2:
                        dve.wait_ge(sem("y_hi_ready"), m)
                    dve.scalar_tensor_tensor(y1[:, :], gate[:, :], 1.0, at[:, :], ALU.add, ALU.mult)\
                       .then_inc(sem("y1_ready"), 1)
                    dve.wait_ge(sem("y_hi_ready"), m + 1)
                    dve.scalar_tensor_tensor(y_lo[:, :], y1[:, :], nwh[:, bass.ds(h1, 1)],
                                             y_hi[:, :].bitcast(F32), ALU.mult, ALU.subtract)\
                       .then_inc(sem("y_lo_ready"), 1)

            heads(dve, chain, 14, slot)
            dve.wait_ge(sem("acc_done"), 4 * SLOTS)
            dve.wait_ge(sem("ss_ps"), 1)
            dve.tensor_scalar(rnorm[:, :], bank[0][:, 0:2 * NT].rearrange("p (t c) -> p t c", c=2)[:, :, 0],
                              1.0 / (LH * P), EPS, ALU.mult, ALU.add).then_inc(sem("ss_ve"), 1)
            dve.wait_ge(sem("ss_sd"), 1)
            chain(dve.reciprocal(rnorm[:, :], rnorm[:, :]))

            for n in range(XL):
                dve.wait_ge(sem(f"x_back{n}"), 16)
            with dve.Fori(0, G) as g:
                for c in range(CH):
                    t = CH * g + c
                    dve.scalar_tensor_tensor(x[:, t, :], x[:, t, :], rnorm[:, bass.ds(t, 1)], x_in[:, t, :],
                                             ALU.mult, ALU.add).then_inc(sem("lin_x"), 1)
                for c in range(CH):
                    dve.wait_ge(sem("lin_x"), CH * g + (c + 1))
                    bn_dve(dve, "ffn_b", CH * g + c)
            dve.wait_ge(sem("lin_x"), NT)
            dve.sem_inc(phase_done["lin"], 1)

        def lin_pool(pool, chain):
            def wlo(kind, n):
                pool.wait_ge(sem(f"w_hi_{KINDS[kind]}"), n + 1)
                if kind == 4:
                    pool.tensor_tensor(ow_lo[:, :], ow_raw[:, :], ow_hi[:, :].bitcast(F32), ALU.subtract)\
                        .then_inc(sem("w_lo_o"), 1)
                else:
                    pool.tensor_tensor(w_lo[:, kind, :, :], w_raw[:, kind, :, :],
                                       w_hi[:, kind, :, :].bitcast(F32), ALU.subtract)\
                        .then_inc(sem(f"w_lo_{KINDS[kind]}"), 1)
            for kind in range(5):
                wlo(kind, 0)
            chain(pool.memset(sq[:, :], 0.0))

            def slot(k, h, g, h1, h2, has1, has2, has0):
                m, g1 = k - 1, (g - 1) % G
                if fixed_below(k, 3) and has2:
                    pool.wait_ge(sem("x_kept"), 16)
                    pool.wait_ge(sem("xn"), past("lin", "xn") + NT)
                    pool.memset(x[:, :, :], 0.0).then_inc(sem("acc_zero"), 1)
                if has0 and g == 3:
                    for kind in (QQ, KK, VV):
                        wlo(kind, h + 1)
                if has1:
                    if g == 0 and has0:
                        wlo(GG, h)
                    if g == 1 and has0 and has2:
                        wlo(4, h)
                    pool.wait_ge(sem("at_ready"), m + 1)
                    chain(pool.tensor_tensor(at2[:, :], at[:, :], at[:, :], ALU.mult))
                    part = sq[:, g1 * GT:(g1 + 1) * GT]
                    chain(pool.tensor_tensor(part, part, at2[:, :], ALU.add))
                    pool.wait_ge(sem("y1_ready"), m + 1)
                    pool.sem_inc(sem("sq_done"), 1)

            heads(pool, chain, 8, slot)

        def lin_sync(sp):
            sp.dma_start(kdec[:, :], a["kdec"]).then_inc(sem("lin_consts"), 16)
            sp.dma_start(bdec[:, :], a["bdec"]).then_inc(sem("lin_consts"), 16)
            sp.dma_start(nwh[:, :], a["norm_w"]).then_inc(sem("lin_consts"), 16)
            sp.dma_start(w_raw[:, :, :, :], a["w_heads"][0]).then_inc(sem("w_loaded"), 16)
            sp.dma_start(ow_raw[:, :], a["ow_heads"][0]).then_inc(sem("ow_loaded"), 16)
            sp.dma_start(dt_tab[:, :, :], a["decay"][0]).then_inc(sem("tab_loaded"), 16)
            sp.dma_start(x_dram.rearrange("t p n -> p t n"), x[:, :, :]).then_inc(sem("x_kept"), 16)

            def head(n):
                sp.wait_ge(sem("w_lo_g"), n)
                sp.dma_start(w_raw[:, :, :, :], a["w_heads"][n]).then_inc(sem("w_loaded"), 16)
                sp.wait_ge(sem("w_lo_o"), n)
                sp.dma_start(ow_raw[:, :], a["ow_heads"][n]).then_inc(sem("ow_loaded"), 16)
                sp.wait_ge(sem("masked"), 4 * n)
                sp.wait_ge(sem("qd_ready"), 4 * n)
                sp.dma_start(dt_tab[:, :, :], a["decay"][n])\
                  .then_inc(sem("tab_loaded"), 16)
            with sp.Fori(1, LH) as n:
                head(n)
            sp.wait_ge(sem("w_lo_g"), LH)
            sp.dma_start(w_raw[:, :, :, :], a["w_heads"][0]).then_inc(sem("w_loaded"), 16)

            sp.wait_ge(sem("proj_g"), SLOTS)
            for n in range(XL):
                w = NT // XL
                sp.dma_start(x_in[:, n * w:(n + 1) * w, :],
                             x_dram[n * w:(n + 1) * w].rearrange("t p n -> p t n")).then_inc(sem(f"x_back{n}"), 16)

        def mem_prep_sync(sp):
            for dst, src in ((small[0:BOT, 0:RDIM], a["wr_t"]), (small[0:RDIM, 64:64 + BOT], a["wr"]),
                             (small2[0:BOT, P:2 * P], a["keys_t"]), (stage[0:BOT, WQM[0]:WQM[1]], a["wq_mem"]),
                             (stage[:, WVD[0]:WVD[1]], a["wvd_t"]), (stage[:, VAL[0]:VAL[1]], a["values_t"]),
                             (stage[0:VB, WVU[0]:WVU[1]], a["wvu_t"]), (kc(WU1), a["wu1_t"]),
                             (brow[:, :], a["bias_mem"]), (wu2[:, :], a["wu2"]), (sc3[:, 0:3], a["scalars"])):
                sp.dma_start(dst, src).then_inc(sem("mem_loaded"), 16)
            for dst, src in ((kc(WQKV), a["wqkv"]), (bqkv[:, :], a["b_qkv"]), (rope[:, :, :, :], a["rope"])):
                sp.dma_start(dst, src).then_inc(sem("att_loaded"), 16)

        MEM_LOADED, ATT_LOADED = 16 * 11, 16 * 3

        def mem_prep_pe(pe):
            pe.wait_ge(sem("mem_loaded"), MEM_LOADED)
            pe.matmul(bank[0][0:RDIM, 0:NSLOT], small[0:BOT, 0:RDIM], small2[0:BOT, P:2 * P], start=True, stop=True)\
              .then_inc(sem("mp_rk"), 1)
            for k in range(KC):
                mm = pe.matmul(bank[1][0:VB, 0:NSLOT], stage[:, WVD[0] + k * VB:WVD[0] + (k + 1) * VB],
                               stage[:, VAL[0] + k * P:VAL[0] + (k + 1) * P], start=(k == 0), stop=(k == KC - 1))
            mm.then_inc(sem("mp_v2"), 1)
            pe.wait_ge(sem("mp_rk_sb"), 1)
            pe.matmul(bank[2][0:BOT, 0:NSLOT], small[0:RDIM, 64:64 + BOT], small[0:RDIM, P:2 * P], start=True, stop=True)\
              .then_inc(sem("mp_m"), 1)
            pe.wait_ge(sem("mp_v2_sb"), 1)
            pe.matmul(bank[3][:, :], v2t[0:VB, :], stage[0:VB, WVU[0]:WVU[1]], start=True, stop=True)\
              .then_inc(sem("mp_v3"), 1)
            pe.wait_ge(sem("mp_m_sb"), 1)
            for k in range(KC):
                pe.matmul(bank[4 + k][:, 0:2 * NSLOT], stage[0:BOT, WQM[0] + k * P:WQM[0] + (k + 1) * P],
                          small2[0:BOT, 0:2 * P], start=True, stop=True).then_inc(sem("mp_w"), 1)

        def mem_prep_act(act):
            act.wait_ge(sem("mp_rk"), 1)
            act.activation(small[0:RDIM, P:2 * P], bank[0][0:RDIM, 0:NSLOT], ACT.Copy).then_inc(sem("mp_rk_sb"), 1)
            act.wait_ge(sem("mp_v2"), 1)
            act.activation(v2t[0:VB, :], bank[1][0:VB, 0:NSLOT], ACT.Copy).then_inc(sem("mp_v2_sb"), 1)
            act.wait_ge(sem("mp_m"), 1)
            act.activation(small2[0:BOT, 0:P], bank[2][0:BOT, 0:NSLOT], ACT.Copy).then_inc(sem("mp_m_sb"), 1)
            act.wait_ge(sem("mp_v3"), 1)
            act.activation(v3[:, :], bank[3][:, :], ACT.Copy).then_inc(sem("mp_v3_sb"), 1)
            for k in range(KC):
                act.wait_ge(sem("mp_w"), k + 1)
                act.activation(kc(W1F)[:, k, 0:P], bank[4 + k][:, 0:P], ACT.Copy, scale=float(1 / np.sqrt(RDIM)))\
                   .then_inc(act_steps, 1)
                act.activation(kc(W1F)[:, k, P:2 * P], bank[4 + k][:, P:2 * P], ACT.Copy, scale=float(1 / np.sqrt(BOT)))\
                   .then_inc(act_steps, 1)
            act.wait_ge(act_steps, 2 * KC)
            for n, (raw, hi, _) in enumerate(MEM_SPLITS):
                act.activation(hi, raw, ACT.Copy).then_inc(sem("mem_hi"), 1)

        def split_att_act(act):
            act.wait_ge(sem("att_loaded"), ATT_LOADED)
            for raw, hi, _ in ATT_SPLITS:
                act.activation(hi, raw, ACT.Copy).then_inc(sem("att_hi"), 1)

        def split_lo_pool(pool, splits, name):
            for n, (raw, hi, lo) in enumerate(splits):
                pool.wait_ge(sem(f"{name}_hi"), n + 1)
                pool.tensor_tensor(lo, raw, hi.bitcast(F32), ALU.subtract).then_inc(sem(f"{name}_lo"), 1)

        MEM_A = [psum[:, 2:4, :], psum[:, 4:6, :]]
        MEM_Y = [bank[6], bank[7]]

        def mem_pe(pe, phase):
            pe.wait_ge(sem("ls"), past(phase, "ls") + 1)
            pe.matmul(MEM_Y[0][:, 0:2], ones[:, :], lsum[:, 0:2], start=True, stop=True).then_inc(sem("lm"), 1)

            def pair(q, r):
                if exists(q - 1, NP):
                    pe.wait_ge(sem("pr"), past(phase, "pr") + q)
                    if not fixed_below(q, 3):
                        pe.wait_ge(sem("prt"), past(phase, "prt") + q - 2)
                    for s in (0, 1):
                        mm = pe.transpose(MEM_A[1 - r][:, s, 384:512], pr[:, 1 - r, s, :], ident[:, :])
                    mm.then_inc(sem("pt"), 1)
                if exists(q + 1, NP):
                    transposes_pe(pe, phase, q + 1)
                if exists(q - 1, NP):
                    pe.wait_ge(sem("prt"), past(phase, "prt") + q)
                    if fixed_below(q, 2):
                        pe.wait_ge(sem("nv"), past(phase, "nv") + 1)
                    for s in (0, 1):
                        if not fixed_below(q, 2):
                            pe.wait_ge(sem("x"), past(phase, "x") + 2 * q + (s - 3))
                        pe.matmul(MEM_Y[s][:, :], prt[:, 1 - r, s, :], v3[:, :], start=True, stop=True)\
                          .then_inc(sem("y"), 1)
                if exists(q + 1, NP):
                    pe.wait_ge(sem("xlo"), past(phase, "xlo") + 2 * q + 4)
                    if not fixed_below(q, 1):
                        pe.wait_ge(sem("read"), past(phase, "read") + q)
                    for s in (0, 1):
                        mm = product_pe(pe, MEM_A[1 - r][:, s, 0:384], s, w1_hi, w1_lo, 0, 384,
                                        XT_HI[1 - r], XT_LO[1 - r])
                    mm.then_inc(sem("used"), 1)
            pairs(pe, None, 0, pair)

        def mem_act(act, phase):
            act.wait_ge(sem("vh"), past(phase, "vh") + 1)
            act.activation(lv[:, :], lv[:, :], ACT.Ln, bias=1.0, accum_out=lsum[:, 0:1]).then_inc(sem("lv"), 1)

            def pair(q, r):
                if exists(q - 1, NP):
                    act.wait_ge(sem("pt"), past(phase, "pt") + q)
                    if not fixed_below(q, 3):
                        act.wait_ge(sem("y"), past(phase, "y") + 2 * (q - 2))
                    act.activation(prt[:, 1 - r, :, :], MEM_A[1 - r][:, :, 384:512], ACT.Copy).then_inc(sem("prt"), 1)
                if exists(q + 1, NP):
                    for s in (0, 1):
                        hi_act(act, phase, 2 * (q + 1) + s, s, None if fixed_below(q, 1) else q, XTB[s], XT_HI[1 - r])
                if exists(q + 2, NP):
                    norms_act(act, q + 2)
                if exists(q - 1, NP):
                    act.wait_ge(sem("learned"), past(phase, "learned") + q)
                    act.activation(th1[:, 1 - r, :], lrn[:, 1 - r, :], ACT.Tanh, scale=0.5).then_inc(sem("t1"), 1)
                    for s in (0, 1):
                        t = 2 * (q - 1) + s
                        if not fixed_below(q, 2):
                            act.wait_ge(sem("x"), past(phase, "x") + t - 1)
                        act.activation(xb[:, s, :], x[:, t, :], ACT.Identity, scale=hr[:, bass.ds(t, 1)],
                                       bias=hn[:, bass.ds(t, 1)]).then_inc(sem("xb"), 1)
                    act.wait_ge(sem("u"), past(phase, "u") + q)
                    act.activation(th2[:, 1 - r, :], uu[:, 1 - r, :], ACT.Tanh, scale=0.5).then_inc(sem("t2"), 1)
                if exists(q, NP):
                    act.wait_ge(sem("cubic"), past(phase, "cubic") + q + 1)
                    act.activation(gt[:, r, :, :], gc[:, r, :, :], ACT.Tanh, scale=GELU_SCALE).then_inc(sem("gt"), 1)
                    act.wait_ge(sem("am"), past(phase, "am") + q + 1)
                    if not fixed_below(q, 2):
                        act.wait_ge(sem("pt"), past(phase, "pt") + q - 1)
                    for s in (0, 1):
                        ins = act.activation(pr[:, r, s, :], rg[:, r, s, P:2 * P], ACT.Exp, bias=nmx[:, r, s:s + 1],
                                             accum_out=psm[:, r, s:s + 1])
                    ins.then_inc(sem("pr"), 1)
            first_norms_act(act, phase)
            pairs(act, None, 0, pair)

        def mem_pool(pool, chain, phase):
            def cubic(q, r):
                pool.wait_ge(sem("read"), past(phase, "read") + q + 1)
                if not fixed_below(q, 2):
                    pool.wait_ge(sem("gt"), past(phase, "gt") + q - 1)
                gu = rg[:, r, :, 2 * P:3 * P]
                chain(pool.tensor_tensor(gc[:, r, :, :], gu, gu, ALU.mult))
                apart(pool, sem("apart_pool"))
                chain(pool.tensor_scalar(gc[:, r, :, :], gc[:, r, :, :], 0.044715, 1.0, ALU.mult, ALU.add))
                pool.tensor_tensor(gc[:, r, :, :], gc[:, r, :, :], gu, ALU.mult).then_inc(sem("cubic"), 1)

            def gelu(q, r):
                pool.wait_ge(sem("gt"), past(phase, "gt") + q + 1)
                if not fixed_below(q, 1):
                    pool.wait_ge(sem("learned"), past(phase, "learned") + q)
                gu = rg[:, r, :, 2 * P:3 * P]
                chain(pool.tensor_tensor(gg[:, :, :], gt[:, r, :, :], gu, ALU.mult))
                chain(pool.tensor_tensor(gg[:, :, :], gg[:, :, :], gu, ALU.add))
                pool.tensor_tensor(gg[:, :, :], gg[:, :, :], wu2[:, :].unsqueeze(1).to_broadcast([P, 2, P]),
                                   ALU.mult).then_inc(sem("gelu"), 1)

            def gate_in(q, r):
                pool.wait_ge(sem("t1"), past(phase, "t1") + q + 1)
                apart(pool, sem("apart_pool"))
                chain(pool.tensor_scalar(gu_in[:, :], th1[:, r, :], 1.25, 1.25, ALU.mult, ALU.add))
                chain(pool.tensor_tensor(gu_in[:, :], gu_in[:, :], nv[:, bass.ds(2 * q, 2)], ALU.add))
                for s1, s2, op0, op1 in ((0.0, 5.0, ALU.max, ALU.min), (-0.5, 1.0 / 1.5, ALU.add, ALU.mult),
                                         (0.0, 1.0, ALU.max, ALU.min)):
                    apart(pool, sem("apart_pool"))
                    chain(pool.tensor_scalar(gu_in[:, :], gu_in[:, :], s1, s2, op0, op1))
                apart(pool, sem("apart_pool"))
                pool.tensor_scalar(uu[:, r, :], gu_in[:, :], sc3[:, 1:2], sc3[:, 2:3], ALU.mult, ALU.add)\
                    .then_inc(sem("u"), 1)

            def pair(q, r):
                if exists(q - 1, NP):
                    gelu(q - 1, 1 - r)
                    gate_in(q - 1, 1 - r)
                if exists(q, NP):
                    cubic(q, r)
            pool.wait_ge(sem("nv"), past(phase, "nv") + 1)
            pairs(pool, chain, 2 * 9, pair)

        def mem_dve(dve, chain, phase):
            chain(dve.tensor_tensor(lv[:, :], rstd[:, :], rstd[:, :], ALU.mult))
            dve.scalar_tensor_tensor(lv[:, :], ve[:, :], -EPS, lv[:, :], ALU.add, ALU.mult).then_inc(sem("vh"), 1)
            chain(dve.memset(lsum[:, 1:2], 0.0))
            chain(dve.tensor_scalar(hr[:, :], rstd[:, :], 0.5, 1.0, ALU.mult, ALU.add))
            chain(dve.tensor_scalar(hn[:, :], nmr[:, :], 0.5, None, ALU.mult))
            dve.wait_ge(sem("lv"), past(phase, "lv") + 1)
            dve.sem_inc(sem("ls"), 1)
            dve.wait_ge(sem("lm"), past(phase, "lm") + 1)
            chain(dve.tensor_scalar(mean1[:, 0:1], MEM_Y[0][:, 0:1], 1.0 / T, 1e-6, ALU.mult, ALU.add))
            chain(dve.reciprocal(mean1[:, 1:2], mean1[:, 0:1]))
            dve.tensor_scalar(nv[:, :], lv[:, :], mean1[:, 1:2], 0.5, ALU.mult, ALU.mult).then_inc(sem("nv"), 1)
            dve.wait_ge(sem("nv"), past(phase, "nv") + 1)

            def learned(q, r):
                dve.wait_ge(sem("gelu"), past(phase, "gelu") + q + 1)
                chain(dve.tensor_reduce(gm[:, 0, :], gg[:, :, :], AX, ALU.add))
                dve.tensor_scalar(lrn[:, r, :], gm[:, 0, :], sc3[:, 0:1], None, ALU.add).then_inc(sem("learned"), 1)

            def route(q, r):
                dve.wait_ge(sem("used"), past(phase, "used") + q + 1)
                if not fixed_below(q, 2):
                    dve.wait_ge(sem("pr"), past(phase, "pr") + q - 1)
                    dve.wait_ge(sem("gelu"), past(phase, "gelu") + q - 1)
                dve.tensor_tensor(rg[:, r, :, :], MEM_A[r][:, :, 0:384], brow[:, :].unsqueeze(1).to_broadcast([P, 2, 384]),
                                  ALU.add).then_inc(sem("read"), 1)
                dve.wait_ge(sem("read"), past(phase, "read") + q + 1)
                apart(dve, sem("apart_dve"))
                for s, done in ((0, chain.beside), (1, chain)):
                    done(dve.max(mtop[:, s, :], rg[:, r, s, 0:P]))
                apart(dve, sem("apart_dve"))
                for s, done in ((0, chain.beside), (1, chain)):
                    done(dve.match_replace(out=rt2[:, s, :], in_to_replace=mtop[:, s, :], in_values=rg[:, r, s, 0:P],
                                           imm_value=TAKEN))
                chain(dve.tensor_scalar(rt2[:, :, :], rt2[:, :, :], TAKEN_LINE, LOW, ALU.is_gt, ALU.mult))
                am = rg[:, r, :, P:2 * P]
                chain(dve.tensor_tensor(am, am, rt2[:, :, :], ALU.add))
                dve.tensor_reduce(nmx[:, r, :], am, AX, ALU.max, negate=True).then_inc(sem("am"), 1)

            def add(q, r):
                dve.wait_ge(sem("t2"), past(phase, "t2") + q + 1)
                chain(dve.tensor_scalar(gm[:, 1, :], th2[:, r, :], 0.5, 0.5, ALU.mult, ALU.add))
                chain(dve.tensor_scalar(gm[:, 2, :], gm[:, 1, :], 0.05, None, ALU.is_ge))
                chain(dve.reciprocal(gm[:, 3, :], psm[:, r, :]))
                chain(dve.scalar_tensor_tensor(gm[:, 2, :], gm[:, 1, :], 0.5, gm[:, 2, :], ALU.mult, ALU.mult))
                chain(dve.tensor_tensor(gm[:, 2, :], gm[:, 2, :], gm[:, 3, :], ALU.mult))
                for s in (0, 1):
                    t = 2 * q + s
                    dve.wait_ge(sem("y"), past(phase, "y") + t + 1)
                    dve.wait_ge(sem("xb"), past(phase, "xb") + t + 1)
                    dve.scalar_tensor_tensor(x[:, t, :], MEM_Y[s][:, :], gm[:, 2, s:s + 1], xb[:, s, :],
                                             ALU.mult, ALU.add).then_inc(sem("x"), 1)
                if phase == "mem_a":
                    for s in (0, 1):
                        dve.wait_ge(sem("x"), past(phase, "x") + 2 * q + (s + 1))
                        bn_dve(dve, "att", 2 * q + s)

            def pair(q, r):
                if exists(q + 1, NP):
                    los_dve(dve, phase, q + 1, 1 - r)
                if exists(q - 1, NP):
                    learned(q - 1, 1 - r)
                if exists(q, NP):
                    route(q, r)
                if exists(q - 1, NP):
                    add(q - 1, 1 - r)
            pairs(dve, chain, 2 * 12, pair)
            dve.wait_ge(sem("x"), past(phase, "x") + NT)
            dve.sem_inc(phase_done[phase], 1)

        PRJ_XT = [bank[0], bank[1]]
        PRJ_Q = [bank[2], bank[3]]
        PRJ_KV = [bank[4], bank[5]]

        def qkv_pe(pe):
            phase = "att"
            transpose_pe(pe, phase, 0, 0, True, PRJ_XT[0])
            pe.wait_ge(sem("att_lo"), KC)

            def tile(t, s, first, last):
                if not last:
                    transpose_pe(pe, phase, t + 1, 1 - s, first and s == 0, PRJ_XT[1 - s])
                pe.wait_ge(sem("xlo"), past("att", "xlo") + t + 1)
                if not first:
                    pe.wait_ge(sem("att_biased"), t - 1)
                product_pe(pe, PRJ_Q[s][:, :], s, wq_hi, wq_lo, 0, 512)
                product_pe(pe, PRJ_KV[s][:, 0:256], s, wq_hi, wq_lo, 512, 768).then_inc(sem("used"), 1)
            tiles(pe, None, 0, tile)

        def qkv_act(act):
            first_norms_act(act, "att")
            hi_act(act, "att", 0, 0, None, PRJ_XT[0])

            def tile(t, s, first, last):
                if not last:
                    hi_act(act, "att", t + 1, 1 - s, None if first and s == 0 else t, PRJ_XT[1 - s])
                if exists(t + 2, NT):
                    norm_act(act, t + 2, s)
            tiles(act, None, 0, tile)

        def qkv_pool(pool):
            def tile(t, s, first, last, pos):
                pool.wait_ge(sem("att_biased"), t + 1)
                if not first:
                    pool.wait_ge(sem("att_qk"), t - 1)
                sin = rope[:, pos, 1, :]
                for half in (0, 1):
                    lo_, hi_ = half * (HD // 2), (1 - half) * (HD // 2)
                    ins = pool.tensor_tensor(rot[:, s, :, lo_:lo_ + HD // 2], qkb[:, s, :, hi_:hi_ + HD // 2],
                                             sin[:, lo_:lo_ + HD // 2].unsqueeze(1).to_broadcast([P, QK, HD // 2]),
                                             ALU.mult)
                ins.then_inc(sem("att_rot"), 1)
            by_sequence(pool, tile)

        def by_sequence(eng, tile):
            for b in range(B):
                for s in (0, 1):
                    tile(b * TB + s, s, b == 0, False, s)
                with eng.Fori(1, TB // 2) as j:
                    for s in (0, 1):
                        tile(b * TB + 2 * j + s, s, False, False, 2 * j + s)

        def qkv_dve(dve, chain):
            dve.wait_ge(sem("att_loaded"), 32)
            lo_dve(dve, "att", 0, 0, PRJ_XT[0])

            def rotated(t, s):
                dve.wait_ge(sem("att_rot"), t + 1)
                dve.wait_ge(sem("att_cos"), t + 1)
                dve.tensor_tensor(qk[:, t, :, :], qk[:, t, :, :], rot[:, s, :, :], ALU.add).then_inc(sem("att_qk"), 1)

            def tile(t, s, first, last, pos):
                if not last:
                    lo_dve(dve, "att", t + 1, 1 - s, PRJ_XT[1 - s])
                dve.wait_ge(sem("used"), past("att", "used") + t + 1)
                if not first:
                    dve.wait_ge(sem("att_rot"), t - 1)
                    dve.wait_ge(sem("att_cos"), t - 1)
                dve.tensor_tensor(vv[:, t, :, :], PRJ_KV[s][:, P:2 * P].rearrange("p (h d) -> p h d", d=HD),
                                  bqkv[:, 640:768].rearrange("p (h d) -> p h d", d=HD), ALU.add)
                dve.tensor_tensor(qkb[:, s, 0:H, :], PRJ_Q[s][:, :].rearrange("p (h d) -> p h d", d=HD),
                                  bqkv[:, 0:512].rearrange("p (h d) -> p h d", d=HD), ALU.add)
                dve.tensor_tensor(qkb[:, s, H:QK, :], PRJ_KV[s][:, 0:P].rearrange("p (h d) -> p h d", d=HD),
                                  bqkv[:, 512:640].rearrange("p (h d) -> p h d", d=HD), ALU.add)\
                   .then_inc(sem("att_biased"), 1)
                if not (first and s == 0):
                    rotated(t - 1, 1 - s)
                dve.wait_ge(sem("att_biased"), t + 1)
                dve.tensor_tensor(qk[:, t, :, :], qkb[:, s, :, :],
                                  rope[:, pos, 0, :].unsqueeze(1).to_broadcast([P, QK, HD]), ALU.mult)\
                   .then_inc(sem("att_cos"), 1)

            for b in range(B):
                for s in (0, 1):
                    tile(b * TB + s, s, b == 0, False, s)
                with dve.Fori(1, TB // 2 - 1) as j:
                    for s in (0, 1):
                        tile(b * TB + 2 * j + s, s, False, False, 2 * j + s)
                for s in (0, 1):
                    tile(b * TB + TB - 2 + s, s, False, b == B - 1 and s == 1, TB - 2 + s)
            rotated(NT - 1, 1)
            dve.wait_ge(sem("att_qk"), NT)
            dve.memset(kst[KS:KS + 2, :, :], 1.0).then_inc(sem("att_preset"), 1)
            dve.memset(vst[:, :, :, :], 0.0).then_inc(sem("att_preset"), 1)
            dve.wait_ge(sem("att_preset"), 2)
            dve.memset(vst[:, :, :, HD:HD + 1], 1.0).then_inc(sem("att_preset"), 1)
            dve.wait_ge(sem("att_preset"), 3)
            dve.sem_inc(sem("att_qkv"), 1)

        SB = [psum[:, 0:2, :], psum[:, 2:4, :]]
        ST = [bank[4], bank[5]]
        PV = bank[6]
        TR = bank[7]
        TRB = TR[:, :].bitcast(BF16)
        SPAN = 2 * TB * 2
        UNITS = 4 * KV
        TURNS = 5
        PAIR = 2

        def at_step(st, offset, every):
            return (st - offset) // every if (st - offset) % every == 0 else None

        def stacks_done(kv, d, j):
            return 10 * kv + TURNS * (d // 2) + 2 + 2 * (d % 2) + j

        def walk(chain, eng, steps, step):
            for st in range(-15, SPAN):
                step(0, st)

            def head(kv):
                for st in range(SPAN):
                    step(kv, st)
            looped([chain] if chain else [], eng, 1, KV - 1, steps, head)
            for st in range(SPAN + 12):
                step(KV - 1, st)

        def att_pe(pe):
            pe.wait_ge(sem("att_qkv"), 1)

            def keys(kv, e):
                n = 2 * kv + e
                if not exists(n, 2 * KV):
                    return
                if not fixed_below(n, 1):
                    pe.wait_ge(sem("stack_sb"), TURNS * n)
                pe.wait_ge(sem("k_stacked"), n + 1)
                for t in range(TB):
                    mm = pe.transpose(TRB[0:KS, t * P:(t + 1) * P], ks[:, t, :], identb[:, :])
                mm.then_inc(sem("stack_ps"), 1)

            def queries(kv, d, j):
                u = 4 * kv + d
                if not exists(u, UNITS):
                    return
                if j == 0 or fixed_below(u, 1):
                    pe.wait_ge(sem("stack_sb"), stacks_done(kv, d, j) - 1)
                else:
                    pe.wait_ge(sem("nmt_ready"), u)
                pe.wait_ge(sem("q_stacked"), u + 1)
                for t in range(TB):
                    mm = pe.transpose(TRB[0:KS, t * P:(t + 1) * P], qs[:, d % 2, t, j, :], identb[:, :])
                mm.then_inc(sem("stack_ps"), 1)

            def score(kv, d, i):
                u = 4 * kv + d
                if not exists(u, UNITS):
                    return
                j, t, hf = i // (2 * TB), i // 2 % TB, i % 2
                if i % (2 * TB) == 0:
                    pe.wait_ge(sem("stack_sb"), stacks_done(kv, d, j))
                if hf == 0 and not fixed_below(16 * u + i // 2, 2):
                    pe.wait_ge(sem("max_read"), 16 * u + (i // 2 - 1))
                mm = pe.matmul(SB[t % 2][:, hf, :], qst[0:KS, d % 4, j, t * P:(t + 1) * P],
                               kst[0:KS, d // 2 % 2, hf * 512:(hf + 1) * 512], start=True, stop=True)
                if hf == 1:
                    mm.then_inc(sem("score2"), 1)

            def maxima(kv, d):
                u = 4 * kv + d
                if not exists(u, UNITS):
                    return
                pe.wait_ge(sem("nm_ready"), u + 1)
                if fixed_below(u, 2):
                    pe.wait_ge(sem("stack_sb"), stacks_done(kv, d + 1, 0))
                else:
                    pe.wait_ge(sem("out_read"), u - 1)
                apart(pe, sem("apart_pe"))
                pe.transpose(TRB[0:2 * PAIR * TB, 0:P], nm[:, :, :].rearrange("p a c -> p (a c)"), identb[:, :])\
                  .then_inc(sem("nm_ps"), 1)

            def values(kv, st):
                g, d, kt = SPAN * kv + st, st // TB, st % TB
                if not exists(g, SPAN * KV):
                    return
                if st % (2 * TB) == 0:
                    pe.wait_ge(sem("v_ready"), 2 * kv + st // (2 * TB) + 1)
                if kt == 0 and not fixed_below(g, 1):
                    pe.wait_ge(sem("pv_sb"), 4 * kv + d)
                pe.wait_ge(sem("probs"), 4 * g + 4)
                for i in range(4):
                    mm = pe.matmul(PV[32 * i:32 * i + 32, :], vst[:, d // 2 % 2, kt, :], pp[:, 4 * (st % 2) + i, :],
                                   start=(kt == 0), stop=(kt == TB - 1), tile_position=(0, 32 * i))
                mm.then_inc(sem("pv_step"), 1)

            def turn_out(kv, d):
                u = 4 * kv + d
                if not exists(u, UNITS):
                    return
                if exists(u + 3, UNITS):
                    pe.wait_ge(sem("stack_sb"), stacks_done(kv, d + 3, 0))
                elif u == UNITS - 3:
                    pe.wait_ge(sem("stack_sb"), TURNS * 2 * KV)
                elif u == UNITS - 2:
                    pe.wait_ge(sem("nmt_ready"), UNITS)
                else:
                    pe.wait_ge(sem("out_read"), UNITS - 1)
                pe.wait_ge(sem("pv_sb"), u + 1)
                for i in range(4):
                    mm = pe.transpose(TR[:, i * P:(i + 1) * P], pvs[:, i * P:(i + 1) * P], ident[:, :])
                mm.then_inc(sem("out_turned"), 1)

            def step(kv, st):
                if (e := at_step(st, -15, 16)) is not None:
                    keys(kv, e)
                g, d, kt = SPAN * kv + st, st // TB, st % TB
                runs = exists(g, SPAN * KV)
                if runs and kt == 0:
                    pe.wait_ge(sem("rows_in"), 32 * (4 * kv + d + 1))
                for i in range(4):
                    if i == 2:
                        for j, offset in ((0, -14), (1, -10)):
                            if (dq := at_step(st, offset, TB)) is not None:
                                queries(kv, dq, j)
                        values(kv, st - 1)
                    if runs:
                        if not fixed_below(4 * g + i, 2):
                            pe.wait_ge(sem("probs"), 4 * g + (i - 1))
                        j, hf = i // 2, i % 2
                        pe.matmul(ST[i % 2][:, :], kst[0:KS + 2, d // 2 % 2, kt * P:(kt + 1) * P],
                                  qst[0:KS + 2, d % 4, j, hf * 512:(hf + 1) * 512], start=True, stop=True)\
                          .then_inc(sem("score1"), 1)
                    for n in ((), (), (0,), (1, 2, 3))[i]:
                        score(kv, (st + 12) // TB, 4 * ((st + 12) % TB) + n)
                if (d := at_step(st, 11, TB)) is not None:
                    turn_out(kv, d)
                if (d := at_step(st, -3, TB)) is not None:
                    maxima(kv, d)

            walk(None, pe, 0, step)

        def att_act(act):
            act.wait_ge(sem("att_qkv"), 1)

            def keys(kv, e):
                n = 2 * kv + e
                if not exists(n, 2 * KV):
                    return
                act.wait_ge(sem("stack_ps"), TURNS * n + 1)
                if not fixed_below(n, 2):
                    act.wait_ge(sem("score1"), 64 * (n - 1))
                act.activation(kst[0:KS, e % 2, :], TRB[0:KS, :], ACT.Copy).then_inc(sem("stack_sb"), 1)

            def queries(kv, d, j):
                u = 4 * kv + d
                if not exists(u, UNITS):
                    return
                act.wait_ge(sem("stack_ps"), stacks_done(kv, d, j))
                if not fixed_below(u, 4):
                    act.wait_ge(sem("score1"), 32 * (u - 3))
                act.activation(qst[0:KS, d % 4, j, :], TRB[0:KS, :], ACT.Copy).then_inc(sem("stack_sb"), 1)

            def step(kv, st):
                g, e = SPAN * kv + st, at_step(st, -15, 16)
                if exists(g, SPAN * KV):
                    for i in range(4):
                        act.wait_ge(sem("score1"), 4 * g + (i + 1))
                        if i == 0 and not fixed_below(g, 2):
                            act.wait_ge(sem("pv_step"), g - 1)
                        act.activation(pp[:, 4 * (st % 2) + i, :], ST[i % 2][:, :], ACT.Exp, scale=0.25)\
                           .then_inc(sem("probs"), 1)
                        if i == 0 and e is not None:
                            keys(kv, e)
                elif e is not None:
                    keys(kv, e)
                for j, offset in ((0, -14), (1, -10)):
                    if (d := at_step(st, offset, TB)) is not None:
                        queries(kv, d, j)
                d = at_step(st, 8, TB)
                if d is not None and exists(4 * kv + d, UNITS):
                    act.wait_ge(sem("pv_step"), TB * (4 * kv + d + 1))
                    if not fixed_below(4 * kv + d, 1):
                        act.wait_ge(sem("out_turned"), 4 * kv + d)
                    act.activation(pvs[:, :], PV[:, :], ACT.Copy).then_inc(sem("pv_sb"), 1)
                d = at_step(st, 11, TB)
                if d is not None and exists(4 * kv + d, UNITS):
                    u = 4 * kv + d
                    act.wait_ge(sem("out_turned"), u + 1)
                    if not fixed_below(u, 1):
                        act.wait_ge(sem("out_added"), u)
                    act.activation(osb[:, :], TR[:, :], ACT.Copy).then_inc(sem("out_read"), 1)
                d = at_step(st, -3, TB)
                if d is not None and exists(4 * kv + d, UNITS):
                    u = 4 * kv + d
                    act.wait_ge(sem("nm_ps"), u + 1)
                    if not fixed_below(u, 1):
                        act.wait_ge(sem("rows_in"), 32 * u)
                    act.activation(nmt[:, :], TRB[0:2 * PAIR * TB, 0:P], ACT.Copy).then_inc(sem("nmt_ready"), 1)

            walk(None, act, 0, step)

        def att_dve(dve, chain):
            def step(kv, st):
                d, pos = (st + 12) // TB, (st + 12) % TB
                u = 4 * kv + d
                if exists(u, UNITS):
                    if pos == 0 and not fixed_below(u, 1):
                        dve.wait_ge(sem("nm_ready"), u)
                    for i in range(2 * pos, 2 * pos + 2):
                        dve.wait_ge(sem("score2"), 16 * u + (i + 1))
                        dve.tensor_reduce(m1[:, i // TB, i % TB:i % TB + 1], SB[i % 2].rearrange("p h n -> p (h n)"),
                                          AX, ALU.max).then_inc(sem("max_read"), 1)
                if pos == TB - 1 and exists(u, UNITS):
                    dve.wait_ge(sem("max_read"), 16 * (u + 1))
                    if not fixed_below(u, 1):
                        dve.wait_ge(sem("nm_ps"), u)
                    flat_m = m1[:, :, :].rearrange("p a c -> p (a c)")
                    chain(dve.tensor_scalar(nm[:, 0, :], flat_m, -1.0, None, ALU.mult))
                    dve.scalar_tensor_tensor(nm[:, 1, :], flat_m, -1.0, nm[:, 0, :], ALU.mult, ALU.subtract)\
                       .then_inc(sem("nm_ready"), 1)
                d = at_step(st, 12, TB)
                if d is not None and exists(4 * kv + d, UNITS):
                    u = 4 * kv + d
                    dve.wait_ge(sem("out_read"), u + 1)
                    if not fixed_below(u, 1):
                        dve.wait_ge(sem("out_added"), u)
                    dve.reciprocal(rec[:, :, :, :].rearrange("p i j h -> p i (j h)"),
                                   osb[:, :].rearrange("p (i q d) -> p i q d", i=4, q=4)[:, :, :, HD])\
                       .then_inc(sem("out_rec"), 1)

                if fixed_below(kv, KV) and kv == KV - 1 and st == SPAN - TB:
                    dve.wait_ge(sem("out_added"), UNITS - 2)
                    with dve.Fori(0, TB) as t:
                        bn_dve(dve, "mem_b", t)

            walk(chain, dve, 4, step)
            dve.wait_ge(sem("out_added"), UNITS)
            with dve.Fori(TB, NT) as t:
                bn_dve(dve, "mem_b", t)
            dve.sem_inc(phase_done["att"], 1)

        def att_pool(pool, chain):
            pool.wait_ge(sem("att_qkv"), 1)

            def stack(src, res, row, order):
                (h0, *hs), (m0, *ms), (l0,) = order
                apart(pool, sem("apart_pool"))
                chain(pool.tensor_copy(row(h0), src))
                chain(pool.tensor_tensor(res, src, row(h0), ALU.subtract))
                apart(pool, sem("apart_pool"))
                chain(pool.tensor_copy(row(m0), res))
                chain(pool.tensor_tensor(row(l0), res, row(m0), ALU.subtract))
                for i, first in [(i, h0) for i in hs] + [(i, m0) for i in ms]:
                    apart(pool, sem("apart_pool"))
                    chain(pool.tensor_copy(row(i), row(first)))

            def add(kv, d):
                u = 4 * kv + d
                if not exists(u, UNITS):
                    return
                pool.wait_ge(sem("out_rec"), u + 1)
                O = osb[:, :].rearrange("p (i j h d) -> p i j h d", i=4, j=PAIR, h=2)
                for hf in range(2):
                    chain(pool.tensor_tensor(oo[:, hf, :, :, :], O[:, :, :, hf, 0:HD],
                                             rec[:, :, :, hf].unsqueeze(3).to_broadcast([P, 4, PAIR, HD]), ALU.mult))
                b = d // 2 % 2
                view = x[:, b * TB:(b + 1) * TB, bass.ds((kv + d // 4) * (REP * HD) + d % 2 * (PAIR * HD), PAIR * HD)]
                pool.tensor_tensor(view, view, oo[:, :, :, :, :].rearrange("p h i j d -> p (h i) (j d)"), ALU.add)\
                    .then_inc(sem("out_added"), 1)

            def queries(kv, e, pair):
                n, t0 = 2 * kv + e, e * TB
                if not fixed_below(n, 1):
                    pool.wait_ge(sem("stack_ps"), TURNS * (n - 1) + 3 + 2 * pair)
                stack(qk[:, t0:t0 + TB, bass.ds(kv * REP + PAIR * pair, PAIR), :], qr,
                      lambda i: qs[:, pair, :, :, i * HD:(i + 1) * HD], ((0, 1, 4), (2, 3), (5,)))
                pool.sem_inc(sem("q_stacked"), 1)

            def slot(kv, e):
                n, t0 = 2 * kv + e, e * TB
                if not fixed_below(n, 1):
                    pool.wait_ge(sem("stack_ps"), TURNS * (n - 1) + 1)
                stack(qk[:, t0:t0 + TB, bass.ds(H + kv, 1), :].rearrange("p t h d -> p t (h d)"), kr,
                      lambda i: ks[:, :, i * HD:(i + 1) * HD], ((0, 2, 5), (1, 3), (4,)))
                pool.sem_inc(sem("k_stacked"), 1)
                queries(kv, e, 0)
                queries(kv, e, 1)
                add(kv, 2 * e - 4)
                if not fixed_below(n, 2):
                    pool.wait_ge(sem("pv_step"), 2 * TB * (n - 1))
                apart(pool, sem("apart_pool"))
                chain(pool.tensor_copy(vst[:, e, :, 0:HD], vv[:, t0:t0 + TB, bass.ds(kv, 1), :]
                                       .rearrange("p t h d -> p t (h d)")))
                pool.sem_inc(sem("v_ready"), 1)
                add(kv, 2 * e - 3)

            def head(kv):
                slot(kv, 0)
                slot(kv, 1)
            head(0)
            looped([chain], pool, 1, KV, 2 * (3 * 7 + 1 + 4), head)
            for d in range(4):
                add(KV, d - 4)

        def att_sync(sp):
            def unit(kv, d):
                u = 4 * kv + d
                sp.wait_ge(sem("nmt_ready"), u + 1)
                for part in range(2):
                    sp.dma_start(qst[KS + part:KS + part + 1, d, :, :].rearrange("p j (t c) -> p (j t) c", c=P),
                                 nmt[part * PAIR * TB:(part + 1) * PAIR * TB, :]).then_inc(sem("rows_in"), 16)
            for d in range(4):
                unit(0, d)
            with sp.Fori(1, KV) as kv:
                for d in range(4):
                    unit(kv, d)

        @block.sync
        def _(sp):
            sp.dma_start(ident[:, :], a["ident"]).then_inc(consts_loaded, 16)
            for n in range(XL):
                w = NT // XL
                sp.dma_start(x[:, n * w:(n + 1) * w, :], a["x"][n * w * P:(n + 1) * w * P, :]
                             .rearrange("(t p) n -> p t n", p=P)).then_inc(sem(f"x_loaded{n}"), 16)
            enter(sp, "lin")
            lin_sync(sp)
            enter(sp, "ffn_b")
            mem_prep_sync(sp)
            enter(sp, "att")
            att_sync(sp)
            for n, t0 in enumerate((0, NT // 2)):
                sp.wait_ge(sem("x"), past("mem_b", "x") + t0 + NT // 2)
                sp.dma_start(out[t0 * P:(t0 + NT // 2) * P, :].rearrange("(t p) n -> p t n", p=P),
                             x[:, t0:t0 + NT // 2, :]).then_inc(sem(f"stored{n}"), 16)
            for n in range(2):
                sp.wait_ge(sem(f"stored{n}"), 16)

        @block.scalar
        def _(act):
            for dst, src in ((kc(WA), a["w_ag_t"]), (kc(WB), a["w_base_t"]), (hb[:, :], a["b_base"]),
                             (lora_b[:, :], a["lora_b_t"])):
                act.dma_start(dst, src).then_inc(sem("ffn_loaded"), 16)
            act.wait_ge(sem("ffn_loaded"), 64)
            for raw, hi, _ in FFN_SPLITS:
                act.activation(hi, raw, ACT.Copy).then_inc(sem("ffn_hi"), 1)
            act.wait_ge(consts_loaded, 16)
            act.activation(identb[:, :], ident[:, :], ACT.Copy).then_inc(sem("identb_ready"), 1)
            stats_act(act, "ffn_a")
            ffn_act(act, "ffn_a")
            enter(act, "lin")
            lin_act(act)
            enter(act, "ffn_b")
            stats_act(act, "ffn_b")
            mem_prep_act(act)
            split_att_act(act)
            ffn_act(act, "ffn_b")
            enter(act, "mem_a")
            stats_act(act, "mem_a")
            mem_act(act, "mem_a")
            enter(act, "att")
            stats_act(act, "att")
            qkv_act(act)
            att_act(act)
            enter(act, "mem_b")
            stats_act(act, "mem_b")
            mem_act(act, "mem_b")

        @block.gpsimd
        def _(pool):
            chain = Chain(pool, pool_steps)
            split_lo_pool(pool, FFN_SPLITS, "ffn")
            pool.wait_ge(sem("hb_ready"), 1)
            ffn_pool(pool, "ffn_a")
            enter(pool, "lin")
            lin_pool(pool, chain)
            enter(pool, "ffn_b")
            split_lo_pool(pool, MEM_SPLITS, "mem")
            ffn_pool(pool, "ffn_b")
            split_lo_pool(pool, ATT_SPLITS, "att")
            enter(pool, "mem_a")
            mem_pool(pool, chain, "mem_a")
            enter(pool, "att")
            qkv_pool(pool)
            att_pool(pool, chain)
            enter(pool, "mem_b")
            mem_pool(pool, chain, "mem_b")

        def presets_dve(dve, chain):
            chain(dve.memset(lg[:, :, :], SENTINEL))
            chain(dve.memset(rep[:, :, :], SENTINEL))

        @block.vector
        def _(dve):
            chain = Chain(dve, dve_steps)
            chain(dve.memset(ones[:, :], 1.0))
            presets_dve(dve, chain)
            for n in range(XL):
                dve.wait_ge(sem(f"x_loaded{n}"), 16)
                with dve.Fori(n * NT // XL, (n + 1) * NT // XL) as t:
                    bn_dve(dve, "ffn_a", t)
            dve.wait_ge(sem("ffn_loaded"), 64)
            chain(dve.tensor_scalar(hb[:, :], hb[:, :], 0.5, None, ALU.mult))
            dve.sem_inc(sem("hb_ready"), 1)
            stats_dve(dve, chain, "ffn_a")
            ffn_dve(dve, chain, "ffn_a")
            lin_dve(dve, chain)
            presets_dve(dve, chain)
            stats_dve(dve, chain, "ffn_b")
            ffn_dve(dve, chain, "ffn_b")
            dve.wait_ge(sem("mem_loaded"), MEM_LOADED)
            chain(dve.tensor_scalar(wu2[:, :], wu2[:, :], 0.5, None, ALU.mult))
            stats_dve(dve, chain, "mem_a")
            mem_dve(dve, chain, "mem_a")
            stats_dve(dve, chain, "att")
            dve.wait_ge(sem("att_loaded"), ATT_LOADED)
            qkv_dve(dve, chain)
            att_dve(dve, chain)
            stats_dve(dve, chain, "mem_b")
            mem_dve(dve, chain, "mem_b")

        @block.tensor
        def _(pe):
            pe.wait_ge(consts_loaded, 16)
            pe.wait_ge(sem("ffn_lo"), 2)
            ffn_pe(pe, "ffn_a")
            enter(pe, "lin")
            lin_pe(pe)
            enter(pe, "ffn_b")
            mem_prep_pe(pe)
            ffn_pe(pe, "ffn_b")
            enter(pe, "mem_a")
            pe.wait_ge(sem("mp_v3_sb"), 1)
            pe.wait_ge(sem("mem_lo"), 2)
            mem_pe(pe, "mem_a")
            enter(pe, "att")
            pe.wait_ge(sem("identb_ready"), 1)
            qkv_pe(pe)
            att_pe(pe)
            enter(pe, "mem_b")
            mem_pe(pe, "mem_b")


def decay_tables():
    f = np.float32
    slope = ((1.0 / 2.0 ** (8.0 / LH)) ** (np.arange(LH) + 1.0) * (1.0 - 1 / (32 - 1 + 1e-05) + 1e-05)).astype(f)
    slope = slope.astype(np.float64)[:, None]
    r = np.arange(P) + 1.0
    q = np.exp(-slope * r)
    k = np.exp(-slope * (P - r))
    diff = r[None, :] - r[:, None]
    diag = np.where(diff >= 0, np.exp(-slope[:, :, None] * np.maximum(diff, 0)), 0.0)
    both = np.stack([diag, np.broadcast_to(q[:, None, :], diag.shape)], axis=2)
    block = np.broadcast_to(np.exp(-slope * P).T, (P, LH))
    return both.astype(f), np.ascontiguousarray(k.T).astype(f), np.ascontiguousarray(block).astype(f)


def rope_tables():
    f = np.float32
    inv = (1.0 / np.power(f(10000.0), np.arange(0, HD, 2, dtype=f) / f(HD))).astype(f)
    ang = (np.arange(TB * P, dtype=f)[:, None] * inv[None, :]).astype(f).astype(np.float64)
    c, s = np.cos(ang), np.sin(ang)
    both = np.stack([np.concatenate([c, c], 1), np.concatenate([-s, s], 1)], axis=1)
    return np.ascontiguousarray(both.reshape(TB, P, 2, HD).transpose(1, 0, 2, 3)).astype(f)


def chunked(w):
    return np.ascontiguousarray(w.reshape(KC, P, -1).transpose(1, 0, 2))


def rows(v):
    return np.ascontiguousarray(np.broadcast_to(v.reshape(1, -1), (P, v.size)))


def kernel(**inputs):
    import concourse.bacc as _bacc
    from concourse.bass_utils import run_bass_kernel_spmd as _run

    i = {n: np.asarray(v) for n, v in inputs.items()}
    f = np.float32
    decay, kdec, bdec = decay_tables()
    arr = {}
    arr["x"] = i["L0_attn_hidden_states"].reshape(T, D)
    arr["ident"] = np.eye(P, dtype=f)
    arr["b_base"] = rows(i["L0_ffn_b_base"])
    arr["w_base_t"] = chunked(i["L0_ffn_W_base"].T)
    a_t = i["L0_ffn_A"].reshape(E * R, D).T
    arr["w_ag_t"] = chunked(np.concatenate([a_t, i["L0_ffn_W_gate"].T, np.zeros((D, 256 - P - E), f)], axis=1))
    arr["lora_b_t"] = i["L0_ffn_B"].transpose(0, 2, 1).reshape(E * R, D)
    qkv = i["L0_attn_qkv_w"].reshape(LH, 3, P, KC, P)
    gw = i["L0_attn_gate_w"].reshape(LH, 1, P, KC, P)
    arr["w_heads"] = np.concatenate([qkv, gw], axis=1).transpose(0, 4, 1, 3, 2)
    arr["ow_heads"] = i["L0_attn_out_w"].T.reshape(LH, P, D)
    arr["norm_w"] = i["L0_attn_norm_w"].reshape(LH, P).T
    arr["decay"], arr["kdec"], arr["bdec"] = decay, kdec, bdec
    arr["wqkv"] = chunked(np.concatenate([i["L1_attn_wq"], i["L1_attn_wk"], i["L1_attn_wv"]], axis=1))
    arr["b_qkv"] = rows(np.concatenate([i["L1_attn_bq"], i["L1_attn_bk"], i["L1_attn_bv"]]))
    arr["rope"] = rope_tables()
    arr["wq_mem"] = i["L1_ffn_Wq"]
    arr["wr"] = i["L1_ffn_Wr"]
    arr["wr_t"] = i["L1_ffn_Wr"].T
    arr["keys_t"] = i["L1_ffn_aux_keys"].T
    arr["values_t"] = chunked(i["L1_ffn_aux_values"].T).reshape(P, KC * NSLOT)
    arr["wvd_t"] = chunked(i["L1_ffn_Wvd"].T).reshape(P, KC * VB)
    arr["wvu_t"] = i["L1_ffn_Wvu"].T
    arr["wu1_t"] = chunked(i["L1_ffn_Wu1"].T)
    arr["bias_mem"] = rows(np.concatenate([i["L1_ffn_log_rel"], i["L1_ffn_log_rel"], i["L1_ffn_bu1"]]))
    arr["wu2"] = rows(i["L1_ffn_Wu2"])
    arr["scalars"] = rows(np.concatenate([i["L1_ffn_bu2"].reshape(1), i["L1_ffn_gate_w1"].reshape(1),
                                          i["L1_ffn_gate_bias"].reshape(1)]))
    arr = {n: np.ascontiguousarray(v) for n, v in arr.items()}

    nc = _bacc.Bacc("TRN2", target_bir_lowering=False, num_devices=1)
    aps = {n: nc.dram_tensor(f"in_{n}", v.shape, F32, kind="ExternalInput").ap() for n, v in arr.items()}
    out = nc.dram_tensor("out_x", (T, D), F32, kind="ExternalOutput").ap()
    program(nc, aps, out)
    r = _run(nc, [{f"in_{n}": v for n, v in arr.items()}], core_ids=[0])
    return np.asarray(r.results[0]["out_x"]).reshape(B, T // B, D)
```
